# Optimizing a Trainium2 kernel written in Bass

```python
import numpy as np
import jax
import jax.numpy as jnp

def _softmax(x, axis=-1):
    return jax.nn.softmax(x, axis=axis)

def _gelu(x):
    return jax.nn.gelu(x, approximate=True)

def _silu(x):
    return jax.nn.silu(x)

def _sigmoid(x):
    return jax.nn.sigmoid(x)

def _layernorm(x, axis=-1, eps=1e-05):
    m = jnp.mean(x, axis=axis, keepdims=True)
    v = jnp.var(x, axis=axis, keepdims=True)
    return (x - m) / jnp.sqrt(v + eps)

def _scatter_add(tgt, idx, src, axis=0):
    return tgt.at[idx].add(src)

def _segment_sum(src, seg, n):
    return jax.ops.segment_sum(src, seg, n)
kernel_name = 'mk_xattn_ffn_d2_seqx_r4_721fcd'

def setup_inputs(seed: int=0):
    np.random.seed(seed)
    _w = jnp.asarray

    def _rec_inputs():
        import jax
        import jax.numpy as jnp
        _rk = jax.random.key(seed)
        x = -0.0005146 + 1 * jax.random.normal(jax.random.fold_in(_rk, 1), (2, 1024, 256), jnp.float32)
        _lenS = 1024 - jax.random.randint(jax.random.fold_in(_rk, 7), (2,), 0, max(1, 1024 // 4) + 1, jnp.int32)
        _lenS2 = 64 - jax.random.randint(jax.random.fold_in(_rk, 8), (2,), 0, max(1, 64 // 4) + 1, jnp.int32)
        _ctx_768P = jax.random.normal(jax.random.fold_in(_rk, 11), (2, 16, 192), jnp.float32)
        _ctx_768c = jax.random.dirichlet(jax.random.fold_in(_rk, 511), 0.3 * jnp.ones((16,), jnp.float32), (2, 64))
        _ctx_768t = jnp.einsum('bsk,bkd->bsd', _ctx_768c, _ctx_768P)
        _ctx_768t = _ctx_768t * jax.lax.rsqrt(jnp.mean(jnp.square(_ctx_768t)) + 1e-12) * 0.953939
        ctx_768 = -0.00040386 + 0.999972 * (_ctx_768t + 0.3 * jax.random.normal(jax.random.fold_in(_rk, 611), (2, 64, 192), jnp.float32))
        _validS = jnp.arange(1024)[None, :] < _lenS[:, None]
        _validS2 = jnp.arange(64)[None, :] < _lenS2[:, None]
        _causal = jnp.tril(jnp.ones((1024, 1024), dtype=bool))
        mask_BxS2_bk0 = jnp.logical_not(jnp.broadcast_to(_validS2[:, :], (2, 64)))
        return (x, ctx_768, mask_BxS2_bk0)
    x, ctx_768, mask_BxS2_bk0 = _rec_inputs()

    def _L0_xattn_setup():
        import jax, jax.numpy as jnp
        import numpy as np
        DIM_IN, DIM_LAT, DIM_HEAD = (192, 256, 64)
        INNER = max(DIM_LAT, DIM_IN)
        HEADS = INNER // DIM_HEAD
        SCALE = DIM_HEAD ** (-0.5)
        RMS_EPS = 1e-08
        LN_EPS = 1e-05

        def layernorm(x, g, b):
            mu = jnp.mean(x, axis=-1, keepdims=True)
            var = jnp.mean((x - mu) ** 2, axis=-1, keepdims=True)
            return (x - mu) * jax.lax.rsqrt(var + LN_EPS) * g + b

        def rmsnorm(x, gamma):
            norm = jnp.sqrt(jnp.sum(x * x, axis=-1, keepdims=True)) * x.shape[-1] ** (-0.5)
            return x / jnp.maximum(norm, RMS_EPS) * gamma
        key = jax.random.key(seed)
        ks = jax.random.split(key, 12)
        b, n, m = (4, 1024, 128)
        x = jax.random.normal(ks[0], (b, n, DIM_IN), jnp.float32)
        latents = jax.random.normal(ks[1], (b, m, DIM_LAT), jnp.float32)
        mask = jax.random.randint(ks[2], (b, n), 0, 2).astype(bool)
        s = lambda k, sh, fan: jax.random.normal(k, sh, jnp.float32) * fan ** (-0.5)
        return {'x': x, 'latents': latents, 'mask': mask, 'ln_x_g': jnp.ones((DIM_IN,), jnp.float32), 'ln_x_b': jnp.zeros((DIM_IN,), jnp.float32), 'ln_l_g': jnp.ones((DIM_LAT,), jnp.float32), 'ln_l_b': jnp.zeros((DIM_LAT,), jnp.float32), 'qn_g': jnp.ones((DIM_HEAD,), jnp.float32), 'kn_g': jnp.ones((DIM_HEAD,), jnp.float32), 'Wq': s(ks[3], (INNER, DIM_LAT), DIM_LAT), 'Wkv': s(ks[4], (2 * INNER, DIM_IN), DIM_IN), 'Wlkv': s(ks[5], (2 * INNER, DIM_LAT), DIM_LAT), 'Wo': s(ks[6], (DIM_LAT, INNER), INNER), 'bo': jnp.zeros((DIM_LAT,), jnp.float32)}
    _L0_xattn_all = _L0_xattn_setup()
    _L0_xattn_in = {k: v for k, v in _L0_xattn_all.items() if k in ('ln_x_g', 'ln_x_b', 'ln_l_g', 'ln_l_b', 'qn_g', 'kn_g', 'Wq', 'Wkv', 'Wlkv', 'Wo', 'bo')}
    del _L0_xattn_all

    def _L0_ffn_setup():
        import jax, jax.numpy as jnp
        import numpy as np
        TOP_K = 2

        def _ffn(x, gw, uw, dw):
            return jax.nn.silu(x @ gw.T) * (x @ uw.T) @ dw.T
        key = jax.random.key(seed)
        ks = jax.random.split(key, 8)
        w = lambda k, shape: jax.random.normal(k, shape, jnp.float32) * 0.02
        return dict(x=jax.random.normal(ks[0], (4, 512, 256), jnp.float32), gate_w=w(ks[1], (8, 256)), expert_gate=w(ks[2], (8, 704, 256)), expert_up=w(ks[3], (8, 704, 256)), expert_down=w(ks[4], (8, 256, 704)), shared_gate=w(ks[5], (704, 256)), shared_up=w(ks[6], (704, 256)), shared_down=w(ks[7], (256, 704)))
    _L0_ffn_all = _L0_ffn_setup()
    _L0_ffn_in = {k: v for k, v in _L0_ffn_all.items() if k in ('gate_w', 'expert_gate', 'expert_up', 'expert_down', 'shared_gate', 'shared_up', 'shared_down')}
    del _L0_ffn_all

    def _L1_xattn_setup():
        import jax, jax.numpy as jnp
        import numpy as np
        DIM_Q = 256
        DIM_KV = 192
        N_HEADS = 4

        def _split_heads(x):
            b, l, d = x.shape
            return x.reshape(b, l, N_HEADS, d // N_HEADS).transpose(0, 2, 1, 3)
        key = jax.random.key(seed)
        ks = jax.random.split(key, 7)
        b, lq, lkv = (4, 512, 512)
        q = jax.random.normal(ks[0], (b, lq, DIM_Q), dtype=jnp.float32)
        kv = jax.random.normal(ks[1], (b, lkv, DIM_KV), dtype=jnp.float32)
        s_q = 1.0 / np.sqrt(DIM_Q)
        s_kv = 1.0 / np.sqrt(DIM_KV)
        Wq = jax.random.normal(ks[2], (DIM_Q, DIM_Q), dtype=jnp.float32) * s_q
        Wk = jax.random.normal(ks[3], (DIM_Q, DIM_KV), dtype=jnp.float32) * s_kv
        Wv = jax.random.normal(ks[4], (DIM_Q, DIM_KV), dtype=jnp.float32) * s_kv
        Wo = jax.random.normal(ks[5], (DIM_Q, DIM_Q), dtype=jnp.float32) * s_q
        bo = jax.random.normal(ks[6], (DIM_Q,), dtype=jnp.float32) * 0.01
        return {'q': q, 'kv': kv, 'Wq': Wq, 'Wk': Wk, 'Wv': Wv, 'Wo': Wo, 'bo': bo}
    _L1_xattn_all = _L1_xattn_setup()
    _L1_xattn_in = {k: v for k, v in _L1_xattn_all.items() if k in ('Wq', 'Wk', 'Wv', 'Wo', 'bo')}
    del _L1_xattn_all

    def _L1_ffn_setup():
        import jax, jax.numpy as jnp
        import numpy as np
        B, L, H, E, FF, C = (4, 512, 256, 8, 1024, 2)
        key = jax.random.key(seed)
        ks = jax.random.split(key, 6)
        s = 0.02
        return {'x': jax.random.normal(ks[0], (B, L, H), dtype=jnp.float32), 'Wg': jax.random.normal(ks[1], (H, E), dtype=jnp.float32) * s, 'W1': jax.random.normal(ks[2], (E, H, FF), dtype=jnp.float32) * s, 'b1': jnp.zeros((E, FF), dtype=jnp.float32), 'W2': jax.random.normal(ks[3], (E, FF, H), dtype=jnp.float32) * s, 'b2': jnp.zeros((E, H), dtype=jnp.float32)}
    _L1_ffn_all = _L1_ffn_setup()
    _L1_ffn_in = {k: v for k, v in _L1_ffn_all.items() if k in ('Wg', 'W1', 'b1', 'W2', 'b2')}
    del _L1_ffn_all
    return {'x': x, 'ctx_768': ctx_768, 'mask_BxS2_bk0': mask_BxS2_bk0, 'L0_xattn_ln_x_g': _L0_xattn_in['ln_x_g'], 'L0_xattn_ln_x_b': _L0_xattn_in['ln_x_b'], 'L0_xattn_ln_l_g': _L0_xattn_in['ln_l_g'], 'L0_xattn_ln_l_b': _L0_xattn_in['ln_l_b'], 'L0_xattn_qn_g': _L0_xattn_in['qn_g'], 'L0_xattn_kn_g': _L0_xattn_in['kn_g'], 'L0_xattn_Wq': _L0_xattn_in['Wq'], 'L0_xattn_Wkv': _L0_xattn_in['Wkv'], 'L0_xattn_Wlkv': _L0_xattn_in['Wlkv'], 'L0_xattn_Wo': _L0_xattn_in['Wo'], 'L0_xattn_bo': _L0_xattn_in['bo'], 'L0_ffn_gate_w': _L0_ffn_in['gate_w'], 'L0_ffn_expert_gate': _L0_ffn_in['expert_gate'], 'L0_ffn_expert_up': _L0_ffn_in['expert_up'], 'L0_ffn_expert_down': _L0_ffn_in['expert_down'], 'L0_ffn_shared_gate': _L0_ffn_in['shared_gate'], 'L0_ffn_shared_up': _L0_ffn_in['shared_up'], 'L0_ffn_shared_down': _L0_ffn_in['shared_down'], 'L1_xattn_Wq': _L1_xattn_in['Wq'], 'L1_xattn_Wk': _L1_xattn_in['Wk'], 'L1_xattn_Wv': _L1_xattn_in['Wv'], 'L1_xattn_Wo': _L1_xattn_in['Wo'], 'L1_xattn_bo': _L1_xattn_in['bo'], 'L1_ffn_Wg': _L1_ffn_in['Wg'], 'L1_ffn_W1': _L1_ffn_in['W1'], 'L1_ffn_b1': _L1_ffn_in['b1'], 'L1_ffn_W2': _L1_ffn_in['W2'], 'L1_ffn_b2': _L1_ffn_in['b2']}

def reference(x, ctx_768, mask_BxS2_bk0, L0_xattn_ln_x_g, L0_xattn_ln_x_b, L0_xattn_ln_l_g, L0_xattn_ln_l_b, L0_xattn_qn_g, L0_xattn_kn_g, L0_xattn_Wq, L0_xattn_Wkv, L0_xattn_Wlkv, L0_xattn_Wo, L0_xattn_bo, L0_ffn_gate_w, L0_ffn_expert_gate, L0_ffn_expert_up, L0_ffn_expert_down, L0_ffn_shared_gate, L0_ffn_shared_up, L0_ffn_shared_down, L1_xattn_Wq, L1_xattn_Wk, L1_xattn_Wv, L1_xattn_Wo, L1_xattn_bo, L1_ffn_Wg, L1_ffn_W1, L1_ffn_b1, L1_ffn_W2, L1_ffn_b2):
    import jax
    import jax.numpy as jnp

    def _L0_xattn_ref(x, latents, mask, ln_x_g, ln_x_b, ln_l_g, ln_l_b, qn_g, kn_g, Wq, Wkv, Wlkv, Wo, bo):
        import jax, jax.numpy as jnp
        import numpy as np
        DIM_IN, DIM_LAT, DIM_HEAD = (192, 256, 64)
        INNER = max(DIM_LAT, DIM_IN)
        HEADS = INNER // DIM_HEAD
        SCALE = DIM_HEAD ** (-0.5)
        RMS_EPS = 1e-08
        LN_EPS = 1e-05

        def layernorm(x, g, b):
            mu = jnp.mean(x, axis=-1, keepdims=True)
            var = jnp.mean((x - mu) ** 2, axis=-1, keepdims=True)
            return (x - mu) * jax.lax.rsqrt(var + LN_EPS) * g + b

        def rmsnorm(x, gamma):
            norm = jnp.sqrt(jnp.sum(x * x, axis=-1, keepdims=True)) * x.shape[-1] ** (-0.5)
            return x / jnp.maximum(norm, RMS_EPS) * gamma
        b, n, _ = x.shape
        m = latents.shape[1]
        xn = layernorm(x, ln_x_g, ln_x_b)
        ln = layernorm(latents, ln_l_g, ln_l_b)
        q = ln @ Wq.T
        kv = jnp.concatenate([xn @ Wkv.T, ln @ Wlkv.T], axis=1)
        k, v = (kv[..., :INNER], kv[..., INNER:])
        split_heads = lambda t: t.reshape(t.shape[0], t.shape[1], HEADS, DIM_HEAD).transpose(0, 2, 1, 3)
        q, k, v = (split_heads(q), split_heads(k), split_heads(v))
        qn = rmsnorm(q, qn_g) * SCALE
        kn = rmsnorm(k, kn_g)
        attn = jnp.einsum('bhid,bhjd->bhij', qn, kn)
        full_mask = jnp.pad(mask, ((0, 0), (0, m)), constant_values=True)
        attn = jnp.where(full_mask[:, None, None, :], attn, -jnp.finfo(attn.dtype).max)
        attn = jax.nn.softmax(attn, axis=-1)
        out = jnp.einsum('bhij,bhjd->bhid', attn, v)
        out = out.transpose(0, 2, 1, 3).reshape(b, m, INNER)
        return out @ Wo.T + bo

    def _L0_ffn_ref(x, gate_w, expert_gate, expert_up, expert_down, shared_gate, shared_up, shared_down):
        import jax, jax.numpy as jnp
        import numpy as np
        TOP_K = 2

        def _ffn(x, gw, uw, dw):
            return jax.nn.silu(x @ gw.T) * (x @ uw.T) @ dw.T
        B, S, H = x.shape
        xf = x.reshape(-1, H)
        T = xf.shape[0]
        E = expert_gate.shape[0]
        shared = _ffn(xf, shared_gate, shared_up, shared_down)
        logits = xf @ gate_w.T
        probs = jax.nn.softmax(logits, axis=-1)
        topw, topi = jax.lax.top_k(probs, TOP_K)
        topw = topw / (topw.sum(-1, keepdims=True) + 1e-20)
        comb = jnp.zeros((T, E), xf.dtype).at[jnp.arange(T)[:, None], topi].add(topw)

        def body(acc, ws):
            gw, uw, dw, wcol = ws
            return (acc + _ffn(xf, gw, uw, dw) * wcol[:, None], None)
        routed, _ = jax.lax.scan(body, jnp.zeros_like(xf), (expert_gate, expert_up, expert_down, comb.T))
        return (shared + routed).reshape(B, S, H)

    def _L1_xattn_ref(q, kv, Wq, Wk, Wv, Wo, bo):
        import jax, jax.numpy as jnp
        import numpy as np
        DIM_Q = 256
        DIM_KV = 192
        N_HEADS = 4

        def _split_heads(x):
            b, l, d = x.shape
            return x.reshape(b, l, N_HEADS, d // N_HEADS).transpose(0, 2, 1, 3)
        qp = q @ Wq.T
        kp = kv @ Wk.T
        vp = kv @ Wv.T
        qh, kh, vh = (_split_heads(qp), _split_heads(kp), _split_heads(vp))
        scale = (DIM_Q // N_HEADS) ** (-0.5)
        scores = jnp.einsum('bhqd,bhkd->bhqk', qh, kh) * scale
        attn = jax.nn.softmax(scores, axis=-1)
        ctx = jnp.einsum('bhqk,bhkd->bhqd', attn, vh)
        b, h, lq, hd = ctx.shape
        ctx = ctx.transpose(0, 2, 1, 3).reshape(b, lq, h * hd)
        return ctx @ Wo.T + bo

    def _L1_ffn_ref(x, Wg, W1, b1, W2, b2):
        import jax, jax.numpy as jnp
        import numpy as np
        B, L, H, E, FF, C = (4, 512, 256, 8, 1024, 2)
        b, l, h = x.shape
        e = Wg.shape[1]
        n = b * l
        k = min(max(int(n * C / e), 1), n)
        xt = x.reshape(n, h)
        S = jax.nn.sigmoid(xt @ Wg).T
        G, I = jax.lax.top_k(S, k)
        ex = xt[I]
        hid = jax.nn.gelu(jnp.einsum('ekh,ehf->ekf', ex, W1) + b1[:, None, :], approximate=False)
        out = (jnp.einsum('ekf,efh->ekh', hid, W2) + b2[:, None, :]) * G[..., None]
        new_x = jnp.zeros_like(xt).at[I.reshape(-1)].add(out.reshape(-1, h))
        return new_x.reshape(b, l, h)
    x = x + _L0_xattn_ref(ctx_768, _layernorm(x, axis=-1), mask_BxS2_bk0, L0_xattn_ln_x_g, L0_xattn_ln_x_b, L0_xattn_ln_l_g, L0_xattn_ln_l_b, L0_xattn_qn_g, L0_xattn_kn_g, L0_xattn_Wq, L0_xattn_Wkv, L0_xattn_Wlkv, L0_xattn_Wo, L0_xattn_bo)
    x = x + _L0_ffn_ref(_layernorm(x, axis=-1), L0_ffn_gate_w, L0_ffn_expert_gate, L0_ffn_expert_up, L0_ffn_expert_down, L0_ffn_shared_gate, L0_ffn_shared_up, L0_ffn_shared_down)
    x = x + _L1_xattn_ref(_layernorm(x, axis=-1), ctx_768, L1_xattn_Wq, L1_xattn_Wk, L1_xattn_Wv, L1_xattn_Wo, L1_xattn_bo)
    x = x + _L1_ffn_ref(_layernorm(x, axis=-1), L1_ffn_Wg, L1_ffn_W1, L1_ffn_b1, L1_ffn_W2, L1_ffn_b2)
    return x

_drawn_inputs = setup_inputs


def setup_inputs(seed=0):
    import zlib

    import numpy as np

    out = dict(_drawn_inputs(seed))
    spreads = {'L0_xattn_ln_x_g': (1.0, 0.6),
     'L0_xattn_ln_x_b': (0.0, 0.8),
     'L0_xattn_ln_l_g': (1.0, 0.2),
     'L0_xattn_ln_l_b': (0.0, 0.1),
     'L0_xattn_qn_g': (1.0, 0.6),
     'L0_xattn_kn_g': (1.0, 0.6),
     'L0_xattn_bo': (0.0, 0.1),
     'L1_ffn_b1': (0.0, 0.307),
     'L1_ffn_b2': (0.0, 0.1)}
    factors = {'L0_xattn_Wkv': 4.281,
     'L0_ffn_gate_w': 3.011,
     'L0_ffn_expert_gate': 2.8,
     'L0_ffn_expert_up': 2.687,
     'L0_ffn_expert_down': 2.758,
     'L1_xattn_bo': 6.038}
    for name, (base, spread) in spreads.items():
        noise = np.random.default_rng([zlib.crc32(name.encode()), seed]).standard_normal(out[name].shape)
        drawn = base * np.exp(spread * noise) if base else spread * noise
        out[name] = jnp.asarray(drawn.astype(out[name].dtype))
    for name, factor in factors.items():
        out[name] = (out[name] * factor).astype(out[name].dtype)
    return out
```

```python
from contextlib import ExitStack

import numpy as np

import concourse.bass as bass
from concourse import mybir

ALU = mybir.AluOpType
ACT = mybir.ActivationFunctionType
AX = mybir.AxisListType
F32 = mybir.dt.float32
F32R = mybir.dt.float32r
BF16 = mybir.dt.bfloat16
I32 = mybir.dt.int32
U32 = mybir.dt.uint32
U8 = mybir.dt.uint8
ds = bass.ds

P = 128
B = 2
S = 1024
T = B * S
TILES = T // P
GT = 4
GROUPS = TILES // GT
GPB = GROUPS // B
D = 256
KC = D // P
C = 64
DC = 192
KX = 2
PX = DC // KX
H = 4
HD = 64
KT = S // P + 1
KEYS = KT * P
CTX0 = S
BIG = 1.0e30
LN_EPS = 1e-5
RMS_EPS = 1e-8
RT_SHIFTED, RT_PICKED, RT_PADDED = 2, 17, 58
R1_GATES, R1_FLAGS, R1_CHOSEN = 2, 6, 23
UNITS = H * GT
E = 8
F = 704
FA = 384
FB = F - FA
FT = 6
FW = 2 * KC * F + FT * D
SHARED = TILES
ROUTED = 2 * T // P + E
CHOSEN = T * 2 // E
CT = CHOSEN // P
F1 = 1024
FT1 = F1 // P
W1 = KC * F1
FW1 = W1 + FT1 * D
BITS = 30
XG = D + E
RING = H + 3 * UNITS + GT


def build(nc, ap, out):
    ctx = ExitStack()
    with ctx:
        def sb(name, shape, dt=F32, scope=ctx):
            return scope.enter_context(nc.sbuf_tensor(name, shape, dt))

        def sem(name):
            return ctx.enter_context(nc.semaphore(name))

        psum = ctx.enter_context(nc.psum_tensor("psum", [P, 8, 512], F32))

        x = sb("x", [P, TILES, D])
        xn = sb("xn", [P, TILES, D])
        ident = sb("ident", [P, P])
        ident_r = sb("ident_r", [P, P], F32R)
        neg_half = sb("neg_half", [P, 4 * H * GT * 2])
        zeros = sb("zeros", [P, D])
        stat = sb("stat", [P, TILES, 6])
        mean_var = sb("mean_var", [P, TILES, 2])
        rstd = sb("rstd", [P, TILES])

        own = [sb(f"own{i}", [P, CT], U32) for i in range(2)]
        tokens = sb("tokens", [P, E, CT], U32)

        att = ExitStack()
        kT = sb("kT", [P, H, 2, KEYS], F32R, att)
        v = sb("v", [P, KT, H, P], F32R, att)
        qT = sb("qT", [P, H, S], F32R, att)
        wqkv_h = sb("wqkv_h", [P, KC, 3 * D], F32R, att)
        wqkv_l = sb("wqkv_l", [P, KC, 3 * D], F32R, att)
        wo_h = sb("wo_h", [P, H, D], F32R, att)
        wo_l = sb("wo_l", [P, H, D], F32R, att)
        qk_gain = sb("qk_gain", [P, 2 * D], F32, att)
        bo = sb("bo", [P, D], F32, att)
        ln_g = sb("ln_g", [P, KC], F32, att)
        ln_b = sb("ln_b", [P, KC], F32, att)
        mask_rows = sb("mask_rows", [P, B, P], BF16, att)
        first_row = sb("first_row", [P, P], BF16, att)
        prj = ExitStack()
        xt = sb("xt", [P, GT, D], F32, prj)
        lnf = sb("lnf", [P, GT, KC, P], F32, prj)
        lnh = sb("lnh", [P, GT, KC, P], F32R, prj)
        lnl = sb("lnl", [P, GT, KC, P], F32R, prj)
        qkv = sb("qkv", [P, GT, 3 * D], F32, prj)
        sq = sb("sq", [P, 2, 2 * D], F32, prj)
        ssq = sb("ssq", [P, GT, 2 * H], F32, prj)
        rms = sb("rms", [P, GT, 2 * H], F32, prj)
        parts = sb("parts", [P, 2, 3 * H, P], F32R, prj)
        prj.close()
        raw = ExitStack()
        wqkv = sb("wqkv", [P, KC, 3 * D], F32, raw)
        wkvx = sb("wkvx", [PX, KX, 2 * D], F32, raw)
        wkvx_h = sb("wkvx_h", [PX, KX, 2 * D], F32R, raw)
        wkvx_l = sb("wkvx_l", [PX, KX, 2 * D], F32R, raw)
        wo = sb("wo", [P, H, D], F32, raw)
        xc = sb("xc", [P, DC], F32, raw)
        xcn = sb("xcn", [P, DC], F32, raw)
        cf = sb("cf", [PX, KX, P], F32, raw)
        ch = sb("ch", [PX, KX, P], F32R, raw)
        cl = sb("cl", [PX, KX, P], F32R, raw)
        lnx_g = sb("lnx_g", [PX, KX], F32, raw)
        lnx_b = sb("lnx_b", [PX, KX], F32, raw)
        ckv = sb("ckv", [P, 2 * D], F32, raw)
        csq = sb("csq", [P, D], F32, raw)
        cstat = sb("cstat", [P, 6], F32, raw)
        cmv = sb("cmv", [P, 2], F32, raw)
        crs = sb("crs", [P, 1], F32, raw)
        cms = sb("cms", [P, H], F32, raw)
        cparts = sb("cparts", [P, 2 * H, P], F32R, raw)
        mask_u8 = sb("mask_u8", [1, B * C], U8, raw)
        mask_f = sb("mask_f", [1, B * C], F32, raw)
        raw.close()
        act_ = ExitStack()
        qs = sb("qs", [P, H, GT * P], F32R, act_)
        prob = sb("prob", [P, 3, KEYS], F32, act_)
        pT_h = sb("pT_h", [P, KT, GT * P], F32R, act_)
        pT_l = sb("pT_l", [P, KT, GT * P], F32R, act_)
        oT_h = sb("oT_h", [P, H, GT * P], F32R, act_)
        oT_l = sb("oT_l", [P, H, GT * P], F32R, act_)
        neg_max = sb("neg_max", [P, UNITS], F32, act_)
        denom = sb("denom", [P, UNITS], F32, act_)
        rdenom = sb("rdenom", [P, UNITS], F32, act_)
        act_.close()
        att.close()

        moe = ExitStack()
        w_raw = sb("w_raw", [P, FW], F32, moe)
        w_h = [sb(f"w_h{i}", [P, FW], F32R, moe) for i in range(2)]
        w_l = [sb(f"w_l{i}", [P, FW], F32R, moe) for i in range(2)]
        xs0 = sb("xs0", [P, GT, D], F32, moe)
        xnT = sb("xnT", [P, GT, KC, P], F32, moe)
        gate_w = sb("gate_w", [P, KC, E], F32, moe)
        xb = sb("xb", [P, D], F32, moe)
        xbT_h = sb("xbT_h", [P, KC, P], F32R, moe)
        xbT_l = sb("xbT_l", [P, KC, P], F32R, moe)
        silu = sb("silu", [P, F], F32, moe)
        hid = sb("hid", [P, FT * P], F32, moe)
        hT_h = sb("hT_h", [P, FT, P], F32R, moe)
        hT_l = sb("hT_l", [P, FT, P], F32R, moe)
        y_sb = sb("y_sb", [P, D], F32, moe)
        logit = sb("logit", [P, TILES, E], F32, moe)
        mx = sb("mx", [P, TILES], F32, moe)
        rsum = sb("rsum", [P, TILES], F32, moe)
        eq = sb("eq", [P, TILES, E], F32, moe)
        pick = [sb(f"pick{i}", [P, TILES, E], F32, moe) for i in range(2)]
        both = sb("both", [P, TILES, E], F32, moe)
        weight = [sb(f"weight{i}", [P, TILES], F32, moe) for i in range(2)]
        scan = [sb(f"scan{i}", [P, TILES, E], F32, moe) for i in range(2)]
        totals = sb("totals", [P, TILES, E], F32, moe)
        blocks = sb("blocks", [P, E], F32, moe)
        blocks_i = sb("blocks_i", [P, E], I32, moe)
        starts = [sb(f"starts{i}", [P, E + 1], F32, moe) for i in range(2)]
        table = sb("table", [P, 2, E + 2], I32, moe)
        slot_f = sb("slot_f", [P, TILES], F32, moe)
        slot = [sb(f"slot{i}", [P, TILES], U32, moe) for i in range(2)]
        before = sb("before", [P, P], F32, moe)
        ones = sb("ones", [P, P], F32, moe)
        favour = sb("favour", [P, TILES, E], F32, moe)
        y_got = sb("y_got", [P, 4, D], F32, moe)
        moe.close()

        at1 = ExitStack()
        a_raw = sb("a_raw", [P, 2, KC, D], F32, at1)
        a_h = sb("a_h", [P, 2, KC, D], F32R, at1)
        a_l = sb("a_l", [P, 2, KC, D], F32R, at1)
        c_raw = sb("c_raw", [PX, 2, KX, D], F32, at1)
        c_h = sb("c_h", [PX, 2, KX, D], F32R, at1)
        c_l = sb("c_l", [PX, 2, KX, D], F32R, at1)
        bo1 = sb("bo1", [P, D], F32, at1)
        xc1 = sb("xc1", [P, DC], F32, at1)
        cT_h = sb("cT_h", [PX, KX, P], F32R, at1)
        cT_l = sb("cT_l", [PX, KX, P], F32R, at1)
        cd_h = sb("cd_h", [PX, KX, B, 2, C], F32R, at1)
        cd_l = sb("cd_l", [PX, KX, B, 2, C], F32R, at1)
        kb_h = sb("kb_h", [P, B, KC, H * C], F32R, at1)
        kb_l = sb("kb_l", [P, B, KC, H * C], F32R, at1)
        vb_h = sb("vb_h", [P, B, KC, P], F32R, at1)
        vb_l = sb("vb_l", [P, B, KC, P], F32R, at1)
        vs_h = sb("vs_h", [P, KC, P], F32R, at1)
        vs_l = sb("vs_l", [P, KC, P], F32R, at1)
        xs1 = sb("xs1", [P, GT, D], F32, at1)
        x1_h = sb("x1_h", [P, KC, GT * P], F32R, at1)
        x1_l = sb("x1_l", [P, KC, GT * P], F32R, at1)
        q1_h = sb("q1_h", [P, KC, GT * P], F32R, at1)
        q1_l = sb("q1_l", [P, KC, GT * P], F32R, at1)
        p1 = sb("p1", [P, GT, H * C], F32, at1)
        m1 = sb("m1", [P, GT, H], F32, at1)
        d1 = sb("d1", [P, GT, H], F32, at1)
        p1T_h = sb("p1T_h", [P, KC, GT * P], F32R, at1)
        p1T_l = sb("p1T_l", [P, KC, GT * P], F32R, at1)
        o1_h = sb("o1_h", [P, KC, GT * P], F32R, at1)
        o1_l = sb("o1_l", [P, KC, GT * P], F32R, at1)
        at1.close()

        ff1 = ExitStack()
        v_raw = sb("v_raw", [P, FW1], F32, ff1)
        v_h = [sb(f"v_h{i}", [P, FW1], F32R, ff1) for i in range(2)]
        v_l = [sb(f"v_l{i}", [P, FW1], F32R, ff1) for i in range(2)]
        b1 = sb("b1", [P, E * FT1], F32, ff1)
        b2 = sb("b2", [P, E, D], F32, ff1)
        cho = ExitStack()
        gate1_w = sb("gate1_w", [P, KC, E], F32, cho)
        xs2 = sb("xs2", [P, GT, D], F32, cho)
        xnT1 = sb("xnT1", [P, GT, KC, P], F32, cho)
        gates = sb("gates", [P, TILES, E], F32, cho)
        thr = sb("thr", [P, E], I32, cho)
        cand = sb("cand", [P, E], I32, cho)
        bit = sb("bit", [P, E], I32, cho)
        over = sb("over", [P, TILES, E], F32, cho)
        tally = sb("tally", [P, E], F32, cho)
        enough = sb("enough", [P, E], U32, cho)
        above = sb("above", [P, TILES, E], F32, cho)
        ties = sb("ties", [P, TILES, E], F32, cho)
        chosen = sb("chosen", [P, TILES, E], F32, cho)
        scan1 = [sb(f"scan1{i}", [P, TILES, E], F32, cho) for i in range(2)]
        totals1 = sb("totals1", [P, TILES, E], F32, cho)
        place_i = sb("place_i", [P, TILES, E], I32, cho)
        row_i = sb("row_i", [P, TILES, E], I32, cho)
        row_f = sb("row_f", [P, TILES, E], F32, cho)
        tile_f = sb("tile_f", [P, TILES, E], F32, cho)
        before1 = sb("before1", [P, P], F32, cho)
        ones1 = sb("ones1", [P, P], F32, cho)
        columns = sb("columns", [P, P], F32, cho)
        lane = sb("lane", [P, 1], F32, cho)
        tile_no = sb("tile_no", [P, TILES], F32, cho)
        hot = sb("hot", [P, 2, E, P], BF16, cho)
        put = sb("put", [P, TILES, E, 2, CT], BF16, cho)
        put_f = sb("put_f", [P, TILES, E, CT], F32, cho)
        found = sb("found", [P, E, 2 * CT], F32, cho)
        cho.close()
        wrk = ExitStack()
        gathered = [sb(f"gathered{i}", [P, CT, XG], F32, wrk) for i in range(2)]
        xe_h = sb("xe_h", [P, KC, CHOSEN], F32R, wrk)
        xe_l = sb("xe_l", [P, KC, CHOSEN], F32R, wrk)
        gl = sb("gl", [P, 2, CHOSEN], F32, wrk)
        g_h = sb("g_h", [P, FT1, CHOSEN], F32R, wrk)
        g_l = sb("g_l", [P, FT1, CHOSEN], F32R, wrk)
        gval = sb("gval", [P, 2, CT], F32, wrk)
        ye1 = sb("ye1", [P, CT, D], F32, wrk)
        wrk.close()
        ff1.close()
        rows1 = nc.dram_tensor("token_rows", [T, XG], F32, kind="Internal").ap()
        rows = nc.dram_tensor("expert_rows", [(ROUTED + TILES) * P, D], F32, kind="Internal").ap()
        results = nc.dram_tensor("expert_results", [(ROUTED + TILES) * P, D], F32, kind="Internal").ap()

        names = """x_in consts w_in ident0 ident1 identr cst stat_s aggr_s veps rstd_s xn_s
            xt_s tp lnf_s lnh_s lnl_s qkv_s raw_s sq_s ss_s rms0 rms_s nrm_s ng_s hi_s lo_s vh_s vl_s t12 ev_a ev_d
            wsp_h wsp_l mask_s c_dve c_act c_pool c_pe qs_s sc_s mx_s exp_s rc_s pn_s pt_s ph_s ring o_s oh_s y_s
            xb_s stored
            cst0 ones_s zero_s zeroed gw_in xs0_s tp0 xnT_s lg_s lgc rt rt_e rt_pe tbl
            scat wr_in ws_h ws_l
            tx xbi xh_s xl_s gu si_s h_s th hh_s hl_s yo ye yst got0 got1 out0
            a1_in a1_h a1_l zk c1_pe c1_act c1_dve vsc xs1_s tp1 x1h x1l q1 q1h q1l sc1 mx1 sb1 e1 sm1 rc1 pn1 pt1 p1h p1l o1 o1h o1l y1 x1a x1b
            v_in vs_hs vs_ls b_in k1c r1 r1_e srch cmpd cnt met own hots hot_pe found_s cnd shf cns eno row1 row1b ga0 ga1 xe_t xe_hs xe_ls h1 gl_s gh_s gls gval_s y1e yb1 ys1 sadd out_i""".split()
        s = {n: sem(n) for n in names}
        block = ctx.enter_context(nc.Block())

        x_tiled = ap["x"].rearrange("(t p) d -> p t d", p=P)
        out_tiled = out.rearrange("(t p) d -> p t d", p=P)

        @block.sync
        def _(sp):
            for g in range(GROUPS):
                sp.dma_start(x[:, g * GT:(g + 1) * GT, :], x_tiled[:, g * GT:(g + 1) * GT, :]).then_inc(s["x_in"], 16)
            sp.dma_start(xc[:], ap["ctx"]).then_inc(s["consts"], 16)
            sp.dma_start(lnx_g[:], ap["lnx_g"]).then_inc(s["consts"], 16)
            sp.dma_start(lnx_b[:], ap["lnx_b"]).then_inc(s["consts"], 16)
            sp.dma_start(ln_g[:], ap["ln_g"]).then_inc(s["consts"], 16)
            sp.dma_start(ln_b[:], ap["ln_b"]).then_inc(s["consts"], 16)
            sp.dma_start(qk_gain[:], ap["qk_gain"].partition_broadcast(P)).then_inc(s["consts"], 16)
            sp.dma_start(bo[:], ap["bo0"].partition_broadcast(P)).then_inc(s["consts"], 16)
            sp.dma_start(mask_u8[:], ap["mask"]).then_inc(s["consts"], 16)
            sp.dma_start(wkvx[:], ap["wkvx"]).then_inc(s["w_in"], 16)
            sp.dma_start(wqkv[:], ap["wqkv"]).then_inc(s["w_in"], 16)
            sp.dma_start(wo[:], ap["wo0"]).then_inc(s["w_in"], 16)
            sp.wait_ge(s["zero_s"], 1)
            for part in (rows[0:ROUTED * P], results[0:ROUTED * P]):
                sp.dma_start(part.rearrange("(n p) d -> p n d", p=P),
                             zeros[:].unsqueeze(1).broadcast_to((P, ROUTED, D))).then_inc(s["zeroed"], 16)
            sp.wait_ge(s["xb_s"], TILES)
            sp.dma_start(gate_w[:], ap["gate0"]).then_inc(s["gw_in"], 16)
            sp.wait_ge(s["xn_s"], 3 * TILES)
            with sp.Fori(0, SHARED) as n:
                sp.wait_ge(s["tx"], n)
                sp.dma_start(xb[:], xn[:, ds(n, 1), :].rearrange("p o d -> p (o d)")).then_inc(s["xbi"], 16)

            def load_block(m):
                sp.wait_ge(s["tx"], m + SHARED)
                sp.dma_start(xb[:], rows[ds(m * P, P), :]).then_inc(s["xbi"], 16)

            sp.wait_ge(s["scat"], 2 * TILES * 16)
            load_block(0)
            sp.wait_ge(s["tbl"], 2)
            with sp.Fori(0, E) as e:
                first = sp.value_load(table[0:1, 0, ds(e + 1, 1)], min_val=0, max_val=ROUTED - 2)
                count = sp.value_load(table[0:1, 1, ds(e + 1, 1)], min_val=1, max_val=TILES)
                with sp.Fori(0, count) as i:
                    n = sp.snap(first + i + SHARED)
                    load_block(first + i + 1)
                    sp.wait_ge(s["ye"], n + 1)
                    sp.dma_start(results[ds((first + i) * P, P), :], y_sb[:]).then_inc(s["yst"], 16)

            sp.wait_ge(s["out0"], TILES)
            sp.dma_start(xc1[:], ap["ctx"]).then_inc(s["a1_in"], 16)
            sp.dma_start(c_raw[:], ap["wkv1"]).then_inc(s["a1_in"], 16)
            sp.dma_start(a_raw[:], ap["wqo1"]).then_inc(s["a1_in"], 16)
            sp.dma_start(bo1[:], ap["bo1"].partition_broadcast(P)).then_inc(s["a1_in"], 16)

            sp.wait_ge(s["x1b"], TILES)
            sp.dma_start(out_tiled, x[:]).then_inc(s["stored"], 16)
            sp.dma_start(gate1_w[:], ap["gate1"]).then_inc(s["gw_in"], 16)
            sp.dma_start(b1[:], ap["b1"]).then_inc(s["b_in"], 16)
            sp.dma_start(b2[:].rearrange("p e d -> p (e d)"), ap["b2"].partition_broadcast(P)).then_inc(s["b_in"], 16)
            rows1_tiled = rows1.rearrange("(t p) d -> p t d", p=P)
            sp.wait_ge(s["xn_s"], 5 * TILES)
            sp.dma_start(rows1_tiled[:, :, 0:D], xn[:]).then_inc(s["row1"], 16)
            sp.wait_ge(s["r1"], R1_GATES)
            sp.dma_start(rows1_tiled[:, :, D:XG], gates[:]).then_inc(s["row1"], 16)
            sp.wait_ge(s["row1"], 32)
            sp.wait_ge(s["stored"], 16)

        @block.gpsimd
        def _(pool):
            pool.memset(zeros[:], 0.0).then_inc(s["zero_s"], 1)
            pool.memset(ident[:], 0.0).then_inc(s["ident0"], 1)
            pool.memset(neg_half[:], -0.5).then_inc(s["cst"], 1)
            pool.wait_ge(s["ident0"], 1)
            pool.affine_select(out=ident[:], in_=ident[:], compare_op=ALU.not_equal, fill=1.0, base=0,
                               pattern=[[-1, P]], channel_multiplier=1).then_inc(s["ident1"], 1)
            pool.memset(mask_rows[:], 0.0).then_inc(s["cst"], 1)
            pool.memset(first_row[:], 0.0).then_inc(s["cst"], 1)
            pool.wait_ge(s["cst"], 3)
            pool.memset(mask_rows[0:1], -BIG).then_inc(s["cst"], 1)
            pool.memset(first_row[0:1], 1.0).then_inc(s["cst"], 1)
            pool.wait_ge(s["consts"], 8 * 16)
            pool.tensor_scalar(qk_gain[:, 0:D], qk_gain[:, 0:D], HD ** -0.5, None, ALU.mult).then_inc(s["cst"], 1)
            pool.wait_ge(s["cst"], 6)

            pool.wait_ge(s["c_dve"], 2)
            pool.tensor_scalar(crs[:], cmv[:, 1:2], LN_EPS, None, ALU.add).then_inc(s["c_pool"], 1)
            pool.wait_ge(s["c_pool"], 1)
            pool.tensor_tensor(crs[:], crs[:], neg_half[:, 0:1], ALU.pow).then_inc(s["c_pool"], 1)

            def inverse_std(n):
                pool.wait_ge(s["aggr_s"], TILES * (n + 1))
                pool.tensor_scalar(rstd[:], mean_var[:, :, 1], LN_EPS, None, ALU.add).then_inc(s["veps"], 1)
                pool.wait_ge(s["veps"], n + 1)
                pool.tensor_tensor(rstd[:], rstd[:], neg_half[:, 0:TILES], ALU.pow).then_inc(s["rstd_s"], 1)

            pool.wait_ge(s["wsp_h"], 3)
            pool.tensor_tensor(wkvx_l[:], wkvx[:], wkvx_h[:].bitcast(F32), ALU.subtract).then_inc(s["wsp_l"], 1)
            pool.tensor_tensor(wqkv_l[:], wqkv[:], wqkv_h[:].bitcast(F32), ALU.subtract).then_inc(s["wsp_l"], 1)
            pool.tensor_tensor(wo_l[:], wo[:], wo_h[:].bitcast(F32), ALU.subtract).then_inc(s["wsp_l"], 1)

            pool.wait_ge(s["c_dve"], 6)
            pool.tensor_scalar(cms[:], cms[:], 1.0 / HD, RMS_EPS ** 2, ALU.mult, ALU.max).then_inc(s["c_pool"], 1)
            pool.wait_ge(s["c_pool"], 3)
            pool.tensor_tensor(cms[:], cms[:], neg_half[:, 0:H], ALU.pow).then_inc(s["c_pool"], 1)

            for n in range(2):
                inverse_std(n)

            with pool.Fori(0, B) as b:
                with pool.Fori(0, GPB) as gg:
                    g = b * GPB + gg
                    for t in range(GT):
                        pool.wait_ge(s["lnh_s"], g * GT + t + 1)
                        pool.tensor_tensor(lnl[:, t], lnf[:, t], lnh[:, t].bitcast(F32), ALU.subtract).then_inc(s["lnl_s"], 1)
                    pool.wait_ge(s["ss_s"], (g + 1) * GT)
                    pool.sem_inc(s["met"], 1)
                    pool.tensor_scalar(rms[:], ssq[:], 1.0 / HD, RMS_EPS ** 2, ALU.mult, ALU.max).then_inc(s["rms0"], 1)
                    pool.wait_ge(s["rms0"], g + 1)
                    pool.tensor_tensor(rms[:], rms[:], neg_half[:, 0:2 * H * GT].rearrange("p (t h) -> p t h", t=GT),
                                       ALU.pow).then_inc(s["rms_s"], 1)
                    for t in range(GT):
                        pool.wait_ge(s["nrm_s"], g * GT + t + 1)
                        pool.tensor_tensor(qkv[:, t, 0:2 * D], qkv[:, t, 0:2 * D], qk_gain[:], ALU.mult).then_inc(s["ng_s"], 1)
                        pool.wait_ge(s["vh_s"], g * GT + t + 1)
                        vt = v[:, ds(gg * GT + t, 1), :, :]
                        pool.tensor_tensor(vt[:, 0, :, HD:P], qkv[:, t, 2 * D:].rearrange("p (h d) -> p h d", h=H),
                                           vt[:, 0, :, 0:HD].bitcast(F32), ALU.subtract).then_inc(s["vl_s"], 1)
                with pool.Fori(0, GPB) as gg:
                    g = b * GPB + gg
                    pool.wait_ge(s["ev_a"], (b + 1) * GPB * 6)
                    pool.tensor_copy(qs[:], qT[:, :, ds(gg * GT * P, GT * P)]).then_inc(s["qs_s"], 1)
                    for u in range(UNITS):
                        pool.wait_ge(s["rc_s"], g * UNITS + u + 1)
                        pool.sem_inc(s["met"], 1)
                        pool.tensor_scalar(prob[:, u % 3, :], prob[:, u % 3, :], rdenom[:, u:u + 1], None,
                                           ALU.mult).then_inc(s["pn_s"], 1)
                    for t in range(GT):
                        pool.wait_ge(s["ring"], g * RING + RING - GT + t + 1)
                        xg = x[:, ds(g * GT + t, 1), :]
                        pool.tensor_tensor(xg[:, 0], xg[:, 0], bo[:], ALU.add).then_inc(s["xb_s"], 1)

            pool.wait_ge(s["xb_s"], TILES)
            pool.memset(ones[:], 1.0).then_inc(s["ones_s"], 1)
            pool.memset(before[:], 1.0).then_inc(s["ones_s"], 1)
            pool.iota(favour[:], pattern=[[0, TILES], [-1, E]], base=E, channel_multiplier=0,
                      allow_small_or_imprecise_dtypes=True).then_inc(s["ones_s"], 1)
            pool.wait_ge(s["ones_s"], 3)
            pool.affine_select(out=before[:], in_=before[:], compare_op=ALU.is_ge, fill=0.0, base=-1,
                               pattern=[[1, P]], channel_multiplier=-1).then_inc(s["ones_s"], 1)
            inverse_std(2)

            def load_weights(w):
                pool.dma_start(w_raw[:], ap["experts0"][ds(w, 1)].rearrange("o p c -> p (o c)")).then_inc(s["wr_in"], 16)

            def split_weights(w, side):
                pool.wait_ge(s["wr_in"], 16 * (w + 1))
                pool.sem_inc(s["met"], 1)
                pool.tensor_copy(w_h[side][:], w_raw[:]).then_inc(s["ws_h"], 1)
                pool.wait_ge(s["ws_h"], w + 1)
                pool.tensor_tensor(w_l[side][:], w_raw[:], w_h[side][:].bitcast(F32), ALU.subtract).then_inc(s["ws_l"], 1)
                pool.wait_ge(s["ws_l"], w + 1)

            load_weights(0)
            split_weights(0, 0)
            load_weights(1)
            split_weights(1, 1)
            load_weights(2)
            pool.wait_ge(s["zeroed"], 32)
            pool.wait_ge(s["tbl"], 2)
            for t in range(TILES):
                for k in range(2):
                    pool.indirect_dma_start(out=rows[0:ROUTED * P], out_offset=bass.IndirectOffsetOnAxis(ap=slot[k][:, t:t + 1], axis=0),
                                            in_=xn[:, t, :], in_offset=None, bounds_check=ROUTED * P - 1,
                                            oob_is_err=False).then_inc(s["scat"], 16)
            with pool.Fori(0, (E - 2) // 2) as p:
                for side in range(2):
                    w = p * 2 + 2 + side
                    done = pool.value_load(table[0:1, 0, ds(w - 1, 1)], min_val=0, max_val=ROUTED)
                    pool.wait_ge(s["yo"], done + SHARED)
                    pool.sem_inc(s["met"], 1)
                    split_weights(w, side)
                    load_weights(w + 1)
            done = pool.value_load(table[0:1, 0, E - 1:E], min_val=0, max_val=ROUTED)
            pool.wait_ge(s["yo"], done + SHARED)
            pool.sem_inc(s["met"], 1)
            split_weights(E, 0)
            total = pool.value_load(table[0:1, 0, E + 1:E + 2], min_val=1, max_val=ROUTED)
            pool.wait_ge(s["yst"], total * 16)
            pool.sem_inc(s["met"], 1)
            for t in range(TILES):
                for k in range(2):
                    n = 2 * t + k
                    if n >= 4:
                        pool.wait_ge(s["out0"], (n - 4) // 2 + 1)
                    pool.indirect_dma_start(out=y_got[:, n % 4, :], out_offset=None, in_=results[0:ROUTED * P],
                                            in_offset=bass.IndirectOffsetOnAxis(ap=slot[k][:, t:t + 1], axis=0),
                                            bounds_check=ROUTED * P - 1, oob_is_err=False).then_inc(s[f"got{t % 2}"], 16)

            pool.wait_ge(s["a1_h"], 2)
            pool.wait_ge(s["a1_in"], 64)
            pool.tensor_tensor(c_l[:], c_raw[:], c_h[:].bitcast(F32), ALU.subtract).then_inc(s["a1_l"], 1)
            pool.tensor_tensor(a_l[:], a_raw[:], a_h[:].bitcast(F32), ALU.subtract).then_inc(s["a1_l"], 1)
            inverse_std(3)
            with pool.Fori(0, GROUPS) as g:
                for t in range(GT):
                    pool.wait_ge(s["x1a"], g * GT + t + 1)
                    xg = x[:, ds(g * GT + t, 1), :]
                    pool.tensor_tensor(xg[:, 0], xg[:, 0], bo1[:], ALU.add).then_inc(s["x1b"], 1)

            pool.wait_ge(s["x1b"], TILES)
            pool.memset(ones1[:], 1.0).then_inc(s["k1c"], 1)
            pool.memset(before1[:], 1.0).then_inc(s["k1c"], 1)
            pool.iota(columns[:], pattern=[[1, P]], base=0, channel_multiplier=0,
                      allow_small_or_imprecise_dtypes=True).then_inc(s["k1c"], 1)
            pool.iota(lane[:], pattern=[[0, 1]], base=0, channel_multiplier=1,
                      allow_small_or_imprecise_dtypes=True).then_inc(s["k1c"], 1)
            pool.iota(tile_no[:], pattern=[[1, TILES]], base=0, channel_multiplier=0,
                      allow_small_or_imprecise_dtypes=True).then_inc(s["k1c"], 1)
            pool.wait_ge(s["k1c"], 5)
            pool.affine_select(out=before1[:], in_=before1[:], compare_op=ALU.is_ge, fill=0.0, base=-1,
                               pattern=[[1, P]], channel_multiplier=-1).then_inc(s["k1c"], 1)
            inverse_std(4)

            def load_weights1(w):
                pool.dma_start(v_raw[:], ap["experts1"][ds(w, 1)].rearrange("o p c -> p (o c)")).then_inc(s["v_in"], 16)

            def split_weights1(w, side):
                pool.wait_ge(s["v_in"], 16 * (w + 1))
                pool.sem_inc(s["met"], 1)
                pool.tensor_copy(v_h[side][:], v_raw[:]).then_inc(s["vs_hs"], 1)
                pool.wait_ge(s["vs_hs"], w + 1)
                pool.tensor_tensor(v_l[side][:], v_raw[:], v_h[side][:].bitcast(F32), ALU.subtract).then_inc(s["vs_ls"], 1)
                pool.wait_ge(s["vs_ls"], w + 1)

            def gather(e, side):
                pool.tensor_copy(own[side][:], tokens[:, ds(e, 1), :].rearrange("p o t -> p (o t)")).then_inc(s["own"], 1)
                pool.wait_ge(s["own"], e + 1)
                pool.sem_inc(s["met"], 1)
                for t in range(CT):
                    pool.indirect_dma_start(
                        out=gathered[side][:, t, :], out_offset=None, in_=rows1,
                        in_offset=bass.IndirectOffsetOnAxis(ap=own[side][:, t:t + 1], axis=0),
                        bounds_check=T - 1, oob_is_err=False).then_inc(s[f"ga{side}"], 16)

            load_weights1(0)
            split_weights1(0, 0)
            load_weights1(1)
            split_weights1(1, 1)
            pool.wait_ge(s["row1"], 32)
            pool.wait_ge(s["found_s"], 2)
            gather(0, 0)

            def expert(e, side, last):
                pool.wait_ge(s["sadd"], e * (CT * 16))
                if not last:
                    pool.wait_ge(s["ys1"], e * CT)
                    pool.sem_inc(s["met"], 1)
                    gather(e + 1, 1 - side)
                pool.wait_ge(s["ys1"], (e + 1) * CT)
                pool.sem_inc(s["met"], 1)
                for t in range(CT):
                    pool.indirect_dma_start(
                        out=out, out_offset=bass.IndirectOffsetOnAxis(ap=own[side][:, t:t + 1], axis=0),
                        in_=ye1[:, t, :], in_offset=None, bounds_check=T - 1, oob_is_err=True,
                        compute_op=ALU.add).then_inc(s["sadd"], 16)

            pool.wait_ge(s["stored"], 16)
            with pool.Fori(0, E // 2 - 1) as p:
                for side in range(2):
                    e = 2 * p + side
                    load_weights1(e + 2)
                    expert(e, side, False)
                    split_weights1(e + 2, side)
            expert(E - 2, 0, False)
            expert(E - 1, 1, True)
            pool.wait_ge(s["sadd"], E * CT * 16)

        @block.scalar
        def _(act):
            def copy(o, i, name, n=1):
                act.activation(o, i, ACT.Copy).then_inc(s[name], n)

            act.wait_ge(s["ident1"], 1)
            copy(ident_r[:], ident[:], "identr")
            act.wait_ge(s["w_in"], 48)
            copy(wkvx_h[:], wkvx[:], "wsp_h")
            copy(wqkv_h[:], wqkv[:], "wsp_h")
            copy(wo_h[:], wo[:], "wsp_h")
            act.wait_ge(s["c_dve"], 5)
            copy(ch[:], cf[:], "c_act")
            act.wait_ge(s["c_pe"], 2)
            copy(ckv[:], psum[:, 1, :], "c_act")
            act.wait_ge(s["c_act"], 2)
            act.activation(csq[:], ckv[:, 0:D], ACT.Square).then_inc(s["c_act"], 1)
            copy(v[:, KT - 1, :, 0:HD], ckv[:, D:].rearrange("p (h d) -> p h d", h=H), "c_act")
            act.wait_ge(s["c_dve"], 9)
            khead = ckv[:, 0:D].rearrange("p (h d) -> p h d", h=H).unsqueeze(2).broadcast_to((P, H, 2, HD))
            copy(cparts[:, 0:H, :].rearrange("p h (r d) -> p h r d", r=2), khead, "c_act")
            act.wait_ge(s["c_pe"], 4)
            copy(kT[:, :, 0, CTX0:], psum[:, 2, :].rearrange("p (h k) -> p h k", h=H), "c_act")

            with act.Fori(0, B) as b:
                with act.Fori(0, GPB) as gg:
                    g = b * GPB + gg
                    for t in range(GT):
                        act.wait_ge(s["lnf_s"], (g * GT + t + 1) * KC)
                        copy(lnh[:, t], lnf[:, t], "lnh_s")
                    for t in range(GT):
                        act.wait_ge(s["qkv_s"], g * GT + t + 1)
                        copy(qkv[:, t, :], psum[:, 2 * (t % 2):2 * (t % 2) + 2, :].rearrange("p b c -> p (b c)")[:, 0:3 * D],
                             "raw_s")
                        act.wait_ge(s["raw_s"], g * GT + t + 1)
                        if t >= 2:
                            act.wait_ge(s["ss_s"], g * GT + t - 1)
                        act.activation(sq[:, t % 2, :], qkv[:, t, 0:2 * D], ACT.Square).then_inc(s["sq_s"], 1)
                        vt = v[:, ds(gg * GT + t, 1), :, 0:HD]
                        copy(vt[:, 0], qkv[:, t, 2 * D:].rearrange("p (h d) -> p h d", h=H), "vh_s")

                    def high_parts(t):
                        act.wait_ge(s["ng_s"], g * GT + t + 1)
                        if t >= 2:
                            act.wait_ge(s["t12"], g * 12 + 3 * (t - 1))
                        copy(parts[:, t % 2, 0:H, 0:HD], qkv[:, t, 0:D].rearrange("p (h d) -> p h d", h=H), "hi_s")
                        kk = qkv[:, t, D:2 * D].rearrange("p (h d) -> p h d", h=H).unsqueeze(2).broadcast_to((P, H, 2, HD))
                        copy(parts[:, t % 2, H:2 * H, :].rearrange("p h (r d) -> p h r d", r=2), kk, "hi_s")

                    def evacuate(t):
                        for c in range(3):
                            if (3 * t + c) % 2 == 0:
                                act.wait_ge(s["t12"], g * 12 + 3 * t + c + 1)
                                src = psum[:, 6, :].rearrange("p (h k) -> p h k", h=H)
                                cols = ds(gg * (GT * P) + t * P, P)
                                dst = qT[:, :, cols] if c == 0 else kT[:, :, c - 1, cols]
                                copy(dst, src, "ev_a")

                    high_parts(0)
                    for t in range(GT):
                        if t + 1 < GT:
                            high_parts(t + 1)
                        evacuate(t)
                with act.Fori(0, GPB) as gg:
                    g = b * GPB + gg

                    def exponentials(u):
                        act.wait_ge(s["mx_s"], g * UNITS + u + 1)
                        if u >= 3:
                            act.wait_ge(s["pt_s"], (g * UNITS + u - 2) * 3)
                        z = 3 * (u % 2)
                        act.activation(prob[:, u % 3, :], psum[:, z:z + 3, :].rearrange("p b c -> p (b c)")[:, 0:KEYS],
                                       ACT.Exp, bias=neg_max[:, u:u + 1],
                                       accum_out=denom[:, u:u + 1]).then_inc(s["exp_s"], 1)

                    ring = [0]

                    def out_high(h):
                        bank = 6 + ring[0] % 2
                        ring[0] += 1
                        act.wait_ge(s["o_s"], g * H + h + 1)
                        copy(oT_h[:, h, :], psum[:, bank, :], "oh_s")

                    exponentials(0)
                    for u in range(UNITS):
                        if u + 1 < UNITS:
                            exponentials(u + 1)
                        if u % GT == 0 and u:
                            out_high(u // GT - 1)
                        for c in range(3):
                            bank = 6 + ring[0] % 2
                            ring[0] += 1
                            act.wait_ge(s["pt_s"], (g * UNITS + u) * 3 + c + 1)
                            n = min(4, KT - 4 * c)
                            copy(pT_h[:, 4 * c:4 * c + n, (u % GT) * P:(u % GT + 1) * P],
                                 psum[:, bank, 0:n * P].rearrange("p (k c) -> p k c", k=n), "ph_s")
                    out_high(H - 1)

            def gate_logits(layer, xs0, xnT, logit):
                act.wait_ge(s["xn_s"], (3 if layer == 0 else 5) * TILES)
                with act.Fori(0, GROUPS) as g0:
                    g = g0 + layer * GROUPS
                    for t in range(GT):
                        copy(xs0[:, t, :], xn[:, ds(g0 * GT + t, 1), :].rearrange("p o d -> p (o d)"), "xs0_s")
                    for t in range(GT):
                        act.wait_ge(s["tp0"], g * GT + t + 1)
                        copy(xnT[:, t], psum[:, t, 0:D].rearrange("p (k c) -> p k c", k=KC), "xnT_s")
                    act.wait_ge(s["lg_s"], g * GT + GT)
                    copy(logit[:, ds(g0 * GT, GT), :], psum[:, 4, 0:GT * E].rearrange("p (t e) -> p t e", t=GT), "lgc")

            gate_logits(0, xs0, xnT, logit)
            act.wait_ge(s["rt"], RT_SHIFTED)
            act.activation(logit[:], logit[:], ACT.Exp).then_inc(s["rt_e"], 1)

            def x_high(n):
                act.wait_ge(s["tx"], n + 1)
                copy(xbT_h[:], psum[:, 4, 0:D].rearrange("p (k c) -> p k c", k=KC), "xh_s")

            def block_high(n):
                for c, (lo, hi) in enumerate(((0, FA), (FA, F))):
                    act.wait_ge(s["gu"], n * 4 + 2 * c + 1)
                    act.activation(silu[:, lo:hi], psum[:, 2 * c, 0:hi - lo], ACT.Silu).then_inc(s["si_s"], 1)
                x_high(n + 1)
                for c in range(2):
                    act.wait_ge(s["th"], n * 2 + c + 1)
                    copy(hT_h[:, 3 * c:3 * c + 3, :], psum[:, 5 + c, 0:3 * P].rearrange("p (k c) -> p k c", k=3), "hh_s")

            x_high(0)
            with act.Fori(0, SHARED) as n:
                block_high(n)
            act.wait_ge(s["tbl"], 2)
            with act.Fori(0, E) as e:
                first = act.value_load(table[0:1, 0, ds(e + 1, 1)], min_val=0, max_val=ROUTED - 2)
                count = act.value_load(table[0:1, 1, ds(e + 1, 1)], min_val=1, max_val=TILES)
                with act.Fori(0, count) as i:
                    n = act.snap(first + i + SHARED)
                    block_high(n)
                    act.wait_ge(s["yo"], n + 1)
                    act.wait_ge(s["yst"], (first + i) * 16)
                    copy(y_sb[:], psum[:, 7, 0:D], "ye")

            act.wait_ge(s["a1_in"], 64)
            copy(c_h[:], c_raw[:], "a1_h")
            copy(a_h[:], a_raw[:], "a1_h")
            act.wait_ge(s["c1_pe"], 1)
            copy(cT_h[:], psum[0:PX, 0, 0:KX * P].rearrange("p (k c) -> p k c", k=KX), "c1_act")
            act.wait_ge(s["c1_dve"], 1)
            for k in range(KX):
                for src, dst in ((cT_h, cd_h), (cT_l, cd_l)):
                    act.wait_ge(s["c1_act"], 1)
                    copy(dst[:, k], src[:, k, :].bitcast(F32).rearrange("p (b c) -> p b c", b=B).unsqueeze(2)
                         .broadcast_to((PX, B, 2, C)), "c1_act")
            act.wait_ge(s["c1_pe"], 3)
            act.wait_ge(s["zk"], 2)
            for k in range(KC):
                for hh in range(2):
                    half = slice(hh * C, (hh + 1) * C)
                    head = 2 * k + hh
                    copy(kb_h[half, :, k, head * C:(head + 1) * C],
                         psum[half, 1, k * P:(k + 1) * P].rearrange("p (b c) -> p b c", b=B), "c1_act")
                    copy(vb_h[half, :, k, hh * HD:(hh + 1) * HD],
                         psum[half, 2, :].rearrange("p (b d) -> p b d", b=B)[:, :, head * HD:(head + 1) * HD], "c1_act")
            act.wait_ge(s["c1_dve"], 1 + 4 * KC)
            act.wait_ge(s["c1_act"], 5 + 4 * KC)
            act.wait_ge(s["xn_s"], 4 * TILES)
            with act.Fori(0, B) as b:
                with act.Fori(0, GPB) as gg:
                    g = b * GPB + gg
                    copy(vs_h[:], vb_h[:, ds(b, 1)].rearrange("p o k d -> p (o k) d").bitcast(F32), "vsc")
                    copy(vs_l[:], vb_l[:, ds(b, 1)].rearrange("p o k d -> p (o k) d").bitcast(F32), "vsc")
                    for t in range(GT):
                        copy(xs1[:, t, :], xn[:, ds(g * GT + t, 1), :].rearrange("p o d -> p (o d)"), "xs1_s")
                    for t in range(GT):
                        act.wait_ge(s["tp1"], g * GT + t + 1)
                        copy(x1_h[:, :, t * P:(t + 1) * P], psum[:, t, 0:D].rearrange("p (k c) -> p k c", k=KC), "x1h")
                    for k in range(KC):
                        act.wait_ge(s["q1"], g * KC + k + 1)
                        act.activation(q1_h[:, k, :], psum[:, 4 + k, :], ACT.Copy, scale=HD ** -0.5).then_inc(s["q1h"], 1)
                    for t in range(GT):
                        act.wait_ge(s["sb1"], g * GT + t + 1)
                        act.activation(p1[:, t, :], p1[:, t, :], ACT.Exp).then_inc(s["e1"], 1)
                    for t in range(GT):
                        act.wait_ge(s["pt1"], g * GT + t + 1)
                        copy(p1T_h[:, :, t * P:(t + 1) * P], psum[:, 4 + t, 0:D].rearrange("p (k c) -> p k c", k=KC), "p1h")
                    for k in range(KC):
                        act.wait_ge(s["o1"], g * KC + k + 1)
                        copy(o1_h[:, k, :], psum[:, k, :], "o1h")

            gate_logits(1, xs2, xnT1, gates)
            act.wait_ge(s["lgc"], 2 * GROUPS)
            act.activation(gates[:], gates[:], ACT.Exp, scale=-1.0).then_inc(s["r1_e"], 1)

            def rows_high(n, count):
                for t in range(CT):
                    act.wait_ge(s["xe_t"], n * CT + t + 1)
                    copy(xe_h[:, :, t * P:(t + 1) * P], psum[:, 6 + t % 2, 0:D].rearrange("p (k c) -> p k c", k=KC), "xe_hs")

            def expert1(e, last):
                for f in range(FT1):
                    act.wait_ge(s["h1"], e * FT1 + f + 1)
                    if f >= 2:
                        act.wait_ge(s["gls"], e * FT1 + f - 1)
                    act.activation(gl[:, f % 2, :], psum[:, f % 2, :], ACT.Gelu, bias=b1[:, ds(e * FT1 + f, 1)]).then_inc(s["gl_s"], 1)
                if not last:
                    rows_high(e + 1, CT)

            act.wait_ge(s["b_in"], 32)
            rows_high(0, CT)
            with act.Fori(0, E - 1) as e:
                expert1(e, False)
            expert1(E - 1, True)

        @block.vector
        def _(dve):
            def norm(n, src):
                for t in range(TILES):
                    dve.bn_stats(stat[:, t, :], src[:, t, :]).then_inc(s["stat_s"], 1)
                dve.wait_ge(s["stat_s"], TILES * (n + 1))
                for t in range(TILES):
                    dve.bn_aggr(mean_var[:, t, :], stat[:, t, :]).then_inc(s["aggr_s"], 1)
                dve.wait_ge(s["rstd_s"], n + 1)
                for t in range(TILES):
                    dve.tensor_scalar(xn[:, t, :], src[:, t, :], mean_var[:, t, 0:1], rstd[:, t:t + 1],
                                      ALU.subtract, ALU.mult).then_inc(s["xn_s"], 1)

            dve.wait_ge(s["consts"], 8 * 16)
            dve.bn_stats(cstat[:], xc[:]).then_inc(s["c_dve"], 1)
            dve.wait_ge(s["c_dve"], 1)
            dve.bn_aggr(cmv[:], cstat[:]).then_inc(s["c_dve"], 1)
            dve.wait_ge(s["c_pool"], 2)
            dve.tensor_scalar(xcn[:], xc[:], cmv[:, 0:1], crs[:], ALU.subtract, ALU.mult).then_inc(s["c_dve"], 1)
            dve.wait_ge(s["c_pe"], 1)
            for k in range(KX):
                dve.tensor_scalar(cf[:, k, :], psum[0:PX, 0, k * P:(k + 1) * P], lnx_g[:, k:k + 1], lnx_b[:, k:k + 1],
                                  ALU.mult, ALU.add).then_inc(s["c_dve"], 1)
            dve.wait_ge(s["c_act"], 1)
            dve.tensor_copy(mask_f[:], mask_u8[:]).then_inc(s["mask_s"], 1)
            dve.wait_ge(s["mask_s"], 1)
            dve.wait_ge(s["cst"], 5)
            for b in range(B):
                dve.tensor_scalar(mask_rows[0:1, b, b * C:(b + 1) * C], mask_f[:, b * C:(b + 1) * C], 1.0, BIG,
                                  ALU.subtract, ALU.mult).then_inc(s["mask_s"], 1)
            dve.tensor_tensor(cl[:], cf[:], ch[:].bitcast(F32), ALU.subtract).then_inc(s["mask_s"], 1)
            dve.wait_ge(s["c_act"], 3)
            dve.tensor_reduce(cms[:], csq[:].rearrange("p (h d) -> p h d", h=H), AX.X, ALU.add).then_inc(s["c_dve"], 1)
            dve.wait_ge(s["c_pool"], 4)
            ck = ckv[:, 0:D].rearrange("p (h d) -> p h d", h=H)
            dve.tensor_tensor(ck, ck, cms[:].unsqueeze(2).broadcast_to((P, H, HD)), ALU.mult).then_inc(s["c_dve"], 1)
            dve.wait_ge(s["c_dve"], 7)
            dve.tensor_tensor(ckv[:, 0:D], ckv[:, 0:D], qk_gain[:, D:], ALU.mult).then_inc(s["c_dve"], 1)
            dve.wait_ge(s["c_act"], 4)
            dve.tensor_tensor(v[:, KT - 1, :, HD:], ckv[:, D:].rearrange("p (h d) -> p h d", h=H),
                              v[:, KT - 1, :, 0:HD].bitcast(F32), ALU.subtract).then_inc(s["c_dve"], 1)
            dve.wait_ge(s["c_act"], 5)
            khead = ck.unsqueeze(2).broadcast_to((P, H, 2, HD))
            dve.tensor_tensor(cparts[:, H:, :].rearrange("p h (r d) -> p h r d", r=2), khead,
                              cparts[:, 0:H, :].rearrange("p h (r d) -> p h r d", r=2).bitcast(F32),
                              ALU.subtract).then_inc(s["c_dve"], 1)
            dve.wait_ge(s["c_pe"], 4)
            dve.tensor_copy(kT[:, :, 1, CTX0:], psum[:, 3, :].rearrange("p (h k) -> p h k", h=H)).then_inc(s["c_dve"], 1)

            dve.wait_ge(s["x_in"], 16 * GROUPS)
            norm(0, x)
            dve.wait_ge(s["xn_s"], TILES)
            norm(1, xn)
            dve.wait_ge(s["xn_s"], 2 * TILES)

            with dve.Fori(0, B) as b:
                with dve.Fori(0, GPB) as gg:
                    g = b * GPB + gg
                    for t in range(GT):
                        dve.tensor_copy(xt[:, t, :], xn[:, ds(g * GT + t, 1), :].rearrange("p o d -> p (o d)")).then_inc(s["xt_s"], 1)
                    for t in range(GT):
                        dve.wait_ge(s["tp"], g * GT + t + 1)
                        for k in range(KC):
                            dve.tensor_scalar(lnf[:, t, k, :], psum[:, 4 + t, k * P:(k + 1) * P], ln_g[:, k:k + 1],
                                              ln_b[:, k:k + 1], ALU.mult, ALU.add).then_inc(s["lnf_s"], 1)
                    for t in range(GT):
                        dve.wait_ge(s["sq_s"], g * GT + t + 1)
                        dve.tensor_reduce(ssq[:, t, :], sq[:, t % 2, :].rearrange("p (h d) -> p h d", d=HD), AX.X,
                                          ALU.add).then_inc(s["ss_s"], 1)
                    dve.wait_ge(s["rms_s"], g + 1)
                    for t in range(GT):
                        qk = qkv[:, t, 0:2 * D].rearrange("p (h d) -> p h d", d=HD)
                        dve.tensor_tensor(qk, qk, rms[:, t, :].unsqueeze(2).broadcast_to((P, 2 * H, HD)),
                                          ALU.mult).then_inc(s["nrm_s"], 1)

                    def low_parts(t):
                        dve.wait_ge(s["hi_s"], (g * GT + t + 1) * 2)
                        dve.tensor_tensor(parts[:, t % 2, 0:H, HD:], qkv[:, t, 0:D].rearrange("p (h d) -> p h d", h=H),
                                          parts[:, t % 2, 0:H, 0:HD].bitcast(F32), ALU.subtract).then_inc(s["lo_s"], 1)
                        kk = qkv[:, t, D:2 * D].rearrange("p (h d) -> p h d", h=H).unsqueeze(2).broadcast_to((P, H, 2, HD))
                        dve.tensor_tensor(parts[:, t % 2, 2 * H:, :].rearrange("p h (r d) -> p h r d", r=2), kk,
                                          parts[:, t % 2, H:2 * H, :].rearrange("p h (r d) -> p h r d", r=2).bitcast(F32),
                                          ALU.subtract).then_inc(s["lo_s"], 1)

                    def evacuate(t):
                        for c in range(3):
                            if (3 * t + c) % 2:
                                dve.wait_ge(s["t12"], g * 12 + 3 * t + c + 1)
                                src = psum[:, 7, :].rearrange("p (h k) -> p h k", h=H)
                                cols = ds(gg * (GT * P) + t * P, P)
                                dst = qT[:, :, cols] if c == 0 else kT[:, :, c - 1, cols]
                                dve.tensor_copy(dst, src).then_inc(s["ev_d"], 1)

                    low_parts(0)
                    for t in range(GT):
                        if t + 1 < GT:
                            low_parts(t + 1)
                        evacuate(t)
                with dve.Fori(0, GPB) as gg:
                    g = b * GPB + gg
                    ring = [0]

                    def maxima(u):
                        dve.wait_ge(s["sc_s"], g * UNITS + u + 1)
                        z = 3 * (u % 2)
                        dve.tensor_reduce(neg_max[:, u:u + 1], psum[:, z:z + 3, :].rearrange("p b c -> p (b c)")[:, 0:KEYS],
                                          AX.X, ALU.max, negate=True).then_inc(s["mx_s"], 1)

                    def reciprocals(u):
                        dve.wait_ge(s["exp_s"], g * UNITS + u + 1)
                        dve.reciprocal(rdenom[:, u:u + 1], denom[:, u:u + 1]).then_inc(s["rc_s"], 1)

                    def out_low(h):
                        bank = 6 + ring[0] % 2
                        ring[0] += 1
                        dve.wait_ge(s["oh_s"], g * H + h + 1)
                        dve.tensor_tensor(oT_l[:, h, :], psum[:, bank, :], oT_h[:, h, :].bitcast(F32),
                                          ALU.subtract).then_inc(s["ring"], 1)

                    maxima(0)
                    reciprocals(0)
                    for u in range(UNITS):
                        if u + 1 < UNITS:
                            maxima(u + 1)
                        if u % GT == 0 and u:
                            out_low(u // GT - 1)
                        for c in range(3):
                            bank = 6 + ring[0] % 2
                            ring[0] += 1
                            n = min(4, KT - 4 * c)
                            cols = slice((u % GT) * P, (u % GT + 1) * P)
                            dve.wait_ge(s["ph_s"], (g * UNITS + u) * 3 + c + 1)
                            dve.tensor_tensor(pT_l[:, 4 * c:4 * c + n, cols],
                                              psum[:, bank, 0:n * P].rearrange("p (k c) -> p k c", k=n),
                                              pT_h[:, 4 * c:4 * c + n, cols].bitcast(F32), ALU.subtract).then_inc(s["ring"], 1)
                        if u + 1 < UNITS:
                            reciprocals(u + 1)
                    out_low(H - 1)
                    for t in range(GT):
                        bank = 6 + ring[0] % 2
                        ring[0] += 1
                        dve.wait_ge(s["y_s"], g * GT + t + 1)
                        xg = x[:, ds(g * GT + t, 1), :]
                        dve.tensor_tensor(xg[:, 0], psum[:, bank, 0:D], xg[:, 0], ALU.add).then_inc(s["ring"], 1)

            dve.wait_ge(s["xb_s"], TILES)
            norm(2, x)
            steps = [0]

            def step(ins):
                ins.then_inc(s["rt"], 1)
                steps[0] += 1
                dve.wait_ge(s["rt"], steps[0])

            def over_experts(a):
                return a[:].unsqueeze(2).broadcast_to((P, TILES, E))

            dve.wait_ge(s["lgc"], GROUPS)
            dve.wait_ge(s["ones_s"], 4)
            step(dve.tensor_reduce(mx[:], logit[:], AX.X, ALU.max))
            step(dve.tensor_tensor(logit[:], logit[:], over_experts(mx), ALU.subtract))
            dve.wait_ge(s["rt_e"], 1)
            step(dve.tensor_reduce(rsum[:], logit[:], AX.X, ALU.add))
            step(dve.reciprocal(rsum[:], rsum[:]))
            step(dve.tensor_tensor(logit[:], logit[:], over_experts(rsum), ALU.mult))
            for k in range(2):
                step(dve.tensor_reduce(weight[k][:], logit[:], AX.X, ALU.max))
                step(dve.tensor_tensor(eq[:], logit[:], over_experts(weight[k]), ALU.is_equal))
                step(dve.tensor_tensor(eq[:], eq[:], favour[:], ALU.mult))
                step(dve.tensor_reduce(mx[:], eq[:], AX.X, ALU.max))
                step(dve.tensor_tensor(pick[k][:], eq[:], over_experts(mx), ALU.is_equal))
                if k == 0:
                    step(dve.scalar_tensor_tensor(out=logit[:], in0=pick[0][:], scalar=-2.0, in1=logit[:],
                                                  op0=ALU.mult, op1=ALU.add))
            step(dve.tensor_tensor(both[:], pick[0][:], pick[1][:], ALU.add))
            def running_totals(n, scan, totals):
                dve.wait_ge(s["rt_pe"], n)
                step(dve.tensor_copy(totals[:], psum[:, 6, 0:P].rearrange("p (t e) -> p t e", e=E)))
                step(dve.tensor_copy(scan[0][:], totals[:]))
                src, shift = 0, 1
                while shift < TILES:
                    a, o = scan[src], scan[1 - src]
                    dve.tensor_copy(o[:, 0:shift], a[:, 0:shift]).then_inc(s["rt"], 1)
                    steps[0] += 1
                    step(dve.tensor_tensor(o[:, shift:], a[:, shift:], a[:, 0:TILES - shift], ALU.add))
                    src, shift = 1 - src, shift * 2
                return scan[src], scan[1 - src]

            def tokens_before(sums, free, totals):
                step(dve.tensor_tensor(free[:], sums[:], totals[:], ALU.subtract))
                step(dve.tensor_tensor(free[:], psum[:, 5, 0:P].rearrange("p (t e) -> p t e", e=E), free[:], ALU.add))
                return free

            sums, free = running_totals(1, scan, totals)
            step(dve.tensor_scalar(blocks[:], sums[:, TILES - 1, :], float(P - 1), None, ALU.add))
            step(dve.tensor_copy(blocks_i[:], blocks[:]))
            step(dve.tensor_scalar(blocks_i[:], blocks_i[:], 7, None, ALU.logical_shift_right))
            step(dve.tensor_copy(blocks[:], blocks_i[:]))
            step(dve.tensor_scalar(blocks[:], blocks[:], 1.0, None, ALU.max))
            step(dve.memset(starts[0][:, 0:1], 0.0))
            step(dve.tensor_copy(starts[0][:, 1:], blocks[:]))
            at, shift = 0, 1
            while shift < E + 1:
                a, o = starts[at], starts[1 - at]
                dve.tensor_copy(o[:, 0:shift], a[:, 0:shift]).then_inc(s["rt"], 1)
                steps[0] += 1
                step(dve.tensor_tensor(o[:, shift:], a[:, shift:], a[:, 0:E + 1 - shift], ALU.add))
                at, shift = 1 - at, shift * 2
            first_block = starts[at]
            ranks = tokens_before(sums, free, totals)
            step(dve.scalar_tensor_tensor(out=totals[:], in0=first_block[:, 0:E].unsqueeze(1).broadcast_to((P, TILES, E)),
                                          scalar=float(P), in1=ranks[:], op0=ALU.mult, op1=ALU.add))
            for k in range(2):
                step(dve.tensor_tensor(eq[:], pick[k][:], totals[:], ALU.mult))
                step(dve.tensor_reduce(slot_f[:], eq[:], AX.X, ALU.add))
                step(dve.tensor_copy(slot[k][:], slot_f[:]))
            step(dve.memset(table[:], 0))
            dve.tensor_copy(table[:, 0, 1:E + 2], first_block[:]).then_inc(s["tbl"], 1)
            dve.tensor_copy(table[:, 1, 1:E + 1], blocks[:]).then_inc(s["tbl"], 1)
            step(dve.tensor_tensor(rsum[:], weight[0][:], weight[1][:], ALU.add))
            step(dve.tensor_scalar(rsum[:], rsum[:], 1e-20, None, ALU.add))
            step(dve.reciprocal(rsum[:], rsum[:]))
            for k in range(2):
                step(dve.tensor_tensor(weight[k][:], weight[k][:], rsum[:], ALU.mult))
            step(dve.memset(hid[:, F:], 0.0))
            assert steps[0] == RT_PADDED

            def x_low(n):
                dve.wait_ge(s["xh_s"], n + 1)
                dve.tensor_tensor(xbT_l[:], psum[:, 4, 0:D].rearrange("p (k c) -> p k c", k=KC), xbT_h[:].bitcast(F32),
                                  ALU.subtract).then_inc(s["xl_s"], 1)

            def block_low(n):
                for c, (lo, hi) in enumerate(((0, FA), (FA, F))):
                    dve.wait_ge(s["si_s"], n * 2 + c + 1)
                    dve.wait_ge(s["gu"], n * 4 + 2 * c + 2)
                    dve.tensor_tensor(hid[:, lo:hi], psum[:, 2 * c + 1, 0:hi - lo], silu[:, lo:hi], ALU.mult).then_inc(s["h_s"], 1)
                x_low(n + 1)
                for c in range(2):
                    dve.wait_ge(s["hh_s"], n * 2 + c + 1)
                    dve.tensor_tensor(hT_l[:, 3 * c:3 * c + 3, :], psum[:, 5 + c, 0:3 * P].rearrange("p (k c) -> p k c", k=3),
                                      hT_h[:, 3 * c:3 * c + 3, :].bitcast(F32), ALU.subtract).then_inc(s["hl_s"], 1)

            x_low(0)
            with dve.Fori(0, SHARED) as n:
                block_low(n)
                dve.wait_ge(s["yo"], n + 1)
                xg = x[:, ds(n, 1), :]
                dve.tensor_tensor(xg[:, 0], psum[:, 7, 0:D], xg[:, 0], ALU.add).then_inc(s["ye"], 1)
            with dve.Fori(0, E) as e:
                first = dve.value_load(table[0:1, 0, ds(e + 1, 1)], min_val=0, max_val=ROUTED - 2)
                count = dve.value_load(table[0:1, 1, ds(e + 1, 1)], min_val=1, max_val=TILES)
                with dve.Fori(0, count) as i:
                    n = dve.snap(first + i + SHARED)
                    block_low(n)
            for t in range(TILES):
                for k in range(2):
                    n = 2 * t + k
                    dve.wait_ge(s[f"got{t % 2}"], 32 * (t // 2 + 1))
                    last = dve.scalar_tensor_tensor(out=x[:, t, :], in0=y_got[:, n % 4, :], scalar=weight[k][:, t:t + 1],
                                                    in1=x[:, t, :], op0=ALU.mult, op1=ALU.add)
                    if k == 0:
                        step(last)
                last.then_inc(s["out0"], 1)

            dve.wait_ge(s["out0"], TILES)
            dve.memset(kb_h[:].bitcast(F32), 0.0)
            dve.memset(kb_l[:].bitcast(F32), 0.0).then_inc(s["zk"], 1)
            dve.memset(vb_h[:].bitcast(F32), 0.0)
            dve.memset(vb_l[:].bitcast(F32), 0.0).then_inc(s["zk"], 1)
            norm(3, x)
            dve.wait_ge(s["c1_act"], 1)
            dve.tensor_tensor(cT_l[:], psum[0:PX, 0, 0:KX * P].rearrange("p (k c) -> p k c", k=KX), cT_h[:].bitcast(F32),
                              ALU.subtract).then_inc(s["c1_dve"], 1)
            dve.wait_ge(s["c1_act"], 5 + 4 * KC)
            dve.wait_ge(s["zk"], 2)
            for k in range(KC):
                for hh in range(2):
                    half = slice(hh * C, (hh + 1) * C)
                    head = 2 * k + hh
                    cols = slice(head * C, (head + 1) * C)
                    dve.tensor_tensor(kb_l[half, :, k, cols], psum[half, 1, k * P:(k + 1) * P].rearrange("p (b c) -> p b c", b=B),
                                      kb_h[half, :, k, cols].bitcast(F32), ALU.subtract).then_inc(s["c1_dve"], 1)
                    cols = slice(hh * HD, (hh + 1) * HD)
                    dve.tensor_tensor(vb_l[half, :, k, cols],
                                      psum[half, 2, :].rearrange("p (b d) -> p b d", b=B)[:, :, head * HD:(head + 1) * HD],
                                      vb_h[half, :, k, cols].bitcast(F32), ALU.subtract).then_inc(s["c1_dve"], 1)
            with dve.Fori(0, B) as b:
                with dve.Fori(0, GPB) as gg:
                    g = b * GPB + gg
                    for t in range(GT):
                        dve.wait_ge(s["x1h"], g * GT + t + 1)
                        cols = slice(t * P, (t + 1) * P)
                        dve.tensor_tensor(x1_l[:, :, cols], psum[:, t, 0:D].rearrange("p (k c) -> p k c", k=KC),
                                          x1_h[:, :, cols].bitcast(F32), ALU.subtract).then_inc(s["x1l"], 1)
                    for k in range(KC):
                        dve.wait_ge(s["q1h"], g * KC + k + 1)
                        dve.scalar_tensor_tensor(out=q1_l[:, k, :], in0=psum[:, 4 + k, :], scalar=HD ** -0.5,
                                                 in1=q1_h[:, k, :].bitcast(F32), op0=ALU.mult, op1=ALU.subtract).then_inc(s["q1l"], 1)

                    def heads(a):
                        return a.rearrange("p (h c) -> p h c", h=H)

                    for t in range(GT):
                        dve.wait_ge(s["sc1"], g * GT + t + 1)
                        dve.tensor_reduce(m1[:, t, :], heads(psum[:, t, 0:H * C]), AX.X, ALU.max).then_inc(s["mx1"], 1)
                        dve.wait_ge(s["mx1"], g * GT + t + 1)
                        dve.tensor_tensor(heads(p1[:, t, :]), heads(psum[:, t, 0:H * C]),
                                          m1[:, t, :].unsqueeze(2).broadcast_to((P, H, C)), ALU.subtract).then_inc(s["sb1"], 1)
                    for t in range(GT):
                        dve.wait_ge(s["e1"], g * GT + t + 1)
                        dve.tensor_reduce(d1[:, t, :], heads(p1[:, t, :]), AX.X, ALU.add).then_inc(s["sm1"], 1)
                    dve.wait_ge(s["sm1"], g * GT + GT)
                    dve.reciprocal(d1[:], d1[:]).then_inc(s["rc1"], 1)
                    dve.wait_ge(s["rc1"], g + 1)
                    for t in range(GT):
                        dve.tensor_tensor(heads(p1[:, t, :]), heads(p1[:, t, :]),
                                          d1[:, t, :].unsqueeze(2).broadcast_to((P, H, C)), ALU.mult).then_inc(s["pn1"], 1)
                    for t in range(GT):
                        dve.wait_ge(s["p1h"], g * GT + t + 1)
                        cols = slice(t * P, (t + 1) * P)
                        dve.tensor_tensor(p1T_l[:, :, cols], psum[:, 4 + t, 0:D].rearrange("p (k c) -> p k c", k=KC),
                                          p1T_h[:, :, cols].bitcast(F32), ALU.subtract).then_inc(s["p1l"], 1)
                    for k in range(KC):
                        dve.wait_ge(s["o1h"], g * KC + k + 1)
                        dve.tensor_tensor(o1_l[:, k, :], psum[:, k, :], o1_h[:, k, :].bitcast(F32),
                                          ALU.subtract).then_inc(s["o1l"], 1)
                    for t in range(GT):
                        dve.wait_ge(s["y1"], g * GT + t + 1)
                        xg = x[:, ds(g * GT + t, 1), :]
                        dve.tensor_tensor(xg[:, 0], psum[:, 4 + t, 0:D], xg[:, 0], ALU.add).then_inc(s["x1a"], 1)

            dve.wait_ge(s["x1b"], TILES)
            norm(4, x)
            dve.wait_ge(s["r1_e"], 1)
            dve.wait_ge(s["k1c"], 6)
            r1 = [0]

            def step1(ins):
                ins.then_inc(s["r1"], 1)
                r1[0] += 1
                dve.wait_ge(s["r1"], r1[0])

            step1(dve.tensor_scalar(gates[:], gates[:], 1.0, None, ALU.add))
            step1(dve.reciprocal(gates[:], gates[:]))
            assert r1[0] == R1_GATES
            step1(dve.memset(thr[:], 0))
            step1(dve.memset(bit[:], 1 << (BITS - 1)))
            with dve.Fori(0, BITS) as i:
                dve.wait_ge(s["srch"], i)
                dve.tensor_tensor(cand[:], thr[:], bit[:], ALU.bitwise_or).then_inc(s["cnd"], 1)
                dve.wait_ge(s["cnd"], i + 1)
                dve.tensor_tensor(over[:], gates[:], cand[:].bitcast(F32).unsqueeze(1).broadcast_to((P, TILES, E)),
                                  ALU.is_ge).then_inc(s["cmpd"], 1)
                dve.tensor_scalar(bit[:], bit[:], 1, None, ALU.logical_shift_right).then_inc(s["shf"], 1)
                dve.wait_ge(s["cnt"], i + 1)
                dve.tensor_reduce(tally[:], psum[:, 7, 0:P].rearrange("p (t e) -> p e t", e=E), AX.X, ALU.add).then_inc(s["cns"], 1)
                dve.wait_ge(s["cns"], i + 1)
                dve.tensor_scalar(enough[:], tally[:], float(CHOSEN), None, ALU.is_ge).then_inc(s["eno"], 1)
                dve.wait_ge(s["eno"], i + 1)
                dve.wait_ge(s["shf"], i + 1)
                dve.sem_inc(s["met"], 1)
                dve.copy_predicated(thr[:], enough[:], cand[:]).then_inc(s["srch"], 1)
            dve.wait_ge(s["srch"], BITS)
            least = thr[:].bitcast(F32).unsqueeze(1).broadcast_to((P, TILES, E))
            step1(dve.tensor_tensor(above[:], gates[:], least, ALU.is_gt))
            step1(dve.tensor_tensor(ties[:], gates[:], least, ALU.is_equal))
            dve.wait_ge(s["cnt"], BITS + 1)
            step1(dve.tensor_reduce(tally[:], psum[:, 7, 0:P].rearrange("p (t e) -> p e t", e=E), AX.X, ALU.add))
            step1(dve.tensor_scalar(tally[:], tally[:], -1.0, float(CHOSEN), ALU.mult, ALU.add))

            def step(ins):
                step1(ins)

            def running1(n):
                dve.wait_ge(s["rt_pe"], n)
                step1(dve.tensor_copy(totals1[:], psum[:, 6, 0:P].rearrange("p (t e) -> p t e", e=E)))
                step1(dve.tensor_copy(scan1[0][:], totals1[:]))
                src, shift = 0, 1
                while shift < TILES:
                    a, o = scan1[src], scan1[1 - src]
                    dve.tensor_copy(o[:, 0:shift], a[:, 0:shift]).then_inc(s["r1"], 1)
                    r1[0] += 1
                    step1(dve.tensor_tensor(o[:, shift:], a[:, shift:], a[:, 0:TILES - shift], ALU.add))
                    src, shift = 1 - src, shift * 2
                free = scan1[1 - src]
                step1(dve.tensor_tensor(free[:], scan1[src][:], totals1[:], ALU.subtract))
                step1(dve.tensor_tensor(free[:], psum[:, 5, 0:P].rearrange("p (t e) -> p t e", e=E), free[:], ALU.add))
                return free

            earlier = running1(2)
            step1(dve.tensor_tensor(chosen[:], earlier[:], tally[:].unsqueeze(1).broadcast_to((P, TILES, E)), ALU.is_lt))
            step1(dve.tensor_tensor(chosen[:], chosen[:], ties[:], ALU.mult))
            step1(dve.tensor_tensor(chosen[:], chosen[:], above[:], ALU.add))
            assert r1[0] == R1_CHOSEN
            earlier = running1(3)
            step1(dve.tensor_copy(place_i[:], earlier[:]))
            step1(dve.tensor_scalar(row_i[:], place_i[:], P - 1, None, ALU.bitwise_and))
            step1(dve.tensor_scalar(place_i[:], place_i[:], 7, None, ALU.logical_shift_right))
            step1(dve.tensor_copy(row_f[:], row_i[:]))
            step1(dve.tensor_copy(tile_f[:], place_i[:]))
            step1(dve.scalar_tensor_tensor(out=row_f[:], in0=row_f[:], scalar=1.0, in1=chosen[:], op0=ALU.add, op1=ALU.mult))
            step1(dve.tensor_scalar(row_f[:], row_f[:], -1.0, None, ALU.add))
            te = (P, TILES * E, CT)
            put_2d = put_f[:].rearrange("p t e c -> p (t e) c")
            step1(dve.tensor_tensor(put_2d, tile_f[:].rearrange("p t e -> p (t e)").unsqueeze(2).broadcast_to(te),
                                    columns[:, 0:CT].unsqueeze(1).broadcast_to(te), ALU.is_equal))
            step1(dve.tensor_scalar(put[:, :, :, 1, :].rearrange("p t e c -> p (t e) c"), put_2d, lane[:], None, ALU.mult))
            step1(dve.tensor_tensor(put[:, :, :, 0, :], put_f[:].rearrange("p t e c -> p t (e c)").rearrange("p t (e c) -> p t e c", e=E),
                                    tile_no[:].unsqueeze(2).unsqueeze(3).broadcast_to((P, TILES, E, CT)), ALU.mult))
            for t in range(TILES):
                if t >= 2:
                    dve.wait_ge(s["hot_pe"], t - 1)
                dve.tensor_tensor(hot[:, t % 2], columns[:].unsqueeze(1).broadcast_to((P, E, P)),
                                  row_f[:, t, :].unsqueeze(2).broadcast_to((P, E, P)), ALU.is_equal).then_inc(s["hots"], 1)
            dve.wait_ge(s["hot_pe"], TILES)
            dve.tensor_copy(found[:], psum[:, :, 0:2 * CT]).then_inc(s["found_s"], 1)
            dve.wait_ge(s["found_s"], 1)
            dve.scalar_tensor_tensor(out=tokens[:], in0=found[:, :, 0:CT], scalar=float(P), in1=found[:, :, CT:],
                                     op0=ALU.mult, op1=ALU.add).then_inc(s["found_s"], 1)

            def rows_low(n):
                for t in range(CT):
                    cols = slice(t * P, (t + 1) * P)
                    dve.wait_ge(s["xe_hs"], n * CT + t + 1)
                    dve.tensor_tensor(xe_l[:, :, cols], psum[:, 6 + t % 2, 0:D].rearrange("p (k c) -> p k c", k=KC),
                                      xe_h[:, :, cols].bitcast(F32), ALU.subtract).then_inc(s["xe_ls"], 1)

            def expert1(e, side, last):
                dve.tensor_copy(gval[:, side, :], gathered[side][:, :, ds(D + e, 1)].rearrange("p t o -> p (t o)")).then_inc(s["gval_s"], 1)
                for f in range(FT1):
                    dve.wait_ge(s["gl_s"], e * FT1 + f + 1)
                    dve.tensor_copy(g_h[:, f, :], gl[:, f % 2, :]).then_inc(s["gh_s"], 1)
                    dve.wait_ge(s["gh_s"], e * FT1 + f + 1)
                    dve.tensor_tensor(g_l[:, f, :], gl[:, f % 2, :], g_h[:, f, :].bitcast(F32), ALU.subtract).then_inc(s["gls"], 1)
                if not last:
                    rows_low(e + 1)
                dve.wait_ge(s["sadd"], e * (CT * 16))
                dve.wait_ge(s["gval_s"], e + 1)
                for t in range(CT):
                    dve.wait_ge(s["yb1"], e * CT + t + 1)
                    dve.tensor_tensor(ye1[:, t, :], psum[:, 2 + t, 0:D], b2[:, ds(e, 1), :].rearrange("p o d -> p (o d)"),
                                      ALU.add).then_inc(s["y1e"], 1)
                for t in range(CT):
                    dve.wait_ge(s["y1e"], e * CT + t + 1)
                    dve.tensor_scalar(ye1[:, t, :], ye1[:, t, :], gval[:, side, t:t + 1], None, ALU.mult).then_inc(s["ys1"], 1)

            rows_low(0)
            dve.wait_ge(s["b_in"], 32)
            with dve.Fori(0, E // 2 - 1) as p:
                for side in range(2):
                    expert1(2 * p + side, side, False)
            expert1(E - 2, 0, False)
            expert1(E - 1, 1, True)

        @block.tensor
        def _(pe):
            def products(o, pairs):
                for n, (l, r) in enumerate(pairs):
                    last = pe.matmul(o, l, r, start=n == 0, stop=n == len(pairs) - 1)
                return last

            pe.wait_ge(s["ident1"], 1)
            pe.wait_ge(s["c_dve"], 3)
            for k in range(KX):
                last = pe.transpose(psum[0:PX, 0, k * P:(k + 1) * P], xcn[:, k * PX:(k + 1) * PX], ident[:])
            last.then_inc(s["c_pe"], 1)
            pe.wait_ge(s["mask_s"], 4)
            pe.wait_ge(s["c_act"], 1)
            pe.wait_ge(s["wsp_l"], 3)
            products(psum[:, 1, :], [(l[:, k, :], r[:, k, :]) for k in range(KX)
                                     for l, r in ((ch, wkvx_h), (ch, wkvx_l), (cl, wkvx_h))]).then_inc(s["c_pe"], 1)
            pe.wait_ge(s["identr"], 1)
            pe.wait_ge(s["c_dve"], 10)
            for r in range(2):
                for h in range(H):
                    last = pe.transpose(psum[:, 2 + r, h * P:(h + 1) * P].bitcast(F32R), cparts[:, r * H + h, :], ident_r[:])
                last.then_inc(s["c_pe"], 1)

            with pe.Fori(0, B) as b:
                with pe.Fori(0, GPB) as gg:
                    g = b * GPB + gg
                    pe.wait_ge(s["ev_a"], g * 6)
                    pe.wait_ge(s["ev_d"], g * 6)
                    pe.wait_ge(s["ring"], b * (GPB * RING))
                    for t in range(GT):
                        pe.wait_ge(s["xt_s"], g * GT + t + 1)
                        for k in range(KC):
                            last = pe.transpose(psum[:, 4 + t, k * P:(k + 1) * P], xt[:, t, k * P:(k + 1) * P], ident[:])
                        last.then_inc(s["tp"], 1)
                    for t in range(GT):
                        pe.wait_ge(s["lnl_s"], g * GT + t + 1)
                        if t >= 2:
                            pe.wait_ge(s["raw_s"], g * GT + t - 1)
                        z = 2 * (t % 2)
                        for bank, lo, hi in ((z, 0, 2 * D), (z + 1, 2 * D, 3 * D)):
                            last = products(psum[:, bank, 0:hi - lo],
                                            [(l[:, t, k, :], r[:, k, lo:hi]) for k in range(KC)
                                             for l, r in ((lnh, wqkv_h), (lnh, wqkv_l), (lnl, wqkv_h))])
                        last.then_inc(s["qkv_s"], 1)
                    for t in range(GT):
                        pe.wait_ge(s["hi_s"], (g * GT + t + 1) * 2)
                        pe.wait_ge(s["lo_s"], (g * GT + t + 1) * 2)
                        for c in range(3):
                            n = 3 * t + c
                            if n >= 2:
                                pe.wait_ge(s["ev_d"] if n % 2 else s["ev_a"], g * 6 + n // 2)
                            for h in range(H):
                                last = pe.transpose(psum[:, 6 + n % 2, h * P:(h + 1) * P].bitcast(F32R),
                                                    parts[:, t % 2, c * H + h, :], ident_r[:])
                            last.then_inc(s["t12"], 1)
                with pe.Fori(0, GPB) as gg:
                    g = b * GPB + gg
                    ring = [0]
                    pe.wait_ge(s["qs_s"], g + 1)
                    pe.wait_ge(s["ev_a"], (b + 1) * (GPB * 6))
                    pe.wait_ge(s["ev_d"], (b + 1) * (GPB * 6))
                    pe.wait_ge(s["ring"], g * RING)

                    def scores(u):
                        if u >= 2:
                            pe.wait_ge(s["exp_s"], g * UNITS + u - 1)
                        h, t = divmod(u, GT)
                        q = qs[:, h, t * P:(t + 1) * P]
                        z = 3 * (u % 2)
                        for c, (lo, hi) in enumerate(((0, 512), (512, 1024), (1024, KEYS))):
                            pairs = [(q, kT[:, h, 0, lo:hi]), (q, kT[:, h, 1, lo:hi])]
                            if hi == KEYS:
                                pairs.insert(0, (first_row[:], mask_rows[:, ds(b, 1), :].rearrange("p o k -> p (o k)")))
                            last = products(psum[:, z + c, 0:hi - lo], pairs)
                        last.then_inc(s["sc_s"], 1)

                    def next_bank():
                        r = ring[0]
                        ring[0] += 1
                        if r >= 2:
                            pe.wait_ge(s["ring"], g * RING + r - 1)
                        return 6 + r % 2

                    def transposes(u):
                        pe.wait_ge(s["pn_s"], g * UNITS + u + 1)
                        for c in range(3):
                            bank = next_bank()
                            n = min(4, KT - 4 * c)
                            for k in range(n):
                                last = pe.transpose(psum[:, bank, k * P:(k + 1) * P],
                                                    prob[:, u % 3, (4 * c + k) * P:(4 * c + k + 1) * P], ident[:])
                            last.then_inc(s["pt_s"], 1)

                    def values(h):
                        bank = next_bank()
                        pe.wait_ge(s["ring"], g * RING + ring[0] - 1)
                        if h == 0:
                            pe.wait_ge(s["vl_s"], (b + 1) * (GPB * GT))
                        products(psum[:, bank, :], [(v[:, k, h, :], p[:, k, :]) for k in range(KT)
                                                    for p in (pT_h, pT_l)]).then_inc(s["o_s"], 1)

                    scores(0)
                    for u in range(UNITS):
                        if u + 1 < UNITS:
                            scores(u + 1)
                        if u % GT == 0 and u:
                            values(u // GT - 1)
                        transposes(u)
                    values(H - 1)
                    for t in range(GT):
                        bank = next_bank()
                        if t == 0:
                            pe.wait_ge(s["ring"], g * RING + ring[0] - 1)
                        cols = slice(t * P, (t + 1) * P)
                        products(psum[:, bank, 0:D], [(o[:, h, cols], w[:, h, :]) for h in range(H)
                                                      for o, w in ((oT_h, wo_h), (oT_h, wo_l), (oT_l, wo_h))]
                                 ).then_inc(s["y_s"], 1)

            def gate_logits(layer, xs0, xnT, gate_w):
                pe.wait_ge(s["gw_in"], 16 * (layer + 1))
                with pe.Fori(0, GROUPS) as g0:
                    g = g0 + layer * GROUPS
                    for t in range(GT):
                        pe.wait_ge(s["xs0_s"], g * GT + t + 1)
                        for k in range(KC):
                            last = pe.transpose(psum[:, t, k * P:(k + 1) * P], xs0[:, t, k * P:(k + 1) * P], ident[:])
                        last.then_inc(s["tp0"], 1)
                    pe.wait_ge(s["lgc"], g)
                    for t in range(GT):
                        pe.wait_ge(s["xnT_s"], g * GT + t + 1)
                        products(psum[:, 4, t * E:(t + 1) * E], [(xnT[:, t, k, :], gate_w[:, k, :]) for k in range(KC)]
                                 ).then_inc(s["lg_s"], 1)

            def count_before(flags, before, ones):
                f = flags[:].rearrange("p t e -> p (t e)")
                pe.matmul(psum[:, 5, 0:P], before[:], f, start=True, stop=True)
                pe.matmul(psum[:, 6, 0:P], ones[:], f, start=True, stop=True).then_inc(s["rt_pe"], 1)

            gate_logits(0, xs0, xnT, gate_w)
            pe.wait_ge(s["lgc"], GROUPS)
            pe.wait_ge(s["rt"], RT_PICKED)
            count_before(both, before, ones)

            def x_transposed(n):
                pe.wait_ge(s["xbi"], (n + 1) * 16)
                for k in range(KC):
                    last = pe.transpose(psum[:, 4, k * P:(k + 1) * P], xb[:, k * P:(k + 1) * P], ident[:])
                last.then_inc(s["tx"], 1)

            def block(n, side):
                wh, wl = w_h[side], w_l[side]
                pe.wait_ge(s["xl_s"], n + 1)
                for c, (lo, hi) in enumerate(((0, FA), (FA, F))):
                    pe.wait_ge(s["h_s"], n * 2)
                    for up in range(2):
                        cols = [slice((up * KC + k) * F + lo, (up * KC + k) * F + hi) for k in range(KC)]
                        products(psum[:, 2 * c + up, 0:hi - lo],
                                 [(a[:, k, :], w[:, cols[k]]) for k in range(KC)
                                  for a, w in ((xbT_h, wh), (xbT_h, wl), (xbT_l, wh))]).then_inc(s["gu"], 1)
                x_transposed(n + 1)
                for c in range(2):
                    pe.wait_ge(s["h_s"], n * 2 + c + 1)
                    for k in range(3):
                        last = pe.transpose(psum[:, 5 + c, k * P:(k + 1) * P], hid[:, (3 * c + k) * P:(3 * c + k + 1) * P], ident[:])
                    last.then_inc(s["th"], 1)
                pe.wait_ge(s["ye"], n)
                down = 2 * KC * F
                for c in range(2):
                    pe.wait_ge(s["hl_s"], n * 2 + c + 1)
                    for k in range(3 * c, 3 * c + 3):
                        for m, (a, w) in enumerate(((hT_h, wh), (hT_h, wl), (hT_l, wh))):
                            last = pe.matmul(psum[:, 7, 0:D], a[:, k, :], w[:, down + k * D:down + (k + 1) * D],
                                             start=k == 0 and m == 0, stop=k == FT - 1 and m == 2)
                last.then_inc(s["yo"], 1)

            pe.wait_ge(s["rt"], RT_PADDED)
            x_transposed(0)
            pe.wait_ge(s["ws_l"], 1)
            with pe.Fori(0, SHARED) as n:
                block(n, 0)
            with pe.Fori(0, E // 2) as p:
                for side in (1, 0):
                    w = 2 * p + (1 if side else 2)
                    first = pe.value_load(table[0:1, 0, ds(w, 1)], min_val=0, max_val=ROUTED - 2)
                    count = pe.value_load(table[0:1, 1, ds(w, 1)], min_val=1, max_val=TILES)
                    pe.wait_ge(s["ws_l"], w + 1)
                    pe.sem_inc(s["met"], 1)
                    with pe.Fori(0, count) as i:
                        n = pe.snap(first + i + SHARED)
                        block(n, side)

            pe.wait_ge(s["a1_in"], 64)
            for k in range(KX):
                last = pe.transpose(psum[0:PX, 0, k * P:(k + 1) * P], xc1[:, k * PX:(k + 1) * PX], ident[:])
            last.then_inc(s["c1_pe"], 1)
            pe.wait_ge(s["a1_l"], 2)
            pe.wait_ge(s["c1_dve"], 1)
            pe.wait_ge(s["c1_act"], 5)
            for k in range(KC):
                cols = slice(k * P, (k + 1) * P)
                last = products(psum[:, 1, cols], [(w[:, 0, c, cols], a[:, c, :]) for c in range(KX)
                                                   for w, a in ((c_h, cT_h), (c_h, cT_l), (c_l, cT_h))])
            last.then_inc(s["c1_pe"], 1)
            for b in range(B):
                last = products(psum[:, 2, b * D:(b + 1) * D],
                                [(a[:, c, b].rearrange("p r c -> p (r c)"), w[:, 1, c, :]) for c in range(KX)
                                 for w, a in ((c_h, cd_h), (c_h, cd_l), (c_l, cd_h))])
            last.then_inc(s["c1_pe"], 1)
            pe.wait_ge(s["c1_dve"], 1 + 4 * KC)
            pe.wait_ge(s["c1_act"], 5 + 4 * KC)
            with pe.Fori(0, B) as b:
                with pe.Fori(0, GPB) as gg:
                    g = b * GPB + gg
                    for t in range(GT):
                        pe.wait_ge(s["xs1_s"], g * GT + t + 1)
                        for k in range(KC):
                            last = pe.transpose(psum[:, t, k * P:(k + 1) * P], xs1[:, t, k * P:(k + 1) * P], ident[:])
                        last.then_inc(s["tp1"], 1)
                    pe.wait_ge(s["x1l"], (g + 1) * GT)
                    pe.wait_ge(s["x1a"], g * GT)
                    for m in range(KC):
                        cols = slice(m * P, (m + 1) * P)
                        products(psum[:, 4 + m, :], [(w[:, 0, k, cols], a[:, k, :]) for k in range(KC)
                                                     for w, a in ((a_h, x1_h), (a_h, x1_l), (a_l, x1_h))]).then_inc(s["q1"], 1)
                    pe.wait_ge(s["q1l"], (g + 1) * KC)
                    for t in range(GT):
                        cols = slice(t * P, (t + 1) * P)
                        keys = [(a[:, ds(b, 1), k, :].rearrange("p o c -> p (o c)")) for k in range(KC) for a in (kb_h, kb_l)]
                        products(psum[:, t, 0:H * C], [pair for k in range(KC) for pair in
                                                       ((q1_h[:, k, cols], keys[2 * k]), (q1_h[:, k, cols], keys[2 * k + 1]),
                                                        (q1_l[:, k, cols], keys[2 * k]))]).then_inc(s["sc1"], 1)
                    for t in range(GT):
                        pe.wait_ge(s["pn1"], g * GT + t + 1)
                        for k in range(KC):
                            last = pe.transpose(psum[:, 4 + t, k * P:(k + 1) * P], p1[:, t, k * P:(k + 1) * P], ident[:])
                        last.then_inc(s["pt1"], 1)
                    pe.wait_ge(s["vsc"], (g + 1) * 2)
                    pe.wait_ge(s["p1l"], (g + 1) * GT)
                    for k in range(KC):
                        products(psum[:, k, :], [(a[:, k, :], p[:, k, :]) for a, p in
                                                 ((vs_h, p1T_h), (vs_h, p1T_l), (vs_l, p1T_h))]).then_inc(s["o1"], 1)
                    pe.wait_ge(s["o1l"], (g + 1) * KC)
                    for t in range(GT):
                        cols = slice(t * P, (t + 1) * P)
                        products(psum[:, 4 + t, 0:D], [(o[:, k, cols], w[:, 1, k, :]) for k in range(KC)
                                                       for o, w in ((o1_h, a_h), (o1_h, a_l), (o1_l, a_h))]).then_inc(s["y1"], 1)

            pe.wait_ge(s["x1b"], TILES)
            gate_logits(1, xs2, xnT1, gate1_w)
            with pe.Fori(0, BITS) as i:
                pe.wait_ge(s["cmpd"], i + 1)
                pe.matmul(psum[:, 7, 0:P], ones1[:], over[:].rearrange("p t e -> p (t e)"), start=True, stop=True).then_inc(s["cnt"], 1)
            pe.wait_ge(s["r1"], R1_FLAGS)
            pe.matmul(psum[:, 7, 0:P], ones1[:], above[:].rearrange("p t e -> p (t e)"), start=True, stop=True).then_inc(s["cnt"], 1)
            count_before(ties, before1, ones1)
            pe.wait_ge(s["r1"], R1_CHOSEN)
            count_before(chosen, before1, ones1)
            pe.wait_ge(s["hots"], 1)
            for t in range(TILES):
                pe.wait_ge(s["hots"], t + 1)
                for e in range(E):
                    last = pe.matmul(psum[:, e, 0:2 * CT], hot[:, t % 2, e, :], put[:, t, e].rearrange("p v c -> p (v c)"),
                                     start=t == 0, stop=t == TILES - 1)
                last.then_inc(s["hot_pe"], 1)

            def rows_transposed(n, side):
                pe.wait_ge(s[f"ga{side}"], (n // 2 + 1) * (CT * 16))
                for t in range(CT):
                    if t >= 2:
                        pe.wait_ge(s["xe_ls"], n * CT + t - 1)
                    for k in range(KC):
                        last = pe.transpose(psum[:, 6 + t % 2, k * P:(k + 1) * P], gathered[side][:, t, k * P:(k + 1) * P], ident[:])
                    last.then_inc(s["xe_t"], 1)

            def expert1(e, side, last_one):
                wh, wl = v_h[side], v_l[side]
                pe.wait_ge(s["vs_ls"], e + 1)
                pe.wait_ge(s["xe_ls"], (e + 1) * CT)
                for f in range(FT1):
                    if f >= 2:
                        pe.wait_ge(s["gl_s"], e * FT1 + f - 1)
                    cols = [slice(k * F1 + f * P, k * F1 + (f + 1) * P) for k in range(KC)]
                    products(psum[:, f % 2, :], [(w[:, cols[k]], a[:, k, :]) for k in range(KC)
                                                 for w, a in ((wh, xe_h), (wh, xe_l), (wl, xe_h))]).then_inc(s["h1"], 1)
                if not last_one:
                    rows_transposed(e + 1, 1 - side)
                pe.wait_ge(s["y1e"], e * CT)
                for f in range(FT1):
                    pe.wait_ge(s["gls"], e * FT1 + f + 1)
                    for t in range(CT):
                        cols = slice(t * P, (t + 1) * P)
                        w2 = slice(W1 + f * D, W1 + (f + 1) * D)
                        for m, (a, w) in enumerate(((g_h, wh), (g_h, wl), (g_l, wh))):
                            last = pe.matmul(psum[:, 2 + t, 0:D], a[:, f, cols], w[:, w2],
                                             start=f == 0 and m == 0, stop=f == FT1 - 1 and m == 2)
                        if f == FT1 - 1:
                            last.then_inc(s["yb1"], 1)

            pe.wait_ge(s["found_s"], 2)
            rows_transposed(0, 0)
            with pe.Fori(0, E // 2 - 1) as p:
                for side in range(2):
                    expert1(2 * p + side, side, False)
            expert1(E - 2, 0, False)
            expert1(E - 1, 1, True)


def kernel(**inputs):
    import concourse.bacc as bacc
    from concourse.bass_utils import run_bass_kernel_spmd

    i = {k: np.asarray(v) for k, v in inputs.items()}

    def chunked(w, n):
        return w.reshape(n, -1, w.shape[-1]).transpose(1, 0, 2)

    def columns(vec, n):
        return vec.reshape(n, -1).T

    def rows_first(w):
        e, r, m = w.shape
        return w.reshape(e, r // P, P, m).transpose(0, 2, 1, 3).reshape(e, P, -1)

    def expert_weights(i):
        gate, up, down = (np.concatenate([i[f"L0_ffn_shared_{n}"][None], i[f"L0_ffn_expert_{n}"]]).transpose(0, 2, 1)
                          for n in ("gate", "up", "down"))
        down = np.pad(down, ((0, 0), (0, FT * P - F), (0, 0)))
        return np.concatenate([rows_first(gate), rows_first(up), rows_first(down)], 2)

    wo = i["L0_xattn_Wo"].T.reshape(H, HD, D)
    arrays = {
        "x": i["x"].reshape(T, D),
        "ctx": i["ctx_768"].reshape(B * C, DC),
        "mask": i["mask_BxS2_bk0"].reshape(1, B * C),
        "lnx_g": columns(i["L0_xattn_ln_x_g"], KX), "lnx_b": columns(i["L0_xattn_ln_x_b"], KX),
        "ln_g": columns(i["L0_xattn_ln_l_g"], KC), "ln_b": columns(i["L0_xattn_ln_l_b"], KC),
        "qk_gain": np.concatenate([i["L0_xattn_qn_g"]] * H + [i["L0_xattn_kn_g"]] * H),
        "bo0": i["L0_xattn_bo"],
        "wkvx": chunked(i["L0_xattn_Wkv"].T, KX),
        "wqkv": chunked(np.concatenate([i["L0_xattn_Wq"].T, i["L0_xattn_Wlkv"].T], 1), KC),
        "gate1": chunked(i["L1_ffn_Wg"], KC),
        "wkv1": np.stack([chunked(i["L1_xattn_Wk"].T, KX), chunked(i["L1_xattn_Wv"].T, KX)], 1),
        "wqo1": np.stack([chunked(i["L1_xattn_Wq"].T, KC), chunked(i["L1_xattn_Wo"].T, KC)], 1),
        "bo1": i["L1_xattn_bo"],
        "b1": i["L1_ffn_b1"].reshape(E, FT1, P).transpose(2, 0, 1).reshape(P, E * FT1),
        "b2": i["L1_ffn_b2"].reshape(E * D),
        "experts1": np.concatenate([rows_first(i["L1_ffn_W1"]), rows_first(i["L1_ffn_W2"])], 2),
        "gate0": chunked(i["L0_ffn_gate_w"].T, KC),
        "experts0": expert_weights(i),
        "wo0": np.concatenate([wo, wo], 1).transpose(1, 0, 2),
    }
    arrays = {k: np.ascontiguousarray(a) for k, a in arrays.items()}
    nc = bacc.Bacc("TRN2", target_bir_lowering=False, num_devices=1)
    ap = {k: nc.dram_tensor("in_" + k, a.shape, mybir.dt.from_np(a.dtype), kind="ExternalInput").ap() for k, a in arrays.items()}
    out = nc.dram_tensor("y", (T, D), F32, kind="ExternalOutput").ap()
    build(nc, ap, out)
    r = run_bass_kernel_spmd(nc, [{"in_" + k: a for k, a in arrays.items()}], core_ids=[0])
    return r.results[0]["y"].reshape(B, S, D)
```

```python
from contextlib import ExitStack

import numpy as np

import concourse.bass as bass
from concourse import mybir

ALU = mybir.AluOpType
ACT = mybir.ActivationFunctionType
AX = mybir.AxisListType
F32 = mybir.dt.float32
F32R = mybir.dt.float32r
BF16 = mybir.dt.bfloat16
I32 = mybir.dt.int32
U32 = mybir.dt.uint32
U8 = mybir.dt.uint8
ds = bass.ds

P = 128
B = 2
S = 1024
T = B * S
TILES = T // P
GT = 4
GROUPS = TILES // GT
GPB = GROUPS // B
D = 256
KC = D // P
C = 64
DC = 192
KX = 2
PX = DC // KX
H = 4
HD = 64
KT = S // P + 1
KEYS = KT * P
CTX0 = S
PIECE = KEYS // 3
BIG = 1.0e30
LN_EPS = 1e-5
RMS_EPS = 1e-8
RT_SHIFTED, RT_PICKED, RT_PADDED = 2, 17, 58
R1_GATES, R1_FLAGS, R1_CHOSEN = 2, 8, 25
UNITS = H * GT
E = 8
F = 704
FA = 384
FB = F - FA
FT = 6
FW = 2 * KC * F + FT * D
SHARED = TILES
ROUTED = 2 * T // P + E
CHOSEN = T * 2 // E
CT = CHOSEN // P
F1 = 1024
FT1 = F1 // P
W1 = KC * F1
FW1 = W1 + FT1 * D
CUTS = 4
CUT = FW1 // CUTS
BITS = 30
ROUNDS = BITS // 2
XG = D + E
COUNT_FROM_ONE = "tx yst ys1 srch ev_d ev_a ring0 ring1 lgc h_s ye x1a y1e yb1 shf".split()


def ring_uses():
    uses, before, bank = {}, [0, 0], 0

    def use(key, b):
        uses[key] = b, before[b]
        before[b] += 1
        return 1 - b

    for u in range(UNITS):
        held = None
        if u % GT == 0 and u:
            held, bank = bank, use(("result", u // GT - 1), bank)
        for c in range(3):
            other = use(("chunk", u, c), bank)
            bank = other if held is None else bank
        if u % GT == GT - 1:
            bank = use(("reciprocals", u // GT), bank)
    bank = use(("result", H - 1), bank)
    for t in range(GT):
        bank = use(("output", t), bank)
    return uses, before


USES, RING = ring_uses()


def build(nc, ap, out):
    ctx = ExitStack()
    with ctx:
        def sb(name, shape, dt=F32, scope=ctx):
            return scope.enter_context(nc.sbuf_tensor(name, shape, dt))

        def sem(name):
            return ctx.enter_context(nc.semaphore(name))

        psum = ctx.enter_context(nc.psum_tensor("psum", [P, 8, 512], F32))

        x = sb("x", [P, TILES, D])
        xn = sb("xn", [P, TILES, D])
        ident = sb("ident", [P, P])
        ident_r = sb("ident_r", [P, P], F32R)
        neg_half = sb("neg_half", [P, 4 * H * GT * 2])
        zeros = sb("zeros", [P, D])
        stat = sb("stat", [P, TILES, 6])
        mean_var = sb("mean_var", [P, TILES, 2])
        rstd = sb("rstd", [P, TILES])

        own = [sb(f"own{i}", [P, CT], U32) for i in range(2)]
        tokens = sb("tokens", [P, E, CT], U32)

        att = ExitStack()
        kT = sb("kT", [P, H, 2, KEYS], F32R, att)
        v = sb("v", [P, KT, H, P], F32R, att)
        qT = sb("qT", [P, H, S], F32R, att)
        wqkv_h = sb("wqkv_h", [P, KC, 3 * D], F32R, att)
        wqkv_l = sb("wqkv_l", [P, KC, 3 * D], F32R, att)
        wo_h = sb("wo_h", [P, H, D], F32R, att)
        wo_l = sb("wo_l", [P, H, D], F32R, att)
        qk_gain = sb("qk_gain", [P, 2 * D], F32, att)
        bo = sb("bo", [P, D], F32, att)
        ln_g = sb("ln_g", [P, KC], F32, att)
        ln_b = sb("ln_b", [P, KC], F32, att)
        mask_rows = sb("mask_rows", [P, B, PIECE], BF16, att)
        first_row = sb("first_row", [P, P], BF16, att)
        prj = ExitStack()
        xt = sb("xt", [P, GT, D], F32, prj)
        lnf = sb("lnf", [P, GT, KC, P], F32, prj)
        lnh = sb("lnh", [P, GT, KC, P], F32R, prj)
        lnl = sb("lnl", [P, GT, KC, P], F32R, prj)
        qkv = sb("qkv", [P, GT, 3 * D], F32, prj)
        sq = sb("sq", [P, 2, 2 * D], F32, prj)
        ssq = sb("ssq", [P, GT, 2 * H], F32, prj)
        rms = sb("rms", [P, GT, 2 * H], F32, prj)
        parts = sb("parts", [P, 2, 3 * H, P], F32R, prj)
        prj.close()
        raw = ExitStack()
        wqkv = sb("wqkv", [P, KC, 3 * D], F32, raw)
        wkvx = sb("wkvx", [PX, KX, 2 * D], F32, raw)
        wkvx_h = sb("wkvx_h", [PX, KX, 2 * D], F32R, raw)
        wkvx_l = sb("wkvx_l", [PX, KX, 2 * D], F32R, raw)
        wo = sb("wo", [P, H, D], F32, raw)
        xc = sb("xc", [P, DC], F32, raw)
        xcn = sb("xcn", [P, DC], F32, raw)
        cf = sb("cf", [PX, KX, P], F32, raw)
        ch = sb("ch", [PX, KX, P], F32R, raw)
        cl = sb("cl", [PX, KX, P], F32R, raw)
        lnx_g = sb("lnx_g", [PX, KX], F32, raw)
        lnx_b = sb("lnx_b", [PX, KX], F32, raw)
        ckv = sb("ckv", [P, 2 * D], F32, raw)
        csq = sb("csq", [P, D], F32, raw)
        cstat = sb("cstat", [P, 6], F32, raw)
        cmv = sb("cmv", [P, 2], F32, raw)
        crs = sb("crs", [P, 1], F32, raw)
        cms = sb("cms", [P, H], F32, raw)
        cparts = sb("cparts", [P, 2 * H, P], F32R, raw)
        mask_u8 = sb("mask_u8", [1, B * C], U8, raw)
        mask_f = sb("mask_f", [1, B * C], F32, raw)
        raw.close()
        act_ = ExitStack()
        qs = sb("qs", [P, H, GT * P], F32R, act_)
        prob = sb("prob", [P, 3, KEYS], F32, act_)
        pT_h = sb("pT_h", [P, KT, GT * P], F32R, act_)
        pT_l = sb("pT_l", [P, KT, GT * P], F32R, act_)
        rep_rd = sb("rep_rd", [P, GT * P], F32, act_)
        oT = sb("oT", [P, GT * P], F32, act_)
        oT_h = sb("oT_h", [P, H, GT * P], F32R, act_)
        oT_l = sb("oT_l", [P, H, GT * P], F32R, act_)
        neg_max = sb("neg_max", [P, UNITS], F32, act_)
        denom = sb("denom", [P, UNITS], F32, act_)
        rdenom = sb("rdenom", [P, UNITS], F32, act_)
        act_.close()
        att.close()

        moe = ExitStack()
        w_raw = sb("w_raw", [P, FW], F32, moe)
        w_h = [sb(f"w_h{i}", [P, FW], F32R, moe) for i in range(2)]
        w_l = [sb(f"w_l{i}", [P, FW], F32R, moe) for i in range(2)]
        xs0 = sb("xs0", [P, GT, D], F32, moe)
        xnT = sb("xnT", [P, GT, KC, P], F32, moe)
        gate_w = sb("gate_w", [P, KC, E], F32, moe)
        xb = sb("xb", [P, D], F32, moe)
        xbT_h = sb("xbT_h", [P, KC, P], F32R, moe)
        xbT_l = sb("xbT_l", [P, KC, P], F32R, moe)
        silu = sb("silu", [P, F], F32, moe)
        hid = sb("hid", [P, FT * P], F32, moe)
        hT_h = sb("hT_h", [P, FT, P], F32R, moe)
        hT_l = sb("hT_l", [P, FT, P], F32R, moe)
        y_sb = sb("y_sb", [P, D], F32, moe)
        logit = sb("logit", [P, TILES, E], F32, moe)
        mx = sb("mx", [P, TILES], F32, moe)
        rsum = sb("rsum", [P, TILES], F32, moe)
        eq = sb("eq", [P, TILES, E], F32, moe)
        pick = [sb(f"pick{i}", [P, TILES, E], F32, moe) for i in range(2)]
        both = sb("both", [P, TILES, E], F32, moe)
        weight = [sb(f"weight{i}", [P, TILES], F32, moe) for i in range(2)]
        scan = [sb(f"scan{i}", [P, TILES, E], F32, moe) for i in range(2)]
        totals = sb("totals", [P, TILES, E], F32, moe)
        blocks = sb("blocks", [P, E], F32, moe)
        blocks_i = sb("blocks_i", [P, E], I32, moe)
        starts = [sb(f"starts{i}", [P, E + 1], F32, moe) for i in range(2)]
        table = sb("table", [P, 2, E + 2], I32, moe)
        slot_f = sb("slot_f", [P, TILES], F32, moe)
        slot = [sb(f"slot{i}", [P, TILES], U32, moe) for i in range(2)]
        before = sb("before", [P, P], F32, moe)
        ones = sb("ones", [P, P], F32, moe)
        favour = sb("favour", [P, TILES, E], F32, moe)
        y_got = sb("y_got", [P, 4, D], F32, moe)
        moe.close()

        at1 = ExitStack()
        a_raw = sb("a_raw", [P, 2, KC, D], F32, at1)
        a_h = sb("a_h", [P, 2, KC, D], F32R, at1)
        a_l = sb("a_l", [P, 2, KC, D], F32R, at1)
        c_raw = sb("c_raw", [PX, 2, KX, D], F32, at1)
        c_h = sb("c_h", [PX, 2, KX, D], F32R, at1)
        c_l = sb("c_l", [PX, 2, KX, D], F32R, at1)
        bo1 = sb("bo1", [P, D], F32, at1)
        xc1 = sb("xc1", [P, DC], F32, at1)
        cT_h = sb("cT_h", [PX, KX, P], F32R, at1)
        cT_l = sb("cT_l", [PX, KX, P], F32R, at1)
        cd_h = sb("cd_h", [PX, KX, B, 2, C], F32R, at1)
        cd_l = sb("cd_l", [PX, KX, B, 2, C], F32R, at1)
        kb_h = sb("kb_h", [P, B, KC, H * C], F32R, at1)
        kb_l = sb("kb_l", [P, B, KC, H * C], F32R, at1)
        vb_h = sb("vb_h", [P, B, KC, P], F32R, at1)
        vb_l = sb("vb_l", [P, B, KC, P], F32R, at1)
        vs_h = sb("vs_h", [P, KC, P], F32R, at1)
        vs_l = sb("vs_l", [P, KC, P], F32R, at1)
        xs1 = sb("xs1", [P, GT, D], F32, at1)
        x1_h = sb("x1_h", [P, KC, GT * P], F32R, at1)
        x1_l = sb("x1_l", [P, KC, GT * P], F32R, at1)
        q1_h = sb("q1_h", [P, KC, GT * P], F32R, at1)
        q1_l = sb("q1_l", [P, KC, GT * P], F32R, at1)
        p1 = sb("p1", [P, GT, H * C], F32, at1)
        m1 = sb("m1", [P, GT, H], F32, at1)
        d1 = sb("d1", [P, GT, H], F32, at1)
        p1T_h = sb("p1T_h", [P, KC, GT * P], F32R, at1)
        p1T_l = sb("p1T_l", [P, KC, GT * P], F32R, at1)
        o1_h = sb("o1_h", [P, KC, GT * P], F32R, at1)
        o1_l = sb("o1_l", [P, KC, GT * P], F32R, at1)
        at1.close()

        ff1 = ExitStack()
        v_raw = sb("v_raw", [P, FW1], F32, ff1)
        v_h = [sb(f"v_h{i}", [P, FW1], F32R, ff1) for i in range(2)]
        v_l = [sb(f"v_l{i}", [P, FW1], F32R, ff1) for i in range(2)]
        b1 = sb("b1", [P, E * FT1], F32, ff1)
        b2 = sb("b2", [P, E, D], F32, ff1)
        cho = ExitStack()
        gate1_w = sb("gate1_w", [P, KC, E], F32, cho)
        xs2 = sb("xs2", [P, GT, D], F32, cho)
        xnT1 = sb("xnT1", [P, GT, KC, P], F32, cho)
        gates = sb("gates", [P, TILES, E], F32, cho)
        known = sb("known", [P, E], F32, cho)
        trial = sb("trial", [P, 3, E], F32, cho)
        best = sb("best", [P, E], F32, cho)
        cand = sb("cand", [P, 3, E], I32, cho)
        pair = sb("pair", [P, 3, E], I32, cho)
        over = sb("over", [P, 3, TILES, E], BF16, cho)
        tally3 = sb("tally3", [P, 3, E], F32, cho)
        ones_b = sb("ones_b", [P, P], BF16, cho)
        tally = sb("tally", [P, E], F32, cho)
        above = sb("above", [P, TILES, E], F32, cho)
        ties = sb("ties", [P, TILES, E], F32, cho)
        chosen = sb("chosen", [P, TILES, E], F32, cho)
        scan1 = [sb(f"scan1{i}", [P, TILES, E], F32, cho) for i in range(2)]
        totals1 = sb("totals1", [P, TILES, E], F32, cho)
        place_i = sb("place_i", [P, TILES, E], I32, cho)
        row_i = sb("row_i", [P, TILES, E], I32, cho)
        row_f = sb("row_f", [P, TILES, E], F32, cho)
        tile_f = sb("tile_f", [P, TILES, E], F32, cho)
        before1 = sb("before1", [P, P], F32, cho)
        ones1 = sb("ones1", [P, P], F32, cho)
        columns = sb("columns", [P, P], F32, cho)
        lane = sb("lane", [P, 1], F32, cho)
        tile_no = sb("tile_no", [P, TILES], F32, cho)
        hot = sb("hot", [P, 2, E, P], BF16, cho)
        put = sb("put", [P, TILES, E, 2, CT], BF16, cho)
        put_f = sb("put_f", [P, TILES, E, CT], F32, cho)
        found = sb("found", [P, E, 2 * CT], F32, cho)
        cho.close()
        wrk = ExitStack()
        gathered = [sb(f"gathered{i}", [P, CT, XG], F32, wrk) for i in range(2)]
        xe_h = sb("xe_h", [P, KC, CHOSEN], F32R, wrk)
        xe_l = sb("xe_l", [P, KC, CHOSEN], F32R, wrk)
        gl = sb("gl", [P, 2, CHOSEN], F32, wrk)
        g_h = sb("g_h", [P, FT1, CHOSEN], F32R, wrk)
        g_l = sb("g_l", [P, FT1, CHOSEN], F32R, wrk)
        gval = sb("gval", [P, 2, CT], F32, wrk)
        ye1 = sb("ye1", [P, CT, D], F32, wrk)
        wrk.close()
        ff1.close()
        rows1 = nc.dram_tensor("token_rows", [T, XG], F32, kind="Internal").ap()
        rows = nc.dram_tensor("expert_rows", [(ROUTED + TILES) * P, D], F32, kind="Internal").ap()
        results = nc.dram_tensor("expert_results", [(ROUTED + TILES) * P, D], F32, kind="Internal").ap()

        names = """x_in consts w_in ident0 ident1 identr cst stat_s aggr_s veps rstd_s xn_s xt_s tp lnf_s
            lnh_s lnl_s qkv_s raw_s sq_s ss_s rms0 rms_s nrm_s ng_s hi_s lo_s vh_s vl_s t12 ev_a
            ev_d wsp_h wsp_l mask_s c_dve c_act c_pool c_pe qs_s sc_s mx_s exp_s rc_s pt_s ph_s
            ring0 ring1 ol_s sr_s o_s oh_s y_s xb_s ones_s zero_s zeroed gw_in xs0_s tp0 xnT_s lg_s
            lgc rt rt_e rt_pe tbl scat wr_in ws_h ws_l tx xbi xh_s xl_s gu si_s h_s th hh_s hl_s yo
            ye yst got0 got1 out0 a1_in a1_h a1_l zk c1_pe c1_act c1_dve vsc xs1_s tp1 x1h x1l q1
            q1h q1l sc1 mx1 sb1 e1 sm1 rc1 pn1 pt1 p1h p1l o1 o1h o1l y1 x1a x1b v_in vs_hs vs_ls
            b_in k1c r1 r1_e srch cmpd cnt met own hots hot_pe found_s cnd shf best cns eno row1 ga0
            ga1 xe_t xe_hs xe_ls h1 gl_s gh_s gls gval_s y1e yb1 ys1 sadd""".split()
        s = {n: sem(n) for n in names}
        block = ctx.enter_context(nc.Block())

        x_tiled = ap["x"].rearrange("(t p) d -> p t d", p=P)
        out_tiled = out.rearrange("(t p) d -> p t d", p=P)

        def projected(engine, b):
            engine.wait_ge(s["vl_s"], (b + 1) * (GPB * GT))
            engine.wait_ge(s["ev_a"], 1 + (b + 1) * (GPB * 6))
            engine.wait_ge(s["ev_d"], 1 + (b + 1) * (GPB * 6))

        def attention_done(engine):
            for bank in range(2):
                engine.wait_ge(s[f"ring{bank}"], 1 + GROUPS * RING[bank])

        @block.sync
        def _(sp):
            for name in COUNT_FROM_ONE:
                sp.sem_inc(s[name], 1)
            for g in range(GROUPS):
                sp.dma_start(x[:, g * GT:(g + 1) * GT, :], x_tiled[:, g * GT:(g + 1) * GT, :]).then_inc(s["x_in"], 16)
            sp.dma_start(xc[:], ap["ctx"]).then_inc(s["consts"], 16)
            sp.dma_start(lnx_g[:], ap["lnx_g"]).then_inc(s["consts"], 16)
            sp.dma_start(lnx_b[:], ap["lnx_b"]).then_inc(s["consts"], 16)
            sp.dma_start(ln_g[:], ap["ln_g"]).then_inc(s["consts"], 16)
            sp.dma_start(ln_b[:], ap["ln_b"]).then_inc(s["consts"], 16)
            sp.dma_start(qk_gain[:], ap["qk_gain"].partition_broadcast(P)).then_inc(s["consts"], 16)
            sp.dma_start(bo[:], ap["bo0"].partition_broadcast(P)).then_inc(s["consts"], 16)
            sp.dma_start(mask_u8[:], ap["mask"]).then_inc(s["consts"], 16)
            sp.dma_start(wkvx[:], ap["wkvx"]).then_inc(s["w_in"], 16)
            sp.dma_start(wqkv[:], ap["wqkv"]).then_inc(s["w_in"], 16)
            sp.dma_start(wo[:], ap["wo0"]).then_inc(s["w_in"], 16)
            sp.wait_ge(s["zero_s"], 1)
            for part in (rows[0:ROUTED * P], results[0:ROUTED * P]):
                sp.dma_start(part.rearrange("(n p) d -> p n d", p=P),
                             zeros[:].unsqueeze(1).broadcast_to((P, ROUTED, D))).then_inc(s["zeroed"], 16)
            attention_done(sp)
            sp.dma_start(gate_w[:], ap["gate0"]).then_inc(s["gw_in"], 16)
            sp.wait_ge(s["xn_s"], 3 * TILES)
            with sp.Fori(0, SHARED) as n:
                sp.wait_ge(s["tx"], 1 + n)
                sp.dma_start(xb[:], xn[:, ds(n, 1), :].rearrange("p o d -> p (o d)")).then_inc(s["xbi"], 16)

            def load_block(m):
                sp.wait_ge(s["tx"], 1 + m + SHARED)
                sp.dma_start(xb[:], rows[ds(m * P, P), :]).then_inc(s["xbi"], 16)

            sp.wait_ge(s["scat"], 2 * TILES * 16)
            load_block(0)
            sp.wait_ge(s["tbl"], 2)
            with sp.Fori(0, E) as e:
                first = sp.value_load(table[0:1, 0, ds(e + 1, 1)], min_val=0, max_val=ROUTED - 2)
                count = sp.value_load(table[0:1, 1, ds(e + 1, 1)], min_val=1, max_val=TILES)
                with sp.Fori(0, count) as i:
                    n = sp.snap(first + i + SHARED)
                    load_block(first + i + 1)
                    sp.wait_ge(s["ye"], 1 + n + 1)
                    sp.dma_start(results[ds((first + i) * P, P), :], y_sb[:]).then_inc(s["yst"], 16)

            sp.wait_ge(s["out0"], TILES)
            sp.dma_start(xc1[:], ap["ctx"]).then_inc(s["a1_in"], 16)
            sp.dma_start(c_raw[:], ap["wkv1"]).then_inc(s["a1_in"], 16)
            sp.dma_start(a_raw[:], ap["wqo1"]).then_inc(s["a1_in"], 16)
            sp.dma_start(bo1[:], ap["bo1"].partition_broadcast(P)).then_inc(s["a1_in"], 16)

            sp.wait_ge(s["x1b"], TILES)
            sp.dma_start(v_raw[:], ap["experts1"][0]).then_inc(s["v_in"], 16)
            sp.dma_start(gate1_w[:], ap["gate1"]).then_inc(s["gw_in"], 16)
            sp.dma_start(b1[:], ap["b1"]).then_inc(s["b_in"], 16)
            sp.dma_start(b2[:].rearrange("p e d -> p (e d)"), ap["b2"].partition_broadcast(P)).then_inc(s["b_in"], 16)
            rows1_tiled = rows1.rearrange("(t p) d -> p t d", p=P)
            sp.wait_ge(s["xn_s"], 5 * TILES)
            sp.dma_start(rows1_tiled[:, :, 0:D], xn[:]).then_inc(s["row1"], 16)
            sp.wait_ge(s["r1"], R1_GATES)
            sp.dma_start(rows1_tiled[:, :, D:XG], gates[:]).then_inc(s["row1"], 16)
            sp.wait_ge(s["row1"], 32)
            with sp.Fori(1, E) as w:
                sp.wait_ge(s["vs_ls"], w * CUTS)
                sp.dma_start(v_raw[:], ap["experts1"][ds(w, 1)].rearrange("o p c -> p (o c)")).then_inc(s["v_in"], 16)

        @block.gpsimd
        def _(pool):
            pool.memset(zeros[:], 0.0).then_inc(s["zero_s"], 1)
            pool.memset(ident[:], 0.0).then_inc(s["ident0"], 1)
            pool.memset(neg_half[:], -0.5).then_inc(s["cst"], 1)
            pool.wait_ge(s["ident0"], 1)
            pool.affine_select(out=ident[:], in_=ident[:], compare_op=ALU.not_equal, fill=1.0, base=0,
                               pattern=[[-1, P]], channel_multiplier=1).then_inc(s["ident1"], 1)
            pool.memset(mask_rows[:], 0.0).then_inc(s["cst"], 1)
            pool.memset(first_row[:], 0.0).then_inc(s["cst"], 1)
            pool.wait_ge(s["cst"], 3)
            pool.memset(mask_rows[0:1, :, PIECE - P:], -BIG).then_inc(s["cst"], 1)
            pool.memset(first_row[0:1], 1.0).then_inc(s["cst"], 1)
            pool.wait_ge(s["consts"], 8 * 16)
            pool.tensor_scalar(qk_gain[:, 0:D], qk_gain[:, 0:D], HD ** -0.5, None, ALU.mult).then_inc(s["cst"], 1)
            pool.wait_ge(s["cst"], 6)

            pool.wait_ge(s["c_dve"], 2)
            pool.tensor_scalar(crs[:], cmv[:, 1:2], LN_EPS, None, ALU.add).then_inc(s["c_pool"], 1)
            pool.wait_ge(s["c_pool"], 1)
            pool.tensor_tensor(crs[:], crs[:], neg_half[:, 0:1], ALU.pow).then_inc(s["c_pool"], 1)

            def inverse_std(n):
                pool.wait_ge(s["aggr_s"], TILES * (n + 1))
                pool.tensor_scalar(rstd[:], mean_var[:, :, 1], LN_EPS, None, ALU.add).then_inc(s["veps"], 1)
                pool.wait_ge(s["veps"], n + 1)
                pool.tensor_tensor(rstd[:], rstd[:], neg_half[:, 0:TILES], ALU.pow).then_inc(s["rstd_s"], 1)

            pool.wait_ge(s["wsp_h"], 3)
            pool.tensor_tensor(wkvx_l[:], wkvx[:], wkvx_h[:].bitcast(F32), ALU.subtract).then_inc(s["wsp_l"], 1)
            pool.tensor_tensor(wqkv_l[:], wqkv[:], wqkv_h[:].bitcast(F32), ALU.subtract).then_inc(s["wsp_l"], 1)
            pool.tensor_tensor(wo_l[:], wo[:], wo_h[:].bitcast(F32), ALU.subtract).then_inc(s["wsp_l"], 1)

            pool.wait_ge(s["c_dve"], 6)
            pool.tensor_scalar(cms[:], cms[:], 1.0 / HD, RMS_EPS ** 2, ALU.mult, ALU.max).then_inc(s["c_pool"], 1)
            pool.wait_ge(s["c_pool"], 3)
            pool.tensor_tensor(cms[:], cms[:], neg_half[:, 0:H], ALU.pow).then_inc(s["c_pool"], 1)

            for n in range(2):
                inverse_std(n)

            pool.wait_ge(s["xn_s"], TILES)
            for t in range(TILES):
                pool.tensor_tensor(x[:, t, :], x[:, t, :], bo[:], ALU.add).then_inc(s["xb_s"], 1)

            with pool.Fori(0, B) as b:
                with pool.Fori(0, GPB) as gg:
                    g = b * GPB + gg
                    for t in range(GT):
                        pool.wait_ge(s["lnh_s"], g * GT + t + 1)
                        pool.tensor_tensor(lnl[:, t], lnf[:, t], lnh[:, t].bitcast(F32), ALU.subtract).then_inc(s["lnl_s"], 1)
                    pool.wait_ge(s["ss_s"], (g + 1) * GT)
                    pool.sem_inc(s["met"], 1)
                    pool.tensor_scalar(rms[:], ssq[:], 1.0 / HD, RMS_EPS ** 2, ALU.mult, ALU.max).then_inc(s["rms0"], 1)
                    pool.wait_ge(s["rms0"], g + 1)
                    pool.tensor_tensor(rms[:], rms[:], neg_half[:, 0:2 * H * GT].rearrange("p (t h) -> p t h", t=GT),
                                       ALU.pow).then_inc(s["rms_s"], 1)
                    for t in range(GT):
                        pool.wait_ge(s["nrm_s"], g * GT + t + 1)
                        pool.tensor_tensor(qkv[:, t, 0:2 * D], qkv[:, t, 0:2 * D], qk_gain[:], ALU.mult).then_inc(s["ng_s"], 1)
                        pool.wait_ge(s["vh_s"], g * GT + t + 1)
                        vt = v[:, ds(gg * GT + t, 1), :, :]
                        pool.tensor_tensor(vt[:, 0, :, HD:P], qkv[:, t, 2 * D:].rearrange("p (h d) -> p h d", h=H),
                                           vt[:, 0, :, 0:HD].bitcast(F32), ALU.subtract).then_inc(s["vl_s"], 1)
                with pool.Fori(0, GPB) as gg:
                    g = b * GPB + gg
                    for h in range(H):
                        pool.wait_ge(s["oh_s"], g * H + h + 1)
                        pool.tensor_tensor(oT_l[:, h, :], oT[:], oT_h[:, h, :].bitcast(F32), ALU.subtract).then_inc(s["ol_s"], 1)

            attention_done(pool)
            pool.memset(ones[:], 1.0).then_inc(s["ones_s"], 1)
            pool.memset(before[:], 1.0).then_inc(s["ones_s"], 1)
            pool.iota(favour[:], pattern=[[0, TILES], [-1, E]], base=E, channel_multiplier=0,
                      allow_small_or_imprecise_dtypes=True).then_inc(s["ones_s"], 1)
            pool.wait_ge(s["ones_s"], 3)
            pool.affine_select(out=before[:], in_=before[:], compare_op=ALU.is_ge, fill=0.0, base=-1,
                               pattern=[[1, P]], channel_multiplier=-1).then_inc(s["ones_s"], 1)
            inverse_std(2)

            def load_weights(w):
                pool.dma_start(w_raw[:], ap["experts0"][ds(w, 1)].rearrange("o p c -> p (o c)")).then_inc(s["wr_in"], 16)

            def split_weights(w, side):
                pool.wait_ge(s["wr_in"], 16 * (w + 1))
                pool.sem_inc(s["met"], 1)
                pool.tensor_copy(w_h[side][:], w_raw[:]).then_inc(s["ws_h"], 1)
                pool.wait_ge(s["ws_h"], w + 1)
                pool.tensor_tensor(w_l[side][:], w_raw[:], w_h[side][:].bitcast(F32), ALU.subtract).then_inc(s["ws_l"], 1)
                pool.wait_ge(s["ws_l"], w + 1)

            load_weights(0)
            split_weights(0, 0)
            load_weights(1)
            split_weights(1, 1)
            load_weights(2)
            pool.wait_ge(s["zeroed"], 32)
            pool.wait_ge(s["tbl"], 2)
            for t in range(TILES):
                for k in range(2):
                    pool.indirect_dma_start(out=rows[0:ROUTED * P], out_offset=bass.IndirectOffsetOnAxis(ap=slot[k][:, t:t + 1], axis=0),
                                            in_=xn[:, t, :], in_offset=None, bounds_check=ROUTED * P - 1,
                                            oob_is_err=False).then_inc(s["scat"], 16)
            with pool.Fori(0, (E - 2) // 2) as p:
                for side in range(2):
                    w = p * 2 + 2 + side
                    done = pool.value_load(table[0:1, 0, ds(w - 1, 1)], min_val=0, max_val=ROUTED)
                    pool.wait_ge(s["yo"], done + SHARED)
                    pool.sem_inc(s["met"], 1)
                    split_weights(w, side)
                    load_weights(w + 1)
            done = pool.value_load(table[0:1, 0, E - 1:E], min_val=0, max_val=ROUTED)
            pool.wait_ge(s["yo"], done + SHARED)
            pool.sem_inc(s["met"], 1)
            split_weights(E, 0)
            total = pool.value_load(table[0:1, 0, E + 1:E + 2], min_val=1, max_val=ROUTED)
            pool.wait_ge(s["yst"], 1 + total * 16)
            pool.sem_inc(s["met"], 1)
            for t in range(TILES):
                for k in range(2):
                    n = 2 * t + k
                    if n >= 4:
                        pool.wait_ge(s["out0"], (n - 4) // 2 + 1)
                    pool.indirect_dma_start(out=y_got[:, n % 4, :], out_offset=None, in_=results[0:ROUTED * P],
                                            in_offset=bass.IndirectOffsetOnAxis(ap=slot[k][:, t:t + 1], axis=0),
                                            bounds_check=ROUTED * P - 1, oob_is_err=False).then_inc(s[f"got{t % 2}"], 16)

            pool.wait_ge(s["a1_h"], 2)
            pool.wait_ge(s["a1_in"], 64)
            pool.tensor_tensor(c_l[:], c_raw[:], c_h[:].bitcast(F32), ALU.subtract).then_inc(s["a1_l"], 1)
            pool.tensor_tensor(a_l[:], a_raw[:], a_h[:].bitcast(F32), ALU.subtract).then_inc(s["a1_l"], 1)
            inverse_std(3)
            with pool.Fori(0, GROUPS) as g:
                for t in range(GT):
                    pool.wait_ge(s["x1a"], 1 + g * GT + t + 1)
                    xg = x[:, ds(g * GT + t, 1), :]
                    pool.tensor_tensor(xg[:, 0], xg[:, 0], bo1[:], ALU.add).then_inc(s["x1b"], 1)

            pool.wait_ge(s["x1b"], TILES)
            pool.dma_start(out_tiled, x[:]).then_inc(s["sadd"], 16)
            pool.memset(ones1[:], 1.0).then_inc(s["k1c"], 1)
            pool.memset(before1[:], 1.0).then_inc(s["k1c"], 1)
            pool.memset(ones_b[:], 1.0).then_inc(s["k1c"], 1)
            pool.iota(columns[:], pattern=[[1, P]], base=0, channel_multiplier=0,
                      allow_small_or_imprecise_dtypes=True).then_inc(s["k1c"], 1)
            pool.iota(lane[:], pattern=[[0, 1]], base=0, channel_multiplier=1,
                      allow_small_or_imprecise_dtypes=True).then_inc(s["k1c"], 1)
            pool.iota(tile_no[:], pattern=[[1, TILES]], base=0, channel_multiplier=0,
                      allow_small_or_imprecise_dtypes=True).then_inc(s["k1c"], 1)
            pool.wait_ge(s["k1c"], 6)
            pool.affine_select(out=before1[:], in_=before1[:], compare_op=ALU.is_ge, fill=0.0, base=-1,
                               pattern=[[1, P]], channel_multiplier=-1).then_inc(s["k1c"], 1)
            inverse_std(4)

            pool.wait_ge(s["vs_hs"], CUTS)
            for c in range(CUTS):
                cols = slice(c * CUT, (c + 1) * CUT)
                pool.tensor_tensor(v_l[0][:, cols], v_raw[:, cols], v_h[0][:, cols].bitcast(F32), ALU.subtract).then_inc(s["vs_ls"], 1)

            def gather(e, side):
                pool.tensor_copy(own[side][:], tokens[:, ds(e, 1), :].rearrange("p o t -> p (o t)")).then_inc(s["own"], 1)
                pool.wait_ge(s["own"], e + 1)
                pool.sem_inc(s["met"], 1)
                for t in range(CT):
                    pool.indirect_dma_start(
                        out=gathered[side][:, t, :], out_offset=None, in_=rows1,
                        in_offset=bass.IndirectOffsetOnAxis(ap=own[side][:, t:t + 1], axis=0),
                        bounds_check=T - 1, oob_is_err=False).then_inc(s[f"ga{side}"], 16)

            pool.wait_ge(s["row1"], 32)
            pool.wait_ge(s["found_s"], 2)
            gather(0, 0)

            def expert(e, side, last):
                pool.wait_ge(s["sadd"], 16 + e * (CT * 16))
                if not last:
                    pool.wait_ge(s["ys1"], 1 + e * CT)
                    pool.sem_inc(s["met"], 1)
                    gather(e + 1, 1 - side)
                pool.wait_ge(s["ys1"], 1 + (e + 1) * CT)
                pool.sem_inc(s["met"], 1)
                for t in range(CT):
                    pool.indirect_dma_start(
                        out=out, out_offset=bass.IndirectOffsetOnAxis(ap=own[side][:, t:t + 1], axis=0),
                        in_=ye1[:, t, :], in_offset=None, bounds_check=T - 1, oob_is_err=True,
                        compute_op=ALU.add).then_inc(s["sadd"], 16)

            with pool.Fori(0, E // 2 - 1) as p:
                for side in range(2):
                    expert(2 * p + side, side, False)
            expert(E - 2, 0, False)
            expert(E - 1, 1, True)
            pool.wait_ge(s["sadd"], 16 + E * CT * 16)

        @block.scalar
        def _(act):
            def copy(o, i, name, n=1):
                act.activation(o, i, ACT.Copy).then_inc(s[name], n)

            act.wait_ge(s["ident1"], 1)
            copy(ident_r[:], ident[:], "identr")
            act.wait_ge(s["w_in"], 48)
            copy(wkvx_h[:], wkvx[:], "wsp_h")
            copy(wqkv_h[:], wqkv[:], "wsp_h")
            copy(wo_h[:], wo[:], "wsp_h")
            act.wait_ge(s["c_dve"], 5)
            copy(ch[:], cf[:], "c_act")
            act.wait_ge(s["c_pe"], 2)
            copy(ckv[:], psum[:, 1, :], "c_act")
            act.wait_ge(s["c_act"], 2)
            act.activation(csq[:], ckv[:, 0:D], ACT.Square).then_inc(s["c_act"], 1)
            copy(v[:, KT - 1, :, 0:HD], ckv[:, D:].rearrange("p (h d) -> p h d", h=H), "c_act")
            act.wait_ge(s["c_dve"], 9)
            khead = ckv[:, 0:D].rearrange("p (h d) -> p h d", h=H).unsqueeze(2).broadcast_to((P, H, 2, HD))
            copy(cparts[:, 0:H, :].rearrange("p h (r d) -> p h r d", r=2), khead, "c_act")
            act.wait_ge(s["c_pe"], 4)
            copy(kT[:, :, 0, CTX0:], psum[:, 2, :].rearrange("p (h k) -> p h k", h=H), "c_act")

            with act.Fori(0, B) as b:
                with act.Fori(0, GPB) as gg:
                    g = b * GPB + gg
                    for t in range(GT):
                        act.wait_ge(s["lnf_s"], (g * GT + t + 1) * KC)
                        copy(lnh[:, t], lnf[:, t], "lnh_s")
                    for t in range(GT):
                        act.wait_ge(s["qkv_s"], g * GT + t + 1)
                        copy(qkv[:, t, :], psum[:, 2 * (t % 2):2 * (t % 2) + 2, :].rearrange("p b c -> p (b c)")[:, 0:3 * D],
                             "raw_s")
                        act.wait_ge(s["raw_s"], g * GT + t + 1)
                        if t >= 2:
                            act.wait_ge(s["ss_s"], g * GT + t - 1)
                        act.activation(sq[:, t % 2, :], qkv[:, t, 0:2 * D], ACT.Square).then_inc(s["sq_s"], 1)
                        vt = v[:, ds(gg * GT + t, 1), :, 0:HD]
                        copy(vt[:, 0], qkv[:, t, 2 * D:].rearrange("p (h d) -> p h d", h=H), "vh_s")

                    def high_parts(t):
                        act.wait_ge(s["ng_s"], g * GT + t + 1)
                        if t >= 2:
                            act.wait_ge(s["t12"], g * 12 + 3 * (t - 1))
                        copy(parts[:, t % 2, 0:H, 0:HD], qkv[:, t, 0:D].rearrange("p (h d) -> p h d", h=H), "hi_s")
                        kk = qkv[:, t, D:2 * D].rearrange("p (h d) -> p h d", h=H).unsqueeze(2).broadcast_to((P, H, 2, HD))
                        copy(parts[:, t % 2, H:2 * H, :].rearrange("p h (r d) -> p h r d", r=2), kk, "hi_s")

                    def evacuate(t):
                        for c in range(3):
                            if (3 * t + c) % 2 == 0:
                                act.wait_ge(s["t12"], g * 12 + 3 * t + c + 1)
                                src = psum[:, 6, :].rearrange("p (h k) -> p h k", h=H)
                                cols = ds(gg * (GT * P) + t * P, P)
                                dst = qT[:, :, cols] if c == 0 else kT[:, :, c - 1, cols]
                                copy(dst, src, "ev_a")

                    high_parts(0)
                    for t in range(GT):
                        if t + 1 < GT:
                            high_parts(t + 1)
                        evacuate(t)
                with act.Fori(0, GPB) as gg:
                    g = b * GPB + gg

                    def exponentials(u):
                        act.wait_ge(s["mx_s"], g * UNITS + u + 1)
                        if u >= 3:
                            act.wait_ge(s["pt_s"], (g * UNITS + u - 2) * 3)
                        z = 3 * (u % 2)
                        act.activation(prob[:, u % 3, :].rearrange("p (c k) -> p c k", c=3), psum[:, z:z + 3, 0:PIECE],
                                       ACT.Exp, bias=neg_max[:, u:u + 1],
                                       accum_out=denom[:, u:u + 1]).then_inc(s["exp_s"], 1)

                    def chunk_high(u, c):
                        act.wait_ge(s["pt_s"], (g * UNITS + u) * 3 + c + 1)
                        n = min(4, KT - 4 * c)
                        copy(pT_h[:, 4 * c:4 * c + n, (u % GT) * P:(u % GT + 1) * P],
                             psum[:, 6 + USES["chunk", u, c][0], 0:n * P].rearrange("p (k c) -> p k c", k=n), "ph_s")

                    def repeated(h):
                        bank, _ = USES["reciprocals", h]
                        act.wait_ge(s["sr_s"], g * H + h + 1)
                        copy(rep_rd[:], psum[:, 6 + bank, :], f"ring{bank}")

                    def out_high(h):
                        bank, before = USES["result", h]
                        act.wait_ge(s[f"ring{bank}"], 1 + g * RING[bank] + before + 1)
                        copy(oT_h[:, h, :], oT[:], "oh_s")

                    projected(act, b)
                    copy(qs[:, 0:2], qT[:, 0:2, ds(gg * GT * P, GT * P)].bitcast(F32), "qs_s")
                    exponentials(0)
                    for u in range(UNITS):
                        chunk_high(u, 0)
                        chunk_high(u, 1)
                        if u + 1 < UNITS:
                            exponentials(u + 1)
                        chunk_high(u, 2)
                        if u % GT == 0 and u:
                            out_high(u // GT - 1)
                        if u % GT == GT - 1:
                            repeated(u // GT)
                    out_high(H - 1)

            def gate_logits(layer, xs0, xnT, logit):
                act.wait_ge(s["xn_s"], (3 if layer == 0 else 5) * TILES)
                with act.Fori(0, GROUPS) as g0:
                    g = g0 + layer * GROUPS
                    for t in range(GT):
                        copy(xs0[:, t, :], xn[:, ds(g0 * GT + t, 1), :].rearrange("p o d -> p (o d)"), "xs0_s")
                    for t in range(GT):
                        act.wait_ge(s["tp0"], g * GT + t + 1)
                        copy(xnT[:, t], psum[:, t, 0:D].rearrange("p (k c) -> p k c", k=KC), "xnT_s")
                    act.wait_ge(s["lg_s"], g * GT + GT)
                    copy(logit[:, ds(g0 * GT, GT), :], psum[:, 4, 0:GT * E].rearrange("p (t e) -> p t e", t=GT), "lgc")

            gate_logits(0, xs0, xnT, logit)
            act.wait_ge(s["rt"], RT_SHIFTED)
            act.activation(logit[:], logit[:], ACT.Exp).then_inc(s["rt_e"], 1)

            def x_high(n):
                act.wait_ge(s["tx"], 1 + n + 1)
                copy(xbT_h[:], psum[:, 4, 0:D].rearrange("p (k c) -> p k c", k=KC), "xh_s")

            def block_high(n):
                for c, (lo, hi) in enumerate(((0, FA), (FA, F))):
                    act.wait_ge(s["gu"], n * 4 + 2 * c + 1)
                    act.activation(silu[:, lo:hi], psum[:, 2 * c, 0:hi - lo], ACT.Silu).then_inc(s["si_s"], 1)
                x_high(n + 1)
                for c in range(2):
                    act.wait_ge(s["th"], n * 2 + c + 1)
                    copy(hT_h[:, 3 * c:3 * c + 3, :], psum[:, 5 + c, 0:3 * P].rearrange("p (k c) -> p k c", k=3), "hh_s")

            x_high(0)
            with act.Fori(0, SHARED) as n:
                block_high(n)
            act.wait_ge(s["tbl"], 2)
            with act.Fori(0, E) as e:
                first = act.value_load(table[0:1, 0, ds(e + 1, 1)], min_val=0, max_val=ROUTED - 2)
                count = act.value_load(table[0:1, 1, ds(e + 1, 1)], min_val=1, max_val=TILES)
                with act.Fori(0, count) as i:
                    n = act.snap(first + i + SHARED)
                    block_high(n)
                    act.wait_ge(s["yo"], n + 1)
                    act.wait_ge(s["yst"], 1 + (first + i) * 16)
                    copy(y_sb[:], psum[:, 7, 0:D], "ye")

            act.wait_ge(s["a1_in"], 64)
            copy(c_h[:], c_raw[:], "a1_h")
            copy(a_h[:], a_raw[:], "a1_h")
            act.wait_ge(s["c1_pe"], 1)
            copy(cT_h[:], psum[0:PX, 0, 0:KX * P].rearrange("p (k c) -> p k c", k=KX), "c1_act")
            act.wait_ge(s["c1_dve"], 1)
            for k in range(KX):
                for src, dst in ((cT_h, cd_h), (cT_l, cd_l)):
                    act.wait_ge(s["c1_act"], 1)
                    copy(dst[:, k], src[:, k, :].bitcast(F32).rearrange("p (b c) -> p b c", b=B).unsqueeze(2)
                         .broadcast_to((PX, B, 2, C)), "c1_act")
            act.wait_ge(s["c1_pe"], 3)
            act.wait_ge(s["zk"], 2)
            for k in range(KC):
                for hh in range(2):
                    half = slice(hh * C, (hh + 1) * C)
                    head = 2 * k + hh
                    copy(kb_h[half, :, k, head * C:(head + 1) * C],
                         psum[half, 1, k * P:(k + 1) * P].rearrange("p (b c) -> p b c", b=B), "c1_act")
                    copy(vb_h[half, :, k, hh * HD:(hh + 1) * HD],
                         psum[half, 2, :].rearrange("p (b d) -> p b d", b=B)[:, :, head * HD:(head + 1) * HD], "c1_act")
            act.wait_ge(s["c1_dve"], 1 + 4 * KC)
            act.wait_ge(s["c1_act"], 5 + 4 * KC)
            act.wait_ge(s["xn_s"], 4 * TILES)
            with act.Fori(0, B) as b:
                with act.Fori(0, GPB) as gg:
                    g = b * GPB + gg
                    copy(vs_h[:], vb_h[:, ds(b, 1)].rearrange("p o k d -> p (o k) d").bitcast(F32), "vsc")
                    copy(vs_l[:], vb_l[:, ds(b, 1)].rearrange("p o k d -> p (o k) d").bitcast(F32), "vsc")
                    for t in range(GT):
                        copy(xs1[:, t, :], xn[:, ds(g * GT + t, 1), :].rearrange("p o d -> p (o d)"), "xs1_s")
                    for t in range(GT):
                        act.wait_ge(s["tp1"], g * GT + t + 1)
                        copy(x1_h[:, :, t * P:(t + 1) * P], psum[:, t, 0:D].rearrange("p (k c) -> p k c", k=KC), "x1h")
                    for k in range(KC):
                        act.wait_ge(s["q1"], g * KC + k + 1)
                        act.activation(q1_h[:, k, :], psum[:, 4 + k, :], ACT.Copy, scale=HD ** -0.5).then_inc(s["q1h"], 1)
                    for t in range(GT):
                        act.wait_ge(s["sb1"], g * GT + t + 1)
                        act.activation(p1[:, t, :], p1[:, t, :], ACT.Exp).then_inc(s["e1"], 1)
                    for t in range(GT):
                        act.wait_ge(s["pt1"], g * GT + t + 1)
                        copy(p1T_h[:, :, t * P:(t + 1) * P], psum[:, 4 + t, 0:D].rearrange("p (k c) -> p k c", k=KC), "p1h")
                    for k in range(KC):
                        act.wait_ge(s["o1"], g * KC + k + 1)
                        copy(o1_h[:, k, :], psum[:, k, :], "o1h")

            gate_logits(1, xs2, xnT1, gates)
            act.wait_ge(s["lgc"], 1 + 2 * GROUPS)
            act.activation(gates[:], gates[:], ACT.Exp, scale=-1.0).then_inc(s["r1_e"], 1)

            def rows_high(n, count):
                for t in range(CT):
                    act.wait_ge(s["xe_t"], n * CT + t + 1)
                    copy(xe_h[:, :, t * P:(t + 1) * P], psum[:, 6 + t % 2, 0:D].rearrange("p (k c) -> p k c", k=KC), "xe_hs")

            def weights_high(w, side):
                act.wait_ge(s["v_in"], 16 * (w + 1))
                for c in range(CUTS):
                    cols = slice(c * CUT, (c + 1) * CUT)
                    copy(v_h[side][:, cols], v_raw[:, cols], "vs_hs")
                    yield

            def expert1(e, side, last):
                if not last:
                    act.wait_ge(s["yb1"], 1 + e * CT)
                    cuts = weights_high(e + 1, 1 - side)
                for f in range(FT1):
                    act.wait_ge(s["h1"], e * FT1 + f + 1)
                    if f >= 2:
                        act.wait_ge(s["gls"], e * FT1 + f - 1)
                    act.activation(gl[:, f % 2, :], psum[:, f % 2, :], ACT.Gelu, bias=b1[:, ds(e * FT1 + f, 1)]).then_inc(s["gl_s"], 1)
                    if not last and f % 2:
                        next(cuts)
                if not last:
                    rows_high(e + 1, CT)

            for _ in weights_high(0, 0):
                pass
            act.wait_ge(s["b_in"], 32)
            rows_high(0, CT)
            with act.Fori(0, E // 2 - 1) as p:
                for side in range(2):
                    expert1(2 * p + side, side, False)
            expert1(E - 2, 0, False)
            expert1(E - 1, 1, True)

        @block.vector
        def _(dve):
            def norm(n, src):
                for t in range(TILES):
                    dve.bn_stats(stat[:, t, :], src[:, t, :]).then_inc(s["stat_s"], 1)
                dve.wait_ge(s["stat_s"], TILES * (n + 1))
                for t in range(TILES):
                    dve.bn_aggr(mean_var[:, t, :], stat[:, t, :]).then_inc(s["aggr_s"], 1)
                dve.wait_ge(s["rstd_s"], n + 1)
                for t in range(TILES):
                    dve.tensor_scalar(xn[:, t, :], src[:, t, :], mean_var[:, t, 0:1], rstd[:, t:t + 1],
                                      ALU.subtract, ALU.mult).then_inc(s["xn_s"], 1)

            dve.wait_ge(s["consts"], 8 * 16)
            dve.bn_stats(cstat[:], xc[:]).then_inc(s["c_dve"], 1)
            dve.wait_ge(s["c_dve"], 1)
            dve.bn_aggr(cmv[:], cstat[:]).then_inc(s["c_dve"], 1)
            dve.wait_ge(s["c_pool"], 2)
            dve.tensor_scalar(xcn[:], xc[:], cmv[:, 0:1], crs[:], ALU.subtract, ALU.mult).then_inc(s["c_dve"], 1)
            dve.wait_ge(s["c_pe"], 1)
            for k in range(KX):
                dve.tensor_scalar(cf[:, k, :], psum[0:PX, 0, k * P:(k + 1) * P], lnx_g[:, k:k + 1], lnx_b[:, k:k + 1],
                                  ALU.mult, ALU.add).then_inc(s["c_dve"], 1)
            dve.wait_ge(s["c_act"], 1)
            dve.tensor_copy(mask_f[:], mask_u8[:]).then_inc(s["mask_s"], 1)
            dve.wait_ge(s["mask_s"], 1)
            dve.wait_ge(s["cst"], 5)
            for b in range(B):
                dve.tensor_scalar(mask_rows[0:1, b, PIECE - P + b * C:PIECE - P + (b + 1) * C], mask_f[:, b * C:(b + 1) * C], 1.0, BIG,
                                  ALU.subtract, ALU.mult).then_inc(s["mask_s"], 1)
            dve.tensor_tensor(cl[:], cf[:], ch[:].bitcast(F32), ALU.subtract).then_inc(s["mask_s"], 1)
            dve.wait_ge(s["c_act"], 3)
            dve.tensor_reduce(cms[:], csq[:].rearrange("p (h d) -> p h d", h=H), AX.X, ALU.add).then_inc(s["c_dve"], 1)
            dve.wait_ge(s["c_pool"], 4)
            ck = ckv[:, 0:D].rearrange("p (h d) -> p h d", h=H)
            dve.tensor_tensor(ck, ck, cms[:].unsqueeze(2).broadcast_to((P, H, HD)), ALU.mult).then_inc(s["c_dve"], 1)
            dve.wait_ge(s["c_dve"], 7)
            dve.tensor_tensor(ckv[:, 0:D], ckv[:, 0:D], qk_gain[:, D:], ALU.mult).then_inc(s["c_dve"], 1)
            dve.wait_ge(s["c_act"], 4)
            dve.tensor_tensor(v[:, KT - 1, :, HD:], ckv[:, D:].rearrange("p (h d) -> p h d", h=H),
                              v[:, KT - 1, :, 0:HD].bitcast(F32), ALU.subtract).then_inc(s["c_dve"], 1)
            dve.wait_ge(s["c_act"], 5)
            khead = ck.unsqueeze(2).broadcast_to((P, H, 2, HD))
            dve.tensor_tensor(cparts[:, H:, :].rearrange("p h (r d) -> p h r d", r=2), khead,
                              cparts[:, 0:H, :].rearrange("p h (r d) -> p h r d", r=2).bitcast(F32),
                              ALU.subtract).then_inc(s["c_dve"], 1)
            dve.wait_ge(s["c_pe"], 4)
            dve.tensor_copy(kT[:, :, 1, CTX0:], psum[:, 3, :].rearrange("p (h k) -> p h k", h=H)).then_inc(s["c_dve"], 1)

            dve.wait_ge(s["x_in"], 16 * GROUPS)
            norm(0, x)
            dve.wait_ge(s["xn_s"], TILES)
            norm(1, xn)
            dve.wait_ge(s["xn_s"], 2 * TILES)

            with dve.Fori(0, B) as b:
                with dve.Fori(0, GPB) as gg:
                    g = b * GPB + gg
                    for t in range(GT):
                        dve.tensor_copy(xt[:, t, :], xn[:, ds(g * GT + t, 1), :].rearrange("p o d -> p (o d)")).then_inc(s["xt_s"], 1)
                    for t in range(GT):
                        dve.wait_ge(s["tp"], g * GT + t + 1)
                        for k in range(KC):
                            dve.tensor_scalar(lnf[:, t, k, :], psum[:, 4 + t, k * P:(k + 1) * P], ln_g[:, k:k + 1],
                                              ln_b[:, k:k + 1], ALU.mult, ALU.add).then_inc(s["lnf_s"], 1)
                    for t in range(GT):
                        dve.wait_ge(s["sq_s"], g * GT + t + 1)
                        dve.tensor_reduce(ssq[:, t, :], sq[:, t % 2, :].rearrange("p (h d) -> p h d", d=HD), AX.X,
                                          ALU.add).then_inc(s["ss_s"], 1)
                    dve.wait_ge(s["rms_s"], g + 1)
                    for t in range(GT):
                        qk = qkv[:, t, 0:2 * D].rearrange("p (h d) -> p h d", d=HD)
                        dve.tensor_tensor(qk, qk, rms[:, t, :].unsqueeze(2).broadcast_to((P, 2 * H, HD)),
                                          ALU.mult).then_inc(s["nrm_s"], 1)

                    def low_parts(t):
                        dve.wait_ge(s["hi_s"], (g * GT + t + 1) * 2)
                        dve.tensor_tensor(parts[:, t % 2, 0:H, HD:], qkv[:, t, 0:D].rearrange("p (h d) -> p h d", h=H),
                                          parts[:, t % 2, 0:H, 0:HD].bitcast(F32), ALU.subtract).then_inc(s["lo_s"], 1)
                        kk = qkv[:, t, D:2 * D].rearrange("p (h d) -> p h d", h=H).unsqueeze(2).broadcast_to((P, H, 2, HD))
                        dve.tensor_tensor(parts[:, t % 2, 2 * H:, :].rearrange("p h (r d) -> p h r d", r=2), kk,
                                          parts[:, t % 2, H:2 * H, :].rearrange("p h (r d) -> p h r d", r=2).bitcast(F32),
                                          ALU.subtract).then_inc(s["lo_s"], 1)

                    def evacuate(t):
                        for c in range(3):
                            if (3 * t + c) % 2:
                                dve.wait_ge(s["t12"], g * 12 + 3 * t + c + 1)
                                src = psum[:, 7, :].rearrange("p (h k) -> p h k", h=H)
                                cols = ds(gg * (GT * P) + t * P, P)
                                dst = qT[:, :, cols] if c == 0 else kT[:, :, c - 1, cols]
                                dve.tensor_copy(dst, src).then_inc(s["ev_d"], 1)

                    low_parts(0)
                    for t in range(GT):
                        if t + 1 < GT:
                            low_parts(t + 1)
                        evacuate(t)
                with dve.Fori(0, GPB) as gg:
                    g = b * GPB + gg
                    def maxima(u):
                        dve.wait_ge(s["sc_s"], g * UNITS + u + 1)
                        z = 3 * (u % 2)
                        dve.tensor_reduce(neg_max[:, u:u + 1], psum[:, z:z + 3, 0:PIECE],
                                          AX.XY, ALU.max, negate=True).then_inc(s["mx_s"], 1)

                    def reciprocals(u):
                        dve.wait_ge(s["exp_s"], g * UNITS + u + 1)
                        dve.reciprocal(rdenom[:, u:u + 1], denom[:, u:u + 1]).then_inc(s["rc_s"], 1)

                    def chunk_low(u, c):
                        bank, _ = USES["chunk", u, c]
                        n = min(4, KT - 4 * c)
                        cols = slice((u % GT) * P, (u % GT + 1) * P)
                        dve.wait_ge(s["ph_s"], (g * UNITS + u) * 3 + c + 1)
                        dve.tensor_tensor(pT_l[:, 4 * c:4 * c + n, cols],
                                          psum[:, 6 + bank, 0:n * P].rearrange("p (k c) -> p k c", k=n),
                                          pT_h[:, 4 * c:4 * c + n, cols].bitcast(F32), ALU.subtract).then_inc(s[f"ring{bank}"], 1)

                    def out_scaled(h):
                        bank, _ = USES["result", h]
                        r_bank, before = USES["reciprocals", h]
                        dve.wait_ge(s[f"ring{r_bank}"], 1 + g * RING[r_bank] + before + 1)
                        dve.wait_ge(s["o_s"], g * H + h + 1)
                        if h:
                            dve.wait_ge(s["ol_s"], g * H + h)
                        dve.tensor_tensor(oT[:], psum[:, 6 + bank, :], rep_rd[:], ALU.mult).then_inc(s[f"ring{bank}"], 1)

                    projected(dve, b)
                    dve.tensor_copy(qs[:, 2:4], qT[:, 2:4, ds(gg * GT * P, GT * P)].bitcast(F32)).then_inc(s["qs_s"], 1)
                    maxima(0)
                    reciprocals(0)
                    maxima(1)
                    for u in range(UNITS):
                        chunk_low(u, 0)
                        chunk_low(u, 1)
                        if u + 2 < UNITS:
                            maxima(u + 2)
                        if u % GT == 0 and u:
                            out_scaled(u // GT - 1)
                        chunk_low(u, 2)
                        if u + 1 < UNITS:
                            reciprocals(u + 1)
                    out_scaled(H - 1)
                    for t in range(GT):
                        bank, _ = USES["output", t]
                        dve.wait_ge(s["y_s"], g * GT + t + 1)
                        if t == 0:
                            dve.wait_ge(s["xb_s"], TILES)
                        xg = x[:, ds(g * GT + t, 1), :]
                        dve.tensor_tensor(xg[:, 0], psum[:, 6 + bank, 0:D], xg[:, 0], ALU.add).then_inc(s[f"ring{bank}"], 1)

            attention_done(dve)
            norm(2, x)
            steps = [0]

            def step(ins):
                ins.then_inc(s["rt"], 1)
                steps[0] += 1
                dve.wait_ge(s["rt"], steps[0])

            def over_experts(a):
                return a[:].unsqueeze(2).broadcast_to((P, TILES, E))

            dve.wait_ge(s["lgc"], 1 + GROUPS)
            dve.wait_ge(s["ones_s"], 4)
            step(dve.tensor_reduce(mx[:], logit[:], AX.X, ALU.max))
            step(dve.tensor_tensor(logit[:], logit[:], over_experts(mx), ALU.subtract))
            dve.wait_ge(s["rt_e"], 1)
            step(dve.tensor_reduce(rsum[:], logit[:], AX.X, ALU.add))
            step(dve.reciprocal(rsum[:], rsum[:]))
            step(dve.tensor_tensor(logit[:], logit[:], over_experts(rsum), ALU.mult))
            for k in range(2):
                step(dve.tensor_reduce(weight[k][:], logit[:], AX.X, ALU.max))
                step(dve.tensor_tensor(eq[:], logit[:], over_experts(weight[k]), ALU.is_equal))
                step(dve.tensor_tensor(eq[:], eq[:], favour[:], ALU.mult))
                step(dve.tensor_reduce(mx[:], eq[:], AX.X, ALU.max))
                step(dve.tensor_tensor(pick[k][:], eq[:], over_experts(mx), ALU.is_equal))
                if k == 0:
                    step(dve.scalar_tensor_tensor(out=logit[:], in0=pick[0][:], scalar=-2.0, in1=logit[:],
                                                  op0=ALU.mult, op1=ALU.add))
            step(dve.tensor_tensor(both[:], pick[0][:], pick[1][:], ALU.add))
            def running_totals(n, scan, totals):
                dve.wait_ge(s["rt_pe"], n)
                step(dve.tensor_copy(totals[:], psum[:, 6, 0:P].rearrange("p (t e) -> p t e", e=E)))
                step(dve.tensor_copy(scan[0][:], totals[:]))
                src, shift = 0, 1
                while shift < TILES:
                    a, o = scan[src], scan[1 - src]
                    dve.tensor_copy(o[:, 0:shift], a[:, 0:shift]).then_inc(s["rt"], 1)
                    steps[0] += 1
                    step(dve.tensor_tensor(o[:, shift:], a[:, shift:], a[:, 0:TILES - shift], ALU.add))
                    src, shift = 1 - src, shift * 2
                return scan[src], scan[1 - src]

            def tokens_before(sums, free, totals):
                step(dve.tensor_tensor(free[:], sums[:], totals[:], ALU.subtract))
                step(dve.tensor_tensor(free[:], psum[:, 5, 0:P].rearrange("p (t e) -> p t e", e=E), free[:], ALU.add))
                return free

            sums, free = running_totals(1, scan, totals)
            step(dve.tensor_scalar(blocks[:], sums[:, TILES - 1, :], float(P - 1), None, ALU.add))
            step(dve.tensor_copy(blocks_i[:], blocks[:]))
            step(dve.tensor_scalar(blocks_i[:], blocks_i[:], 7, None, ALU.logical_shift_right))
            step(dve.tensor_copy(blocks[:], blocks_i[:]))
            step(dve.tensor_scalar(blocks[:], blocks[:], 1.0, None, ALU.max))
            step(dve.memset(starts[0][:, 0:1], 0.0))
            step(dve.tensor_copy(starts[0][:, 1:], blocks[:]))
            at, shift = 0, 1
            while shift < E + 1:
                a, o = starts[at], starts[1 - at]
                dve.tensor_copy(o[:, 0:shift], a[:, 0:shift]).then_inc(s["rt"], 1)
                steps[0] += 1
                step(dve.tensor_tensor(o[:, shift:], a[:, shift:], a[:, 0:E + 1 - shift], ALU.add))
                at, shift = 1 - at, shift * 2
            first_block = starts[at]
            ranks = tokens_before(sums, free, totals)
            step(dve.scalar_tensor_tensor(out=totals[:], in0=first_block[:, 0:E].unsqueeze(1).broadcast_to((P, TILES, E)),
                                          scalar=float(P), in1=ranks[:], op0=ALU.mult, op1=ALU.add))
            for k in range(2):
                step(dve.tensor_tensor(eq[:], pick[k][:], totals[:], ALU.mult))
                step(dve.tensor_reduce(slot_f[:], eq[:], AX.X, ALU.add))
                step(dve.tensor_copy(slot[k][:], slot_f[:]))
            step(dve.memset(table[:], 0))
            dve.tensor_copy(table[:, 0, 1:E + 2], first_block[:]).then_inc(s["tbl"], 1)
            dve.tensor_copy(table[:, 1, 1:E + 1], blocks[:]).then_inc(s["tbl"], 1)
            step(dve.tensor_tensor(rsum[:], weight[0][:], weight[1][:], ALU.add))
            step(dve.tensor_scalar(rsum[:], rsum[:], 1e-20, None, ALU.add))
            step(dve.reciprocal(rsum[:], rsum[:]))
            for k in range(2):
                step(dve.tensor_tensor(weight[k][:], weight[k][:], rsum[:], ALU.mult))
            step(dve.memset(hid[:, F:], 0.0))
            assert steps[0] == RT_PADDED

            def x_low(n):
                dve.wait_ge(s["xh_s"], n + 1)
                dve.tensor_tensor(xbT_l[:], psum[:, 4, 0:D].rearrange("p (k c) -> p k c", k=KC), xbT_h[:].bitcast(F32),
                                  ALU.subtract).then_inc(s["xl_s"], 1)

            def block_low(n):
                for c, (lo, hi) in enumerate(((0, FA), (FA, F))):
                    dve.wait_ge(s["si_s"], n * 2 + c + 1)
                    dve.wait_ge(s["gu"], n * 4 + 2 * c + 2)
                    dve.tensor_tensor(hid[:, lo:hi], psum[:, 2 * c + 1, 0:hi - lo], silu[:, lo:hi], ALU.mult).then_inc(s["h_s"], 1)
                x_low(n + 1)
                for c in range(2):
                    dve.wait_ge(s["hh_s"], n * 2 + c + 1)
                    dve.tensor_tensor(hT_l[:, 3 * c:3 * c + 3, :], psum[:, 5 + c, 0:3 * P].rearrange("p (k c) -> p k c", k=3),
                                      hT_h[:, 3 * c:3 * c + 3, :].bitcast(F32), ALU.subtract).then_inc(s["hl_s"], 1)

            x_low(0)
            with dve.Fori(0, SHARED) as n:
                block_low(n)
                dve.wait_ge(s["yo"], n + 1)
                xg = x[:, ds(n, 1), :]
                dve.tensor_tensor(xg[:, 0], psum[:, 7, 0:D], xg[:, 0], ALU.add).then_inc(s["ye"], 1)
            with dve.Fori(0, E) as e:
                first = dve.value_load(table[0:1, 0, ds(e + 1, 1)], min_val=0, max_val=ROUTED - 2)
                count = dve.value_load(table[0:1, 1, ds(e + 1, 1)], min_val=1, max_val=TILES)
                with dve.Fori(0, count) as i:
                    n = dve.snap(first + i + SHARED)
                    block_low(n)
            for t in range(TILES):
                for k in range(2):
                    n = 2 * t + k
                    dve.wait_ge(s[f"got{t % 2}"], 32 * (t // 2 + 1))
                    last = dve.scalar_tensor_tensor(out=x[:, t, :], in0=y_got[:, n % 4, :], scalar=weight[k][:, t:t + 1],
                                                    in1=x[:, t, :], op0=ALU.mult, op1=ALU.add)
                    if k == 0:
                        step(last)
                last.then_inc(s["out0"], 1)

            dve.wait_ge(s["out0"], TILES)
            dve.memset(kb_h[:].bitcast(F32), 0.0)
            dve.memset(kb_l[:].bitcast(F32), 0.0).then_inc(s["zk"], 1)
            dve.memset(vb_h[:].bitcast(F32), 0.0)
            dve.memset(vb_l[:].bitcast(F32), 0.0).then_inc(s["zk"], 1)
            norm(3, x)
            dve.wait_ge(s["c1_act"], 1)
            dve.tensor_tensor(cT_l[:], psum[0:PX, 0, 0:KX * P].rearrange("p (k c) -> p k c", k=KX), cT_h[:].bitcast(F32),
                              ALU.subtract).then_inc(s["c1_dve"], 1)
            dve.wait_ge(s["c1_act"], 5 + 4 * KC)
            dve.wait_ge(s["zk"], 2)
            for k in range(KC):
                for hh in range(2):
                    half = slice(hh * C, (hh + 1) * C)
                    head = 2 * k + hh
                    cols = slice(head * C, (head + 1) * C)
                    dve.tensor_tensor(kb_l[half, :, k, cols], psum[half, 1, k * P:(k + 1) * P].rearrange("p (b c) -> p b c", b=B),
                                      kb_h[half, :, k, cols].bitcast(F32), ALU.subtract).then_inc(s["c1_dve"], 1)
                    cols = slice(hh * HD, (hh + 1) * HD)
                    dve.tensor_tensor(vb_l[half, :, k, cols],
                                      psum[half, 2, :].rearrange("p (b d) -> p b d", b=B)[:, :, head * HD:(head + 1) * HD],
                                      vb_h[half, :, k, cols].bitcast(F32), ALU.subtract).then_inc(s["c1_dve"], 1)
            with dve.Fori(0, B) as b:
                with dve.Fori(0, GPB) as gg:
                    g = b * GPB + gg
                    for t in range(GT):
                        dve.wait_ge(s["x1h"], g * GT + t + 1)
                        cols = slice(t * P, (t + 1) * P)
                        dve.tensor_tensor(x1_l[:, :, cols], psum[:, t, 0:D].rearrange("p (k c) -> p k c", k=KC),
                                          x1_h[:, :, cols].bitcast(F32), ALU.subtract).then_inc(s["x1l"], 1)
                    for k in range(KC):
                        dve.wait_ge(s["q1h"], g * KC + k + 1)
                        dve.scalar_tensor_tensor(out=q1_l[:, k, :], in0=psum[:, 4 + k, :], scalar=HD ** -0.5,
                                                 in1=q1_h[:, k, :].bitcast(F32), op0=ALU.mult, op1=ALU.subtract).then_inc(s["q1l"], 1)

                    def heads(a):
                        return a.rearrange("p (h c) -> p h c", h=H)

                    for t in range(GT):
                        dve.wait_ge(s["sc1"], g * GT + t + 1)
                        dve.tensor_reduce(m1[:, t, :], heads(psum[:, t, 0:H * C]), AX.X, ALU.max).then_inc(s["mx1"], 1)
                        dve.wait_ge(s["mx1"], g * GT + t + 1)
                        dve.tensor_tensor(heads(p1[:, t, :]), heads(psum[:, t, 0:H * C]),
                                          m1[:, t, :].unsqueeze(2).broadcast_to((P, H, C)), ALU.subtract).then_inc(s["sb1"], 1)
                    for t in range(GT):
                        dve.wait_ge(s["e1"], g * GT + t + 1)
                        dve.tensor_reduce(d1[:, t, :], heads(p1[:, t, :]), AX.X, ALU.add).then_inc(s["sm1"], 1)
                    dve.wait_ge(s["sm1"], g * GT + GT)
                    dve.reciprocal(d1[:], d1[:]).then_inc(s["rc1"], 1)
                    dve.wait_ge(s["rc1"], g + 1)
                    for t in range(GT):
                        dve.tensor_tensor(heads(p1[:, t, :]), heads(p1[:, t, :]),
                                          d1[:, t, :].unsqueeze(2).broadcast_to((P, H, C)), ALU.mult).then_inc(s["pn1"], 1)
                    for t in range(GT):
                        dve.wait_ge(s["p1h"], g * GT + t + 1)
                        cols = slice(t * P, (t + 1) * P)
                        dve.tensor_tensor(p1T_l[:, :, cols], psum[:, 4 + t, 0:D].rearrange("p (k c) -> p k c", k=KC),
                                          p1T_h[:, :, cols].bitcast(F32), ALU.subtract).then_inc(s["p1l"], 1)
                    for k in range(KC):
                        dve.wait_ge(s["o1h"], g * KC + k + 1)
                        dve.tensor_tensor(o1_l[:, k, :], psum[:, k, :], o1_h[:, k, :].bitcast(F32),
                                          ALU.subtract).then_inc(s["o1l"], 1)
                    for t in range(GT):
                        dve.wait_ge(s["y1"], g * GT + t + 1)
                        xg = x[:, ds(g * GT + t, 1), :]
                        dve.tensor_tensor(xg[:, 0], psum[:, 4 + t, 0:D], xg[:, 0], ALU.add).then_inc(s["x1a"], 1)

            dve.wait_ge(s["x1b"], TILES)
            norm(4, x)
            dve.wait_ge(s["r1_e"], 1)
            dve.wait_ge(s["k1c"], 7)
            r1 = [0]

            def step1(ins):
                ins.then_inc(s["r1"], 1)
                r1[0] += 1
                dve.wait_ge(s["r1"], r1[0])

            step1(dve.tensor_scalar(gates[:], gates[:], 1.0, None, ALU.add))
            step1(dve.reciprocal(gates[:], gates[:]))
            assert r1[0] == R1_GATES
            step1(dve.memset(known[:], 0.0))
            for j in range(3):
                step1(dve.memset(pair[:, j, :], (j + 1) << (BITS - 2)))
            with dve.Fori(0, ROUNDS) as i:
                dve.wait_ge(s["srch"], 1 + i)
                dve.wait_ge(s["shf"], 1 + i)
                dve.tensor_tensor(cand[:], known[:].bitcast(I32).unsqueeze(1).broadcast_to((P, 3, E)), pair[:],
                                  ALU.bitwise_or).then_inc(s["cnd"], 1)
                dve.wait_ge(s["cnd"], i + 1)
                dve.tensor_tensor(over[:], gates[:].unsqueeze(1).broadcast_to((P, 3, TILES, E)),
                                  cand[:].bitcast(F32).unsqueeze(2).broadcast_to((P, 3, TILES, E)),
                                  ALU.is_ge).then_inc(s["cmpd"], 1)
                dve.tensor_scalar(pair[:], pair[:], 2, None, ALU.logical_shift_right).then_inc(s["shf"], 1)
                dve.wait_ge(s["cnt"], i + 1)
                dve.tensor_reduce(tally3[:], psum[:, 7, 0:3 * P].rearrange("p (j t e) -> p j e t", j=3, e=E), AX.X,
                                  ALU.add).then_inc(s["cns"], 1)
                dve.wait_ge(s["cns"], i + 1)
                dve.scalar_tensor_tensor(out=trial[:], in0=tally3[:], scalar=float(CHOSEN), in1=cand[:].bitcast(F32),
                                         op0=ALU.is_ge, op1=ALU.mult).then_inc(s["eno"], 1)
                dve.wait_ge(s["eno"], i + 1)
                dve.tensor_reduce(best[:], trial[:].rearrange("p j e -> p e j"), AX.X, ALU.max).then_inc(s["best"], 1)
                dve.wait_ge(s["best"], i + 1)
                dve.tensor_tensor(known[:], known[:], best[:], ALU.max).then_inc(s["srch"], 1)
            dve.wait_ge(s["srch"], 1 + ROUNDS)
            least = known[:].unsqueeze(1).broadcast_to((P, TILES, E))
            step1(dve.tensor_tensor(above[:], gates[:], least, ALU.is_gt))
            step1(dve.tensor_tensor(ties[:], gates[:], least, ALU.is_equal))
            dve.wait_ge(s["cnt"], ROUNDS + 1)
            step1(dve.tensor_reduce(tally[:], psum[:, 7, 0:P].rearrange("p (t e) -> p e t", e=E), AX.X, ALU.add))
            step1(dve.tensor_scalar(tally[:], tally[:], -1.0, float(CHOSEN), ALU.mult, ALU.add))

            def step(ins):
                step1(ins)

            def running1(n):
                dve.wait_ge(s["rt_pe"], n)
                step1(dve.tensor_copy(totals1[:], psum[:, 6, 0:P].rearrange("p (t e) -> p t e", e=E)))
                step1(dve.tensor_copy(scan1[0][:], totals1[:]))
                src, shift = 0, 1
                while shift < TILES:
                    a, o = scan1[src], scan1[1 - src]
                    dve.tensor_copy(o[:, 0:shift], a[:, 0:shift]).then_inc(s["r1"], 1)
                    r1[0] += 1
                    step1(dve.tensor_tensor(o[:, shift:], a[:, shift:], a[:, 0:TILES - shift], ALU.add))
                    src, shift = 1 - src, shift * 2
                free = scan1[1 - src]
                step1(dve.tensor_tensor(free[:], scan1[src][:], totals1[:], ALU.subtract))
                step1(dve.tensor_tensor(free[:], psum[:, 5, 0:P].rearrange("p (t e) -> p t e", e=E), free[:], ALU.add))
                return free

            earlier = running1(2)
            step1(dve.tensor_tensor(chosen[:], earlier[:], tally[:].unsqueeze(1).broadcast_to((P, TILES, E)), ALU.is_lt))
            step1(dve.tensor_tensor(chosen[:], chosen[:], ties[:], ALU.mult))
            step1(dve.tensor_tensor(chosen[:], chosen[:], above[:], ALU.add))
            assert r1[0] == R1_CHOSEN
            earlier = running1(3)
            step1(dve.tensor_copy(place_i[:], earlier[:]))
            step1(dve.tensor_scalar(row_i[:], place_i[:], P - 1, None, ALU.bitwise_and))
            step1(dve.tensor_scalar(place_i[:], place_i[:], 7, None, ALU.logical_shift_right))
            step1(dve.tensor_copy(row_f[:], row_i[:]))
            step1(dve.tensor_copy(tile_f[:], place_i[:]))
            step1(dve.scalar_tensor_tensor(out=row_f[:], in0=row_f[:], scalar=1.0, in1=chosen[:], op0=ALU.add, op1=ALU.mult))
            step1(dve.tensor_scalar(row_f[:], row_f[:], -1.0, None, ALU.add))
            te = (P, TILES * E, CT)
            put_2d = put_f[:].rearrange("p t e c -> p (t e) c")
            step1(dve.tensor_tensor(put_2d, tile_f[:].rearrange("p t e -> p (t e)").unsqueeze(2).broadcast_to(te),
                                    columns[:, 0:CT].unsqueeze(1).broadcast_to(te), ALU.is_equal))
            step1(dve.tensor_scalar(put[:, :, :, 1, :].rearrange("p t e c -> p (t e) c"), put_2d, lane[:], None, ALU.mult))
            step1(dve.tensor_tensor(put[:, :, :, 0, :], put_f[:].rearrange("p t e c -> p t (e c)").rearrange("p t (e c) -> p t e c", e=E),
                                    tile_no[:].unsqueeze(2).unsqueeze(3).broadcast_to((P, TILES, E, CT)), ALU.mult))
            for t in range(TILES):
                if t >= 2:
                    dve.wait_ge(s["hot_pe"], t - 1)
                dve.tensor_tensor(hot[:, t % 2], columns[:].unsqueeze(1).broadcast_to((P, E, P)),
                                  row_f[:, t, :].unsqueeze(2).broadcast_to((P, E, P)), ALU.is_equal).then_inc(s["hots"], 1)
            dve.wait_ge(s["hot_pe"], TILES)
            dve.tensor_copy(found[:], psum[:, :, 0:2 * CT]).then_inc(s["found_s"], 1)
            dve.wait_ge(s["found_s"], 1)
            dve.scalar_tensor_tensor(out=tokens[:], in0=found[:, :, 0:CT], scalar=float(P), in1=found[:, :, CT:],
                                     op0=ALU.mult, op1=ALU.add).then_inc(s["found_s"], 1)

            def rows_low(n):
                for t in range(CT):
                    cols = slice(t * P, (t + 1) * P)
                    dve.wait_ge(s["xe_hs"], n * CT + t + 1)
                    dve.tensor_tensor(xe_l[:, :, cols], psum[:, 6 + t % 2, 0:D].rearrange("p (k c) -> p k c", k=KC),
                                      xe_h[:, :, cols].bitcast(F32), ALU.subtract).then_inc(s["xe_ls"], 1)

            def weights_low(w, side, c):
                cols = slice(c * CUT, (c + 1) * CUT)
                dve.wait_ge(s["vs_hs"], w * CUTS + c + 1)
                dve.tensor_tensor(v_l[side][:, cols], v_raw[:, cols], v_h[side][:, cols].bitcast(F32), ALU.subtract).then_inc(s["vs_ls"], 1)

            def expert1(e, side, last):
                dve.tensor_copy(gval[:, side, :], gathered[side][:, :, ds(D + e, 1)].rearrange("p t o -> p (t o)")).then_inc(s["gval_s"], 1)
                for f in range(FT1):
                    dve.wait_ge(s["gl_s"], e * FT1 + f + 1)
                    dve.tensor_copy(g_h[:, f, :], gl[:, f % 2, :]).then_inc(s["gh_s"], 1)
                    dve.wait_ge(s["gh_s"], e * FT1 + f + 1)
                    dve.tensor_tensor(g_l[:, f, :], gl[:, f % 2, :], g_h[:, f, :].bitcast(F32), ALU.subtract).then_inc(s["gls"], 1)
                    if not last and f % 4 == 3:
                        weights_low(e + 1, 1 - side, f // 4)
                if not last:
                    rows_low(e + 1)
                    for c in range(2, CUTS):
                        weights_low(e + 1, 1 - side, c)
                dve.wait_ge(s["sadd"], 16 + e * (CT * 16))
                dve.wait_ge(s["gval_s"], e + 1)
                for t in range(CT):
                    dve.wait_ge(s["yb1"], 1 + e * CT + t + 1)
                    dve.tensor_tensor(ye1[:, t, :], psum[:, 2 + t, 0:D], b2[:, ds(e, 1), :].rearrange("p o d -> p (o d)"),
                                      ALU.add).then_inc(s["y1e"], 1)
                for t in range(CT):
                    dve.wait_ge(s["y1e"], 1 + e * CT + t + 1)
                    dve.tensor_scalar(ye1[:, t, :], ye1[:, t, :], gval[:, side, t:t + 1], None, ALU.mult).then_inc(s["ys1"], 1)

            rows_low(0)
            dve.wait_ge(s["b_in"], 32)
            with dve.Fori(0, E // 2 - 1) as p:
                for side in range(2):
                    expert1(2 * p + side, side, False)
            expert1(E - 2, 0, False)
            expert1(E - 1, 1, True)

        @block.tensor
        def _(pe):
            def products(o, pairs):
                for n, (l, r) in enumerate(pairs):
                    last = pe.matmul(o, l, r, start=n == 0, stop=n == len(pairs) - 1)
                return last

            pe.wait_ge(s["ident1"], 1)
            pe.wait_ge(s["c_dve"], 3)
            for k in range(KX):
                last = pe.transpose(psum[0:PX, 0, k * P:(k + 1) * P], xcn[:, k * PX:(k + 1) * PX], ident[:])
            last.then_inc(s["c_pe"], 1)
            pe.wait_ge(s["mask_s"], 4)
            pe.wait_ge(s["c_act"], 1)
            pe.wait_ge(s["wsp_l"], 3)
            products(psum[:, 1, :], [(l[:, k, :], r[:, k, :]) for k in range(KX)
                                     for l, r in ((ch, wkvx_h), (ch, wkvx_l), (cl, wkvx_h))]).then_inc(s["c_pe"], 1)
            pe.wait_ge(s["identr"], 1)
            pe.wait_ge(s["c_dve"], 10)
            for r in range(2):
                for h in range(H):
                    last = pe.transpose(psum[:, 2 + r, h * P:(h + 1) * P].bitcast(F32R), cparts[:, r * H + h, :], ident_r[:])
                last.then_inc(s["c_pe"], 1)

            with pe.Fori(0, B) as b:
                with pe.Fori(0, GPB) as gg:
                    g = b * GPB + gg
                    pe.wait_ge(s["ev_a"], 1 + g * 6)
                    pe.wait_ge(s["ev_d"], 1 + g * 6)
                    for bank in range(2):
                        pe.wait_ge(s[f"ring{bank}"], 1 + b * (GPB * RING[bank]))
                    for t in range(GT):
                        pe.wait_ge(s["xt_s"], g * GT + t + 1)
                        for k in range(KC):
                            last = pe.transpose(psum[:, 4 + t, k * P:(k + 1) * P], xt[:, t, k * P:(k + 1) * P], ident[:])
                        last.then_inc(s["tp"], 1)
                    for t in range(GT):
                        pe.wait_ge(s["lnl_s"], g * GT + t + 1)
                        if t >= 2:
                            pe.wait_ge(s["raw_s"], g * GT + t - 1)
                        z = 2 * (t % 2)
                        for bank, lo, hi in ((z, 0, 2 * D), (z + 1, 2 * D, 3 * D)):
                            last = products(psum[:, bank, 0:hi - lo],
                                            [(l[:, t, k, :], r[:, k, lo:hi]) for k in range(KC)
                                             for l, r in ((lnh, wqkv_h), (lnh, wqkv_l), (lnl, wqkv_h))])
                        last.then_inc(s["qkv_s"], 1)
                    for t in range(GT):
                        pe.wait_ge(s["hi_s"], (g * GT + t + 1) * 2)
                        pe.wait_ge(s["lo_s"], (g * GT + t + 1) * 2)
                        for c in range(3):
                            n = 3 * t + c
                            if n >= 2:
                                pe.wait_ge(s["ev_d"] if n % 2 else s["ev_a"], 1 + g * 6 + n // 2)
                            for h in range(H):
                                last = pe.transpose(psum[:, 6 + n % 2, h * P:(h + 1) * P].bitcast(F32R),
                                                    parts[:, t % 2, c * H + h, :], ident_r[:])
                            last.then_inc(s["t12"], 1)
                with pe.Fori(0, GPB) as gg:
                    g = b * GPB + gg
                    pe.wait_ge(s["qs_s"], g * 2 + 2)
                    pe.wait_ge(s["ev_a"], 1 + (b + 1) * (GPB * 6))
                    pe.wait_ge(s["ev_d"], 1 + (b + 1) * (GPB * 6))

                    def scores(u):
                        if u >= 2:
                            pe.wait_ge(s["exp_s"], g * UNITS + u - 1)
                        h, t = divmod(u, GT)
                        q = qs[:, h, t * P:(t + 1) * P]
                        z = 3 * (u % 2)
                        for c in range(3):
                            lo, hi = c * PIECE, (c + 1) * PIECE
                            pairs = [(q, kT[:, h, 0, lo:hi]), (q, kT[:, h, 1, lo:hi])]
                            if hi == KEYS:
                                pairs.insert(0, (first_row[:], mask_rows[:, ds(b, 1), :].rearrange("p o k -> p (o k)")))
                            last = products(psum[:, z + c, 0:hi - lo], pairs)
                        last.then_inc(s["sc_s"], 1)

                    def ring_bank(*use):
                        bank, before = USES[use]
                        pe.wait_ge(s[f"ring{bank}"], 1 + g * RING[bank] + before)
                        return 6 + bank

                    def transposes(u, c):
                        pe.wait_ge(s["exp_s"], g * UNITS + u + 1)
                        bank = ring_bank("chunk", u, c)
                        n = min(4, KT - 4 * c)
                        for k in range(n):
                            last = pe.transpose(psum[:, bank, k * P:(k + 1) * P],
                                                prob[:, u % 3, (4 * c + k) * P:(4 * c + k + 1) * P], ident[:])
                        last.then_inc(s["pt_s"], 1)

                    def repeat_reciprocals(h):
                        pe.wait_ge(s["rc_s"], g * UNITS + (h + 1) * GT)
                        bank = ring_bank("reciprocals", h)
                        for t in range(GT):
                            last = pe.matmul(psum[:, bank, t * P:(t + 1) * P],
                                             rdenom[:, h * GT + t:h * GT + t + 1].broadcast_to((P, P)), ident[:],
                                             start=True, stop=True)
                        last.then_inc(s["sr_s"], 1)

                    def values(h, c):
                        if h == 0 and c == 0:
                            pe.wait_ge(s["vl_s"], (b + 1) * (GPB * GT))
                        bank = ring_bank("result", h) if c == 0 else 6 + USES["result", h][0]
                        chunk_bank, before = USES["chunk", h * GT + GT - 1, c]
                        pe.wait_ge(s[f"ring{chunk_bank}"], 1 + g * RING[chunk_bank] + before + 1)
                        for k in range(4 * c, min(4 * c + 4, KT)):
                            for part in (pT_h, pT_l):
                                last = pe.matmul(psum[:, bank, :], v[:, k, h, :], part[:, k, :],
                                                 start=k == 0 and part is pT_h, stop=k == KT - 1 and part is pT_l)
                        if c == 2:
                            last.then_inc(s["o_s"], 1)

                    scores(0)
                    scores(1)
                    for u in range(UNITS):
                        for c in range(3):
                            if u % GT == 0 and u:
                                values(u // GT - 1, c)
                            if c == 2 and u + 2 < UNITS:
                                scores(u + 2)
                            transposes(u, c)
                        if u % GT == GT - 1:
                            repeat_reciprocals(u // GT)
                    for c in range(3):
                        values(H - 1, c)
                    for t in range(GT):
                        bank = ring_bank("output", t)
                        if t == 0:
                            pe.wait_ge(s["ol_s"], (g + 1) * H)
                        cols = slice(t * P, (t + 1) * P)
                        products(psum[:, bank, 0:D], [(o[:, h, cols], w[:, h, :]) for h in range(H)
                                                      for o, w in ((oT_h, wo_h), (oT_h, wo_l), (oT_l, wo_h))]
                                 ).then_inc(s["y_s"], 1)

            def gate_logits(layer, xs0, xnT, gate_w):
                pe.wait_ge(s["gw_in"], 16 * (layer + 1))
                with pe.Fori(0, GROUPS) as g0:
                    g = g0 + layer * GROUPS
                    for t in range(GT):
                        pe.wait_ge(s["xs0_s"], g * GT + t + 1)
                        for k in range(KC):
                            last = pe.transpose(psum[:, t, k * P:(k + 1) * P], xs0[:, t, k * P:(k + 1) * P], ident[:])
                        last.then_inc(s["tp0"], 1)
                    pe.wait_ge(s["lgc"], 1 + g)
                    for t in range(GT):
                        pe.wait_ge(s["xnT_s"], g * GT + t + 1)
                        products(psum[:, 4, t * E:(t + 1) * E], [(xnT[:, t, k, :], gate_w[:, k, :]) for k in range(KC)]
                                 ).then_inc(s["lg_s"], 1)

            def count_before(flags, before, ones):
                f = flags[:].rearrange("p t e -> p (t e)")
                pe.matmul(psum[:, 5, 0:P], before[:], f, start=True, stop=True)
                pe.matmul(psum[:, 6, 0:P], ones[:], f, start=True, stop=True).then_inc(s["rt_pe"], 1)

            gate_logits(0, xs0, xnT, gate_w)
            pe.wait_ge(s["lgc"], 1 + GROUPS)
            pe.wait_ge(s["rt"], RT_PICKED)
            count_before(both, before, ones)

            def x_transposed(n):
                pe.wait_ge(s["xbi"], (n + 1) * 16)
                for k in range(KC):
                    last = pe.transpose(psum[:, 4, k * P:(k + 1) * P], xb[:, k * P:(k + 1) * P], ident[:])
                last.then_inc(s["tx"], 1)

            def block(n, side):
                wh, wl = w_h[side], w_l[side]
                pe.wait_ge(s["xl_s"], n + 1)
                for c, (lo, hi) in enumerate(((0, FA), (FA, F))):
                    pe.wait_ge(s["h_s"], 1 + n * 2)
                    for up in range(2):
                        cols = [slice((up * KC + k) * F + lo, (up * KC + k) * F + hi) for k in range(KC)]
                        products(psum[:, 2 * c + up, 0:hi - lo],
                                 [(a[:, k, :], w[:, cols[k]]) for k in range(KC)
                                  for a, w in ((xbT_h, wh), (xbT_h, wl), (xbT_l, wh))]).then_inc(s["gu"], 1)
                x_transposed(n + 1)
                for c in range(2):
                    pe.wait_ge(s["h_s"], 1 + n * 2 + c + 1)
                    for k in range(3):
                        last = pe.transpose(psum[:, 5 + c, k * P:(k + 1) * P], hid[:, (3 * c + k) * P:(3 * c + k + 1) * P], ident[:])
                    last.then_inc(s["th"], 1)
                pe.wait_ge(s["ye"], 1 + n)
                down = 2 * KC * F
                for c in range(2):
                    pe.wait_ge(s["hl_s"], n * 2 + c + 1)
                    for k in range(3 * c, 3 * c + 3):
                        for m, (a, w) in enumerate(((hT_h, wh), (hT_h, wl), (hT_l, wh))):
                            last = pe.matmul(psum[:, 7, 0:D], a[:, k, :], w[:, down + k * D:down + (k + 1) * D],
                                             start=k == 0 and m == 0, stop=k == FT - 1 and m == 2)
                last.then_inc(s["yo"], 1)

            pe.wait_ge(s["rt"], RT_PADDED)
            x_transposed(0)
            pe.wait_ge(s["ws_l"], 1)
            with pe.Fori(0, SHARED) as n:
                block(n, 0)
            with pe.Fori(0, E // 2) as p:
                for side in (1, 0):
                    w = 2 * p + (1 if side else 2)
                    first = pe.value_load(table[0:1, 0, ds(w, 1)], min_val=0, max_val=ROUTED - 2)
                    count = pe.value_load(table[0:1, 1, ds(w, 1)], min_val=1, max_val=TILES)
                    pe.wait_ge(s["ws_l"], w + 1)
                    pe.sem_inc(s["met"], 1)
                    with pe.Fori(0, count) as i:
                        n = pe.snap(first + i + SHARED)
                        block(n, side)

            pe.wait_ge(s["a1_in"], 64)
            for k in range(KX):
                last = pe.transpose(psum[0:PX, 0, k * P:(k + 1) * P], xc1[:, k * PX:(k + 1) * PX], ident[:])
            last.then_inc(s["c1_pe"], 1)
            pe.wait_ge(s["a1_l"], 2)
            pe.wait_ge(s["c1_dve"], 1)
            pe.wait_ge(s["c1_act"], 5)
            for k in range(KC):
                cols = slice(k * P, (k + 1) * P)
                last = products(psum[:, 1, cols], [(w[:, 0, c, cols], a[:, c, :]) for c in range(KX)
                                                   for w, a in ((c_h, cT_h), (c_h, cT_l), (c_l, cT_h))])
            last.then_inc(s["c1_pe"], 1)
            for b in range(B):
                last = products(psum[:, 2, b * D:(b + 1) * D],
                                [(a[:, c, b].rearrange("p r c -> p (r c)"), w[:, 1, c, :]) for c in range(KX)
                                 for w, a in ((c_h, cd_h), (c_h, cd_l), (c_l, cd_h))])
            last.then_inc(s["c1_pe"], 1)
            pe.wait_ge(s["c1_dve"], 1 + 4 * KC)
            pe.wait_ge(s["c1_act"], 5 + 4 * KC)
            with pe.Fori(0, B) as b:
                with pe.Fori(0, GPB) as gg:
                    g = b * GPB + gg
                    for t in range(GT):
                        pe.wait_ge(s["xs1_s"], g * GT + t + 1)
                        for k in range(KC):
                            last = pe.transpose(psum[:, t, k * P:(k + 1) * P], xs1[:, t, k * P:(k + 1) * P], ident[:])
                        last.then_inc(s["tp1"], 1)
                    pe.wait_ge(s["x1l"], (g + 1) * GT)
                    pe.wait_ge(s["x1a"], 1 + g * GT)
                    for m in range(KC):
                        cols = slice(m * P, (m + 1) * P)
                        products(psum[:, 4 + m, :], [(w[:, 0, k, cols], a[:, k, :]) for k in range(KC)
                                                     for w, a in ((a_h, x1_h), (a_h, x1_l), (a_l, x1_h))]).then_inc(s["q1"], 1)
                    pe.wait_ge(s["q1l"], (g + 1) * KC)
                    for t in range(GT):
                        cols = slice(t * P, (t + 1) * P)
                        keys = [(a[:, ds(b, 1), k, :].rearrange("p o c -> p (o c)")) for k in range(KC) for a in (kb_h, kb_l)]
                        products(psum[:, t, 0:H * C], [pair for k in range(KC) for pair in
                                                       ((q1_h[:, k, cols], keys[2 * k]), (q1_h[:, k, cols], keys[2 * k + 1]),
                                                        (q1_l[:, k, cols], keys[2 * k]))]).then_inc(s["sc1"], 1)
                    for t in range(GT):
                        pe.wait_ge(s["pn1"], g * GT + t + 1)
                        for k in range(KC):
                            last = pe.transpose(psum[:, 4 + t, k * P:(k + 1) * P], p1[:, t, k * P:(k + 1) * P], ident[:])
                        last.then_inc(s["pt1"], 1)
                    pe.wait_ge(s["vsc"], (g + 1) * 2)
                    pe.wait_ge(s["p1l"], (g + 1) * GT)
                    for k in range(KC):
                        products(psum[:, k, :], [(a[:, k, :], p[:, k, :]) for a, p in
                                                 ((vs_h, p1T_h), (vs_h, p1T_l), (vs_l, p1T_h))]).then_inc(s["o1"], 1)
                    pe.wait_ge(s["o1l"], (g + 1) * KC)
                    for t in range(GT):
                        cols = slice(t * P, (t + 1) * P)
                        products(psum[:, 4 + t, 0:D], [(o[:, k, cols], w[:, 1, k, :]) for k in range(KC)
                                                       for o, w in ((o1_h, a_h), (o1_h, a_l), (o1_l, a_h))]).then_inc(s["y1"], 1)

            pe.wait_ge(s["x1b"], TILES)
            gate_logits(1, xs2, xnT1, gate1_w)
            with pe.Fori(0, ROUNDS) as i:
                pe.wait_ge(s["cmpd"], i + 1)
                pe.matmul(psum[:, 7, 0:3 * P], ones_b[:], over[:].rearrange("p j t e -> p (j t e)"), start=True, stop=True).then_inc(s["cnt"], 1)
            pe.wait_ge(s["r1"], R1_FLAGS)
            pe.matmul(psum[:, 7, 0:P], ones1[:], above[:].rearrange("p t e -> p (t e)"), start=True, stop=True).then_inc(s["cnt"], 1)
            count_before(ties, before1, ones1)
            pe.wait_ge(s["r1"], R1_CHOSEN)
            count_before(chosen, before1, ones1)
            pe.wait_ge(s["hots"], 1)
            for t in range(TILES):
                pe.wait_ge(s["hots"], t + 1)
                for e in range(E):
                    last = pe.matmul(psum[:, e, 0:2 * CT], hot[:, t % 2, e, :], put[:, t, e].rearrange("p v c -> p (v c)"),
                                     start=t == 0, stop=t == TILES - 1)
                last.then_inc(s["hot_pe"], 1)

            def rows_transposed(n, side):
                pe.wait_ge(s[f"ga{side}"], (n // 2 + 1) * (CT * 16))
                for t in range(CT):
                    if t >= 2:
                        pe.wait_ge(s["xe_ls"], n * CT + t - 1)
                    for k in range(KC):
                        last = pe.transpose(psum[:, 6 + t % 2, k * P:(k + 1) * P], gathered[side][:, t, k * P:(k + 1) * P], ident[:])
                    last.then_inc(s["xe_t"], 1)

            def expert1(e, side, last_one):
                wh, wl = v_h[side], v_l[side]
                pe.wait_ge(s["vs_ls"], (e + 1) * CUTS)
                pe.wait_ge(s["xe_ls"], (e + 1) * CT)
                for f in range(FT1):
                    if f >= 2:
                        pe.wait_ge(s["gl_s"], e * FT1 + f - 1)
                    cols = [slice(k * F1 + f * P, k * F1 + (f + 1) * P) for k in range(KC)]
                    products(psum[:, f % 2, :], [(w[:, cols[k]], a[:, k, :]) for k in range(KC)
                                                 for w, a in ((wh, xe_h), (wh, xe_l), (wl, xe_h))]).then_inc(s["h1"], 1)
                if not last_one:
                    rows_transposed(e + 1, 1 - side)
                pe.wait_ge(s["y1e"], 1 + e * CT)
                for f in range(FT1):
                    pe.wait_ge(s["gls"], e * FT1 + f + 1)
                    for t in range(CT):
                        cols = slice(t * P, (t + 1) * P)
                        w2 = slice(W1 + f * D, W1 + (f + 1) * D)
                        for m, (a, w) in enumerate(((g_h, wh), (g_h, wl), (g_l, wh))):
                            last = pe.matmul(psum[:, 2 + t, 0:D], a[:, f, cols], w[:, w2],
                                             start=f == 0 and m == 0, stop=f == FT1 - 1 and m == 2)
                        if f == FT1 - 1:
                            last.then_inc(s["yb1"], 1)

            pe.wait_ge(s["found_s"], 2)
            rows_transposed(0, 0)
            with pe.Fori(0, E // 2 - 1) as p:
                for side in range(2):
                    expert1(2 * p + side, side, False)
            expert1(E - 2, 0, False)
            expert1(E - 1, 1, True)


def kernel(**inputs):
    import concourse.bacc as bacc
    from concourse.bass_utils import run_bass_kernel_spmd

    i = {k: np.asarray(v) for k, v in inputs.items()}

    def chunked(w, n):
        return w.reshape(n, -1, w.shape[-1]).transpose(1, 0, 2)

    def columns(vec, n):
        return vec.reshape(n, -1).T

    def rows_first(w):
        e, r, m = w.shape
        return w.reshape(e, r // P, P, m).transpose(0, 2, 1, 3).reshape(e, P, -1)

    def expert_weights(i):
        gate, up, down = (np.concatenate([i[f"L0_ffn_shared_{n}"][None], i[f"L0_ffn_expert_{n}"]]).transpose(0, 2, 1)
                          for n in ("gate", "up", "down"))
        down = np.pad(down, ((0, 0), (0, FT * P - F), (0, 0)))
        return np.concatenate([rows_first(gate), rows_first(up), rows_first(down)], 2)

    wo = i["L0_xattn_Wo"].T.reshape(H, HD, D)
    arrays = {
        "x": i["x"].reshape(T, D),
        "ctx": i["ctx_768"].reshape(B * C, DC),
        "mask": i["mask_BxS2_bk0"].reshape(1, B * C),
        "lnx_g": columns(i["L0_xattn_ln_x_g"], KX), "lnx_b": columns(i["L0_xattn_ln_x_b"], KX),
        "ln_g": columns(i["L0_xattn_ln_l_g"], KC), "ln_b": columns(i["L0_xattn_ln_l_b"], KC),
        "qk_gain": np.concatenate([i["L0_xattn_qn_g"]] * H + [i["L0_xattn_kn_g"]] * H),
        "bo0": i["L0_xattn_bo"],
        "wkvx": chunked(i["L0_xattn_Wkv"].T, KX),
        "wqkv": chunked(np.concatenate([i["L0_xattn_Wq"].T, i["L0_xattn_Wlkv"].T], 1), KC),
        "gate1": chunked(i["L1_ffn_Wg"], KC),
        "wkv1": np.stack([chunked(i["L1_xattn_Wk"].T, KX), chunked(i["L1_xattn_Wv"].T, KX)], 1),
        "wqo1": np.stack([chunked(i["L1_xattn_Wq"].T, KC), chunked(i["L1_xattn_Wo"].T, KC)], 1),
        "bo1": i["L1_xattn_bo"],
        "b1": i["L1_ffn_b1"].reshape(E, FT1, P).transpose(2, 0, 1).reshape(P, E * FT1),
        "b2": i["L1_ffn_b2"].reshape(E * D),
        "experts1": np.concatenate([rows_first(i["L1_ffn_W1"]), rows_first(i["L1_ffn_W2"])], 2),
        "gate0": chunked(i["L0_ffn_gate_w"].T, KC),
        "experts0": expert_weights(i),
        "wo0": np.concatenate([wo, wo], 1).transpose(1, 0, 2),
    }
    arrays = {k: np.ascontiguousarray(a) for k, a in arrays.items()}
    nc = bacc.Bacc("TRN2", target_bir_lowering=False, num_devices=1)
    ap = {k: nc.dram_tensor("in_" + k, a.shape, mybir.dt.from_np(a.dtype), kind="ExternalInput").ap() for k, a in arrays.items()}
    out = nc.dram_tensor("y", (T, D), F32, kind="ExternalOutput").ap()
    build(nc, ap, out)
    r = run_bass_kernel_spmd(nc, [{"in_" + k: a for k, a in arrays.items()}], core_ids=[0])
    return r.results[0]["y"].reshape(B, S, D)
```

```python
from contextlib import ExitStack

import numpy as np

import concourse.bass as bass
from concourse import mybir

ALU = mybir.AluOpType
ACT = mybir.ActivationFunctionType
AX = mybir.AxisListType
F32 = mybir.dt.float32
F32R = mybir.dt.float32r
BF16 = mybir.dt.bfloat16
I32 = mybir.dt.int32
U32 = mybir.dt.uint32
U8 = mybir.dt.uint8
ds = bass.ds

P = 128
B = 2
S = 1024
T = B * S
TILES = T // P
GT = 4
GROUPS = TILES // GT
GPB = GROUPS // B
D = 256
KC = D // P
C = 64
DC = 192
KX = 2
PX = DC // KX
H = 4
HD = 64
KT = S // P + 1
KEYS = KT * P
CTX0 = S
CK = KT // 3
PIECE = CK * P
BIG = 1.0e30
LN_EPS = 1e-5
RMS_EPS = 1e-8
RT_SHIFTED, RT_PICKED, RT_PADDED = 2, 17, 58
R1_GATES, R1_FLAGS, R1_CHOSEN = 2, 8, 25
UNITS = H * GT
PAIRS = UNITS // 2
E = 8
F = 704
FA = 384
FB = F - FA
FT = 6
FW = 2 * KC * F + FT * D
WCUTS = 4
WCUT = FW // WCUTS
SHARED = TILES
LEAST = 2
ROUTED = 2 * T // P + LEAST * E
CHOSEN = T * 2 // E
CT = CHOSEN // P
F1 = 1024
FT1 = F1 // P
W1 = KC * F1
FW1 = W1 + FT1 * D
CUTS = 4
CUT = FW1 // CUTS
BITS = 30
ROUNDS = BITS // 2
XG = D + E
COUNT_FROM_ONE = "tx yst ys1 srch ev_d ev_a ring0 ring1 h_s ye x1a y1e yb1 shf".split()


def ring_uses():
    uses, before = {}, [0, 0]
    order = []
    for u in range(UNITS):
        order += [("chunk", u, c) for c in range(3)]
        if u % 2 == 0 and u:
            order.append(("result", u // 2 - 1))
        if u % 2:
            order.append(("reciprocals", u // 2))
    order += [("result", PAIRS - 1)] + [("output", t) for t in range(GT)]
    for n, use in enumerate(order):
        uses[use] = n % 2, before[n % 2]
        before[n % 2] += 1
    return uses, before


USES, RING = ring_uses()


def build(nc, ap, out):
    ctx = ExitStack()
    with ctx:
        def sb(name, shape, dt=F32, scope=ctx):
            return scope.enter_context(nc.sbuf_tensor(name, shape, dt))

        def sem(name):
            return ctx.enter_context(nc.semaphore(name))

        psum = ctx.enter_context(nc.psum_tensor("psum", [P, 8, 512], F32))

        x = sb("x", [P, TILES, D])
        xn = sb("xn", [P, TILES, D])
        ident = sb("ident", [P, P])
        ident_r = sb("ident_r", [P, P], F32R)
        neg_half = sb("neg_half", [P, 4 * H * GT * 2])
        zeros = sb("zeros", [P, D])
        stat = sb("stat", [P, TILES, 6])
        mean_var = sb("mean_var", [P, TILES, 2])
        rstd = sb("rstd", [P, TILES])

        own = [sb(f"own{i}", [P, CT], U32) for i in range(2)]
        tokens = sb("tokens", [P, E, CT], U32)

        att = ExitStack()
        kT = sb("kT", [P, H, 2, KEYS], F32R, att)
        v = sb("v", [P, KT, H, P], F32R, att)
        qT = sb("qT", [P, H, S], F32R, att)
        wqkv_h = sb("wqkv_h", [P, KC, 3 * D], F32R, att)
        wqkv_l = sb("wqkv_l", [P, KC, 3 * D], F32R, att)
        wo_h = sb("wo_h", [P, H, D], F32R, att)
        wo_l = sb("wo_l", [P, H, D], F32R, att)
        qk_gain = sb("qk_gain", [P, 2 * D], F32, att)
        bo = sb("bo", [P, D], F32, att)
        ln_g = sb("ln_g", [P, KC], F32, att)
        ln_b = sb("ln_b", [P, KC], F32, att)
        mask_rows = sb("mask_rows", [P, B, PIECE], BF16, att)
        first_row = sb("first_row", [P, P], BF16, att)
        prj = ExitStack()
        xt = sb("xt", [P, GT, D], F32, prj)
        lnf = sb("lnf", [P, GT, KC, P], F32, prj)
        lnh = sb("lnh", [P, GT, KC, P], F32R, prj)
        lnl = sb("lnl", [P, GT, KC, P], F32R, prj)
        qkv = sb("qkv", [P, GT, 3 * D], F32, prj)
        sq = sb("sq", [P, 2, 2 * D], F32, prj)
        ssq = sb("ssq", [P, GT, 2 * H], F32, prj)
        rms = sb("rms", [P, GT, 2 * H], F32, prj)
        parts = sb("parts", [P, 2, 3 * H, P], F32R, prj)
        prj.close()
        raw = ExitStack()
        wqkv = sb("wqkv", [P, KC, 3 * D], F32, raw)
        wkvx = sb("wkvx", [PX, KX, 2 * D], F32, raw)
        wkvx_h = sb("wkvx_h", [PX, KX, 2 * D], F32R, raw)
        wkvx_l = sb("wkvx_l", [PX, KX, 2 * D], F32R, raw)
        wo = sb("wo", [P, H, D], F32, raw)
        xc = sb("xc", [P, DC], F32, raw)
        xcn = sb("xcn", [P, DC], F32, raw)
        cf = sb("cf", [PX, KX, P], F32, raw)
        ch = sb("ch", [PX, KX, P], F32R, raw)
        cl = sb("cl", [PX, KX, P], F32R, raw)
        lnx_g = sb("lnx_g", [PX, KX], F32, raw)
        lnx_b = sb("lnx_b", [PX, KX], F32, raw)
        ckv = sb("ckv", [P, 2 * D], F32, raw)
        csq = sb("csq", [P, D], F32, raw)
        cstat = sb("cstat", [P, 6], F32, raw)
        cmv = sb("cmv", [P, 2], F32, raw)
        crs = sb("crs", [P, 1], F32, raw)
        cms = sb("cms", [P, H], F32, raw)
        cparts = sb("cparts", [P, 2 * H, P], F32R, raw)
        mask_u8 = sb("mask_u8", [1, B * C], U8, raw)
        mask_f = sb("mask_f", [1, B * C], F32, raw)
        raw.close()
        act_ = ExitStack()
        qs = sb("qs", [P, H, GT * P], F32R, act_)
        prob = sb("prob", [P, 3, KEYS], F32, act_)
        pT_h = sb("pT_h", [P, KT, GT * P], F32R, act_)
        pT_l = sb("pT_l", [P, KT, GT * P], F32R, act_)
        rep_rd = sb("rep_rd", [P, 2, 2 * P], F32, act_)
        oT = sb("oT", [P, 2, 2 * P], F32, act_)
        oT_h = sb("oT_h", [P, H, GT * P], F32R, act_)
        oT_l = sb("oT_l", [P, H, GT * P], F32R, act_)
        neg_max = sb("neg_max", [P, UNITS], F32, act_)
        denom = sb("denom", [P, UNITS], F32, act_)
        rdenom = sb("rdenom", [P, UNITS], F32, act_)
        act_.close()
        att.close()

        cmb = ExitStack()
        weight = [sb(f"weight{i}", [P, TILES], F32, cmb) for i in range(2)]
        table = sb("table", [P, 3, E + 2], I32, cmb)
        slot = [sb(f"slot{i}", [P, TILES], U32, cmb) for i in range(2)]
        y_got = sb("y_got", [P, 8, D], F32, cmb)
        moe = ExitStack()
        w_raw = sb("w_raw", [P, FW], F32, moe)
        w_h = [sb(f"w_h{i}", [P, FW], F32R, moe) for i in range(2)]
        w_l = [sb(f"w_l{i}", [P, FW], F32R, moe) for i in range(2)]
        xT_h = sb("xT_h", [P, KC, T], F32R, moe)
        xT_l = sb("xT_l", [P, KC, T], F32R, moe)
        logitT = sb("logitT", [E, T], F32, moe)
        gate_h = sb("gate_h", [P, KC, E], F32R, moe)
        gate_l = sb("gate_l", [P, KC, E], F32R, moe)
        gate_w = sb("gate_w", [P, KC, E], F32, moe)
        xb = sb("xb", [P, D], F32, moe)
        xbT_h = sb("xbT_h", [P, KC, P], F32R, moe)
        xbT_l = sb("xbT_l", [P, KC, P], F32R, moe)
        silu = sb("silu", [P, F], F32, moe)
        hid = sb("hid", [P, FT * P], F32, moe)
        hT_h = sb("hT_h", [P, FT, P], F32R, moe)
        hT_l = sb("hT_l", [P, FT, P], F32R, moe)
        y_sb = sb("y_sb", [P, D], F32, moe)
        logit = sb("logit", [P, TILES, E], F32, moe)
        mx = sb("mx", [P, TILES], F32, moe)
        rsum = sb("rsum", [P, TILES], F32, moe)
        eq = sb("eq", [P, TILES, E], F32, moe)
        pick = [sb(f"pick{i}", [P, TILES, E], F32, moe) for i in range(2)]
        both = sb("both", [P, TILES, E], F32, moe)
        scan = [sb(f"scan{i}", [P, TILES, E], F32, moe) for i in range(2)]
        totals = sb("totals", [P, TILES, E], F32, moe)
        blocks = sb("blocks", [P, E], F32, moe)
        blocks_i = sb("blocks_i", [P, E], I32, moe)
        starts = [sb(f"starts{i}", [P, E + 1], F32, moe) for i in range(2)]
        slot_f = sb("slot_f", [P, TILES], F32, moe)
        before = sb("before", [P, P], F32, moe)
        ones = sb("ones", [P, P], F32, moe)
        favour = sb("favour", [P, TILES, E], F32, moe)
        moe.close()

        at1 = ExitStack()
        a_raw = sb("a_raw", [P, 2, KC, D], F32, at1)
        a_h = sb("a_h", [P, 2, KC, D], F32R, at1)
        a_l = sb("a_l", [P, 2, KC, D], F32R, at1)
        c_raw = sb("c_raw", [PX, 2, KX, D], F32, at1)
        c_h = sb("c_h", [PX, 2, KX, D], F32R, at1)
        c_l = sb("c_l", [PX, 2, KX, D], F32R, at1)
        bo1 = sb("bo1", [P, D], F32, at1)
        xc1 = sb("xc1", [P, DC], F32, at1)
        cT_h = sb("cT_h", [PX, KX, P], F32R, at1)
        cT_l = sb("cT_l", [PX, KX, P], F32R, at1)
        cd_h = sb("cd_h", [PX, KX, B, 2, C], F32R, at1)
        cd_l = sb("cd_l", [PX, KX, B, 2, C], F32R, at1)
        kb_h = sb("kb_h", [P, B, KC, H * C], F32R, at1)
        kb_l = sb("kb_l", [P, B, KC, H * C], F32R, at1)
        vb_h = sb("vb_h", [P, B, KC, P], F32R, at1)
        vb_l = sb("vb_l", [P, B, KC, P], F32R, at1)
        xs1 = sb("xs1", [P, GT, D], F32, at1)
        x1_h = sb("x1_h", [P, KC, GT * P], F32R, at1)
        x1_l = sb("x1_l", [P, KC, GT * P], F32R, at1)
        q1_h = sb("q1_h", [P, KC, GT * P], F32R, at1)
        q1_l = sb("q1_l", [P, KC, GT * P], F32R, at1)
        p1 = sb("p1", [P, GT, H * C], F32, at1)
        m1 = sb("m1", [P, GT, H], F32, at1)
        d1 = sb("d1", [P, GT, H], F32, at1)
        p1T_h = sb("p1T_h", [P, KC, GT * P], F32R, at1)
        p1T_l = sb("p1T_l", [P, KC, GT * P], F32R, at1)
        o1_h = sb("o1_h", [P, KC, GT * P], F32R, at1)
        o1_l = sb("o1_l", [P, KC, GT * P], F32R, at1)
        at1.close()
        cmb.close()

        ff1 = ExitStack()
        v_raw = sb("v_raw", [P, FW1], F32, ff1)
        v_h = [sb(f"v_h{i}", [P, FW1], F32R, ff1) for i in range(2)]
        v_l = [sb(f"v_l{i}", [P, FW1], F32R, ff1) for i in range(2)]
        b1 = sb("b1", [P, E * FT1], F32, ff1)
        b2 = sb("b2", [P, E, D], F32, ff1)
        cho = ExitStack()
        gate1_w = sb("gate1_w", [P, KC, E], F32, cho)
        x2T_h = sb("x2T_h", [P, KC, 2 * GT * P], F32R, cho)
        x2T_l = sb("x2T_l", [P, KC, 2 * GT * P], F32R, cho)
        logit1T = sb("logit1T", [E, T], F32, cho)
        gate1_h = sb("gate1_h", [P, KC, E], F32R, cho)
        gate1_l = sb("gate1_l", [P, KC, E], F32R, cho)
        gates = sb("gates", [P, TILES, E], F32, cho)
        known = sb("known", [P, E], F32, cho)
        trial = sb("trial", [P, 3, E], F32, cho)
        best = sb("best", [P, E], F32, cho)
        cand = sb("cand", [P, 3, E], I32, cho)
        pair = sb("pair", [P, 3, E], I32, cho)
        over = sb("over", [P, 3, TILES, E], BF16, cho)
        tally3 = sb("tally3", [P, 3, E], F32, cho)
        ones_b = sb("ones_b", [P, P], BF16, cho)
        tally = sb("tally", [P, E], F32, cho)
        above = sb("above", [P, TILES, E], F32, cho)
        ties = sb("ties", [P, TILES, E], F32, cho)
        chosen = sb("chosen", [P, TILES, E], F32, cho)
        scan1 = [sb(f"scan1{i}", [P, TILES, E], F32, cho) for i in range(2)]
        totals1 = sb("totals1", [P, TILES, E], F32, cho)
        place_i = sb("place_i", [P, TILES, E], I32, cho)
        row_i = sb("row_i", [P, TILES, E], I32, cho)
        row_f = sb("row_f", [P, TILES, E], F32, cho)
        tile_f = sb("tile_f", [P, TILES, E], F32, cho)
        before1 = sb("before1", [P, P], F32, cho)
        ones1 = sb("ones1", [P, P], F32, cho)
        columns = sb("columns", [P, P], F32, cho)
        lane = sb("lane", [P, 1], F32, cho)
        tile_no = sb("tile_no", [P, TILES], F32, cho)
        hot = sb("hot", [P, 2, E, P], BF16, cho)
        put = sb("put", [P, TILES, E, 2, CT], BF16, cho)
        put_f = sb("put_f", [P, TILES, E, CT], F32, cho)
        found = sb("found", [P, E, 2 * CT], F32, cho)
        cho.close()
        wrk = ExitStack()
        gathered = [sb(f"gathered{i}", [P, CT, XG], F32, wrk) for i in range(2)]
        xe_h = sb("xe_h", [P, KC, CHOSEN], F32R, wrk)
        xe_l = sb("xe_l", [P, KC, CHOSEN], F32R, wrk)
        gl = sb("gl", [P, 2, CHOSEN], F32, wrk)
        g_h = sb("g_h", [P, FT1, CHOSEN], F32R, wrk)
        g_l = sb("g_l", [P, FT1, CHOSEN], F32R, wrk)
        gval = sb("gval", [P, 2, CT], F32, wrk)
        ye1 = sb("ye1", [P, CT, D], F32, wrk)
        wrk.close()
        ff1.close()
        rows1 = nc.dram_tensor("token_rows", [T, XG], F32, kind="Internal").ap()
        rows = nc.dram_tensor("expert_rows", [(ROUTED + TILES) * P, D], F32, kind="Internal").ap()
        results = nc.dram_tensor("expert_results", [(ROUTED + TILES) * P, D], F32, kind="Internal").ap()

        names = """x_in consts w_in ident cst stat_s aggr_s veps rstd_s xn_s xt_s tp lnf_s lnh_s lnl_s
            qkv_s raw_s sq_s ss_s rms0 rms_s nrm_s ng_s hi_s lo_s vh_s vl_s t12 ev_a ev_d wsp_h
            wsp_l mask_s c_dve c_act c_pool c_pe qs_s sc_s mx_s exp_s rc_s pt_s ph_s ring0 ring1
            ol_s sr_s o_s oh_s y_s xb_s zero_s zeroed shared_in gw_in gw_hs gw_ls gx_h gx_l tp0 lgt
            lg_t lg_s lgc rt rt_e rt_pe tbl scat wr_in ws_h ws_l tx xbi xh_s xl_s gu si_s h_s th
            hh_s hl_s yo ye yst got0 got1 got2 got3 out0 a1_in a1_h a1_l zk c1_pe c1_act c1_dve
            xs1_s tp1 x1h x1l q1 q1h q1l sc1 mx1 sb1 e1 sm1 rc1 pn1 pt1 p1h p1l o1 o1h o1l y1 x1a
            x1b v_in vs_hs vs_ls b_in k1c r1 r1_e srch cmpd cnt met own hots hot_pe found_s round
            cnd shf best row1 ga0 ga1 xe_t xe_hs xe_ls h1 gl_s gh_s gls gval_s y1e yb1 ys1 sadd""".split()
        s = {n: sem(n) for n in names}
        block = ctx.enter_context(nc.Block())

        x_tiled = ap["x"].rearrange("(t p) d -> p t d", p=P)
        out_tiled = out.rearrange("(t p) d -> p t d", p=P)

        def projected(engine, b):
            engine.wait_ge(s["vl_s"], (b + 1) * (GPB * GT))
            engine.wait_ge(s["ev_a"], 1 + (b + 1) * (GPB * 6))
            engine.wait_ge(s["ev_d"], 1 + (b + 1) * (GPB * 6))

        def attention_done(engine):
            for bank in range(2):
                engine.wait_ge(s[f"ring{bank}"], 1 + GROUPS * RING[bank])

        def x1_bank(half):
            return psum[:, 6 + half, :].rearrange("p (k c) -> p k c", k=KC)

        def blocks_done(engine):
            total = engine.value_load(table[0:1, 0, E + 1:E + 2], min_val=1, max_val=ROUTED)
            engine.wait_ge(s["yst"], 1 + total * 16)
            engine.sem_inc(s["met"], 1)

        @block.sync
        def _(sp):
            for name in COUNT_FROM_ONE:
                sp.sem_inc(s[name], 1)
            for g in range(GROUPS):
                sp.dma_start(x[:, g * GT:(g + 1) * GT, :], x_tiled[:, g * GT:(g + 1) * GT, :]).then_inc(s["x_in"], 16)
            sp.dma_start(xc[:], ap["ctx"]).then_inc(s["consts"], 16)
            sp.dma_start(lnx_g[:], ap["lnx_g"]).then_inc(s["consts"], 16)
            sp.dma_start(lnx_b[:], ap["lnx_b"]).then_inc(s["consts"], 16)
            sp.dma_start(ln_g[:], ap["ln_g"]).then_inc(s["consts"], 16)
            sp.dma_start(ln_b[:], ap["ln_b"]).then_inc(s["consts"], 16)
            sp.dma_start(qk_gain[:], ap["qk_gain"].partition_broadcast(P)).then_inc(s["consts"], 16)
            sp.dma_start(bo[:], ap["bo0"].partition_broadcast(P)).then_inc(s["consts"], 16)
            sp.dma_start(mask_u8[:], ap["mask"]).then_inc(s["consts"], 16)
            sp.dma_start(wkvx[:], ap["wkvx"]).then_inc(s["w_in"], 16)
            sp.dma_start(wqkv[:], ap["wqkv"]).then_inc(s["w_in"], 16)
            sp.dma_start(wo[:], ap["wo0"]).then_inc(s["w_in"], 16)
            sp.wait_ge(s["zero_s"], 1)
            for part in (rows[0:ROUTED * P], results[0:ROUTED * P]):
                sp.dma_start(part.rearrange("(n p) d -> p n d", p=P),
                             zeros[:].unsqueeze(1).broadcast_to((P, ROUTED, D))).then_inc(s["zeroed"], 16)
            attention_done(sp)
            sp.dma_start(gate_w[:], ap["gate0"]).then_inc(s["gw_in"], 16)
            sp.dma_start(w_raw[:], ap["experts0"][0]).then_inc(s["shared_in"], 16)

            def load_block(m):
                sp.wait_ge(s["tx"], 1 + m)
                sp.dma_start(xb[:], rows[ds(m * P, P), :]).then_inc(s["xbi"], 16)

            sp.wait_ge(s["scat"], 2 * TILES * 16)
            load_block(0)
            sp.wait_ge(s["tbl"], 3)
            total = sp.value_load(table[0:1, 0, E + 1:E + 2], min_val=LEAST * E, max_val=ROUTED)
            with sp.Fori(0, total) as m:
                load_block(m + 1)

            blocks_done(sp)
            sp.dma_start(xc1[:], ap["ctx"]).then_inc(s["a1_in"], 16)
            sp.dma_start(c_raw[:], ap["wkv1"]).then_inc(s["a1_in"], 16)
            sp.dma_start(a_raw[:], ap["wqo1"]).then_inc(s["a1_in"], 16)
            sp.dma_start(bo1[:], ap["bo1"].partition_broadcast(P)).then_inc(s["a1_in"], 16)

            sp.wait_ge(s["x1a"], 1 + TILES)
            sp.dma_start(v_raw[:], ap["experts1"][0]).then_inc(s["v_in"], 16)
            sp.dma_start(gate1_w[:], ap["gate1"]).then_inc(s["gw_in"], 16)
            sp.dma_start(b1[:], ap["b1"]).then_inc(s["b_in"], 16)
            sp.dma_start(b2[:].rearrange("p e d -> p (e d)"), ap["b2"].partition_broadcast(P)).then_inc(s["b_in"], 16)
            rows1_tiled = rows1.rearrange("(t p) d -> p t d", p=P)
            sp.wait_ge(s["xn_s"], 4 * TILES)
            sp.dma_start(rows1_tiled[:, :, 0:D], xn[:]).then_inc(s["row1"], 16)
            sp.wait_ge(s["r1"], R1_GATES)
            sp.dma_start(rows1_tiled[:, :, D:XG], gates[:]).then_inc(s["row1"], 16)
            sp.wait_ge(s["row1"], 32)
            with sp.Fori(1, E) as w:
                sp.wait_ge(s["vs_ls"], w * CUTS)
                sp.dma_start(v_raw[:], ap["experts1"][ds(w, 1)].rearrange("o p c -> p (o c)")).then_inc(s["v_in"], 16)

        @block.gpsimd
        def _(pool):
            pool.memset(zeros[:], 0.0).then_inc(s["zero_s"], 1)
            pool.memset(ident[:], 0.0).then_inc(s["ident"], 1)
            pool.memset(neg_half[:], -0.5).then_inc(s["cst"], 1)
            pool.wait_ge(s["ident"], 1)
            pool.affine_select(out=ident[:], in_=ident[:], compare_op=ALU.not_equal, fill=1.0, base=0,
                               pattern=[[-1, P]], channel_multiplier=1).then_inc(s["ident"], 1)
            pool.memset(mask_rows[:], 0.0).then_inc(s["cst"], 1)
            pool.memset(first_row[:], 0.0).then_inc(s["cst"], 1)
            pool.wait_ge(s["cst"], 3)
            pool.memset(mask_rows[0:1, :, PIECE - P:], -BIG).then_inc(s["cst"], 1)
            pool.memset(first_row[0:1], 1.0).then_inc(s["cst"], 1)
            pool.wait_ge(s["consts"], 8 * 16)
            pool.tensor_scalar(qk_gain[:, 0:D], qk_gain[:, 0:D], HD ** -0.5, None, ALU.mult).then_inc(s["cst"], 1)
            pool.wait_ge(s["cst"], 6)
            pool.tensor_tensor(qk_gain[:, D:], qk_gain[:, D:], qk_gain[:, 0:D], ALU.mult).then_inc(s["cst"], 1)
            pool.wait_ge(s["cst"], 7)

            pool.wait_ge(s["c_dve"], 2)
            pool.tensor_scalar(crs[:], cmv[:, 1:2], LN_EPS, None, ALU.add).then_inc(s["c_pool"], 1)
            pool.wait_ge(s["c_pool"], 1)
            pool.tensor_tensor(crs[:], crs[:], neg_half[:, 0:1], ALU.pow).then_inc(s["c_pool"], 1)

            def inverse_group(n, g, slope, shift):
                r = rstd[:, g * GT:(g + 1) * GT]
                pool.wait_ge(s["aggr_s"], n * TILES + (g + 1) * GT)
                pool.tensor_scalar(r, mean_var[:, g * GT:(g + 1) * GT, 1], slope, shift, ALU.mult, ALU.add).then_inc(s["veps"], 1)
                pool.wait_ge(s["veps"], n * GROUPS + g + 1)
                pool.tensor_tensor(r, r, neg_half[:, 0:GT], ALU.pow).then_inc(s["rstd_s"], 1)

            def inverse_std(n, slope=1.0, shift=LN_EPS):
                for g in range(GROUPS):
                    inverse_group(n, g, slope, shift)

            inverse_std(0, 1.0 + LN_EPS, LN_EPS * LN_EPS)

            pool.wait_ge(s["wsp_h"], 3)
            pool.tensor_tensor(wqkv_l[:], wqkv[:], wqkv_h[:].bitcast(F32), ALU.subtract).then_inc(s["wsp_l"], 1)
            pool.tensor_tensor(wo_l[:], wo[:], wo_h[:].bitcast(F32), ALU.subtract).then_inc(s["wsp_l"], 1)

            pool.wait_ge(s["c_dve"], 6)
            pool.tensor_scalar(cms[:], cms[:], 1.0 / HD, RMS_EPS ** 2, ALU.mult, ALU.max).then_inc(s["c_pool"], 1)
            pool.wait_ge(s["c_pool"], 3)
            pool.tensor_tensor(cms[:], cms[:], neg_half[:, 0:H], ALU.pow).then_inc(s["c_pool"], 1)

            with pool.Fori(0, B) as b:
                with pool.Fori(0, GPB) as gg:
                    g = b * GPB + gg
                    for t in range(GT):
                        pool.wait_ge(s["lnh_s"], g * GT + t + 1)
                        pool.tensor_tensor(lnl[:, t], lnf[:, t], lnh[:, t].bitcast(F32), ALU.subtract).then_inc(s["lnl_s"], 1)

                    def reciprocal_rms(t):
                        pool.wait_ge(s["ss_s"], g * GT + t + 1)
                        pool.sem_inc(s["met"], 1)
                        pool.tensor_scalar(rms[:, t, :], ssq[:, t, :], 1.0 / HD, RMS_EPS ** 2, ALU.mult, ALU.max).then_inc(s["rms0"], 1)
                        pool.wait_ge(s["rms0"], g * GT + t + 1)
                        pool.tensor_tensor(rms[:, t, :], rms[:, t, :], neg_half[:, 0:2 * H], ALU.pow).then_inc(s["rms_s"], 1)

                    for t in range(GT):
                        reciprocal_rms(t)
                    pool.wait_ge(s["raw_s"], (g + 1) * GT)
                    pool.sem_inc(s["met"], 1)
                    for t in range(GT):
                        pool.wait_ge(s["vh_s"], g * GT + t + 1)
                        vt = v[:, ds(gg * GT + t, 1), :, :]
                        pool.tensor_tensor(vt[:, 0, :, HD:P], qkv[:, t, 2 * D:].rearrange("p (h d) -> p h d", h=H),
                                           vt[:, 0, :, 0:HD].bitcast(F32), ALU.subtract).then_inc(s["vl_s"], 1)
                with pool.Fori(0, GPB) as gg:
                    g = b * GPB + gg
                    for t in range(GT):
                        xg = x[:, ds(g * GT + t, 1), :]
                        pool.tensor_tensor(xg[:, 0], xg[:, 0], bo[:], ALU.add).then_inc(s["xb_s"], 1)
                    for p in range(PAIRS):
                        pool.wait_ge(s["oh_s"], g * PAIRS + p + 1)
                        o = (slice(None), p // 2, slice(p % 2 * 2 * P, (p % 2 + 1) * 2 * P))
                        pool.tensor_tensor(oT_l[o], oT[:, p % 2, :], oT_h[o].bitcast(F32), ALU.subtract).then_inc(s["ol_s"], 1)

            attention_done(pool)
            pool.memset(ones[:], 1.0).then_inc(s["cst"], 1)
            pool.memset(before[:], 1.0).then_inc(s["cst"], 1)
            pool.iota(favour[:], pattern=[[0, TILES], [-1, E]], base=E, channel_multiplier=0,
                      allow_small_or_imprecise_dtypes=True).then_inc(s["cst"], 1)
            pool.wait_ge(s["cst"], 10)
            pool.affine_select(out=before[:], in_=before[:], compare_op=ALU.is_ge, fill=0.0, base=-1,
                               pattern=[[1, P]], channel_multiplier=-1).then_inc(s["cst"], 1)
            inverse_std(1)

            def load_weights(w):
                pool.dma_start(w_raw[:], ap["experts0"][ds(w, 1)].rearrange("o p c -> p (o c)")).then_inc(s["wr_in"], 16)

            def split_weights(w, side, cols=slice((WCUTS - 1) * WCUT, FW)):
                pool.wait_ge(s["wr_in"], 16 * w)
                pool.sem_inc(s["met"], 1)
                pool.tensor_copy(w_h[side][:, cols], w_raw[:, cols]).then_inc(s["ws_h"], 1)
                pool.wait_ge(s["ws_h"], 2 + (w - 1) * WCUTS)
                pool.tensor_tensor(w_l[side][:], w_raw[:], w_h[side][:].bitcast(F32), ALU.subtract).then_inc(s["ws_l"], 1)
                pool.wait_ge(s["ws_l"], w + 1)

            pool.wait_ge(s["ws_h"], 1)
            pool.tensor_tensor(w_l[0][:], w_raw[:], w_h[0][:].bitcast(F32), ALU.subtract).then_inc(s["ws_l"], 1)
            pool.wait_ge(s["ws_l"], 1)
            load_weights(1)
            split_weights(1, 1, slice(0, FW))
            load_weights(2)
            pool.wait_ge(s["zeroed"], 32)
            pool.wait_ge(s["tbl"], 3)
            for t in range(TILES):
                for k in range(2):
                    pool.indirect_dma_start(out=rows[0:ROUTED * P], out_offset=bass.IndirectOffsetOnAxis(ap=slot[k][:, t:t + 1], axis=0),
                                            in_=xn[:, t, :], in_offset=None, bounds_check=ROUTED * P - 1,
                                            oob_is_err=False).then_inc(s["scat"], 16)
            with pool.Fori(0, (E - 2) // 2) as p:
                for side in range(2):
                    w = p * 2 + 2 + side
                    done = pool.value_load(table[0:1, 0, ds(w - 1, 1)], min_val=0, max_val=ROUTED)
                    pool.wait_ge(s["yo"], done + SHARED)
                    pool.sem_inc(s["met"], 1)
                    split_weights(w, side)
                    load_weights(w + 1)
            done = pool.value_load(table[0:1, 0, E - 1:E], min_val=0, max_val=ROUTED)
            pool.wait_ge(s["yo"], done + SHARED)
            pool.sem_inc(s["met"], 1)
            split_weights(E, 0)
            blocks_done(pool)
            for t in range(TILES):
                for k in range(2):
                    if t >= 4:
                        pool.wait_ge(s["out0"], t - 3)
                    pool.indirect_dma_start(out=y_got[:, 2 * (t % 4) + k, :], out_offset=None, in_=results[0:ROUTED * P],
                                            in_offset=bass.IndirectOffsetOnAxis(ap=slot[k][:, t:t + 1], axis=0),
                                            bounds_check=ROUTED * P - 1, oob_is_err=False).then_inc(s[f"got{t % 4}"], 16)
                if t % GT == GT - 1 and t > GT:
                    inverse_group(2, t // GT - 1, 1.0, LN_EPS)
            inverse_group(2, GROUPS - 1, 1.0, LN_EPS)

            pool.wait_ge(s["a1_in"], 64)
            pool.wait_ge(s["xn_s"], 3 * TILES)
            for t in range(TILES):
                pool.tensor_tensor(x[:, t, :], x[:, t, :], bo1[:], ALU.add).then_inc(s["x1b"], 1)

            pool.wait_ge(s["x1a"], 1 + TILES)
            pool.dma_start(out_tiled, x[:]).then_inc(s["sadd"], 16)
            pool.memset(ones1[:], 1.0).then_inc(s["k1c"], 1)
            pool.memset(before1[:], 1.0).then_inc(s["k1c"], 1)
            pool.memset(ones_b[:], 1.0).then_inc(s["k1c"], 1)
            pool.iota(columns[:], pattern=[[1, P]], base=0, channel_multiplier=0,
                      allow_small_or_imprecise_dtypes=True).then_inc(s["k1c"], 1)
            pool.iota(lane[:], pattern=[[0, 1]], base=0, channel_multiplier=1,
                      allow_small_or_imprecise_dtypes=True).then_inc(s["k1c"], 1)
            pool.iota(tile_no[:], pattern=[[1, TILES]], base=0, channel_multiplier=0,
                      allow_small_or_imprecise_dtypes=True).then_inc(s["k1c"], 1)
            pool.wait_ge(s["k1c"], 6)
            pool.affine_select(out=before1[:], in_=before1[:], compare_op=ALU.is_ge, fill=0.0, base=-1,
                               pattern=[[1, P]], channel_multiplier=-1).then_inc(s["k1c"], 1)
            inverse_std(3)

            pool.wait_ge(s["vs_hs"], CUTS)
            for c in range(CUTS):
                cols = slice(c * CUT, (c + 1) * CUT)
                pool.tensor_tensor(v_l[0][:, cols], v_raw[:, cols], v_h[0][:, cols].bitcast(F32), ALU.subtract).then_inc(s["vs_ls"], 1)

            def gather(e, side):
                pool.tensor_copy(own[side][:], tokens[:, ds(e, 1), :].rearrange("p o t -> p (o t)")).then_inc(s["own"], 1)
                pool.wait_ge(s["own"], e + 1)
                pool.sem_inc(s["met"], 1)
                for t in range(CT):
                    pool.indirect_dma_start(
                        out=gathered[side][:, t, :], out_offset=None, in_=rows1,
                        in_offset=bass.IndirectOffsetOnAxis(ap=own[side][:, t:t + 1], axis=0),
                        bounds_check=T - 1, oob_is_err=False).then_inc(s[f"ga{side}"], 16)

            pool.wait_ge(s["row1"], 32)
            pool.wait_ge(s["found_s"], 2)
            gather(0, 0)

            def expert(e, side, last):
                pool.wait_ge(s["sadd"], 16 + e * (CT * 16))
                if not last:
                    pool.wait_ge(s["ys1"], 1 + e * CT)
                    pool.sem_inc(s["met"], 1)
                    gather(e + 1, 1 - side)
                pool.wait_ge(s["ys1"], 1 + (e + 1) * CT)
                pool.sem_inc(s["met"], 1)
                for t in range(CT):
                    pool.indirect_dma_start(
                        out=out, out_offset=bass.IndirectOffsetOnAxis(ap=own[side][:, t:t + 1], axis=0),
                        in_=ye1[:, t, :], in_offset=None, bounds_check=T - 1, oob_is_err=True,
                        compute_op=ALU.add).then_inc(s["sadd"], 16)

            with pool.Fori(0, E // 2 - 1) as p:
                for side in range(2):
                    expert(2 * p + side, side, False)
            expert(E - 2, 0, False)
            expert(E - 1, 1, True)
            pool.wait_ge(s["sadd"], 16 + E * CT * 16)

        @block.scalar
        def _(act):
            def copy(o, i, name, n=1):
                act.activation(o, i, ACT.Copy).then_inc(s[name], n)

            act.wait_ge(s["ident"], 2)
            copy(ident_r[:], ident[:], "ident")
            act.wait_ge(s["w_in"], 48)
            copy(wkvx_h[:], wkvx[:], "wsp_h")
            copy(wqkv_h[:], wqkv[:], "wsp_h")
            copy(wo_h[:], wo[:], "wsp_h")
            act.wait_ge(s["c_dve"], 5)
            copy(ch[:], cf[:], "c_act")
            act.wait_ge(s["c_pe"], 2)
            copy(ckv[:], psum[:, 1, :], "c_act")
            act.wait_ge(s["c_act"], 2)
            act.activation(csq[:], ckv[:, 0:D], ACT.Square).then_inc(s["c_act"], 1)
            copy(v[:, KT - 1, :, 0:HD], ckv[:, D:].rearrange("p (h d) -> p h d", h=H), "c_act")
            act.wait_ge(s["c_dve"], 9)
            khead = ckv[:, 0:D].rearrange("p (h d) -> p h d", h=H).unsqueeze(2).broadcast_to((P, H, 2, HD))
            copy(cparts[:, 0:H, :].rearrange("p h (r d) -> p h r d", r=2), khead, "c_act")
            act.wait_ge(s["c_pe"], 4)
            copy(kT[:, :, 0, CTX0:], psum[:, 2, :].rearrange("p (h k) -> p h k", h=H), "c_act")

            with act.Fori(0, B) as b:
                with act.Fori(0, GPB) as gg:
                    g = b * GPB + gg
                    for t in range(GT):
                        act.wait_ge(s["lnf_s"], (g * GT + t + 1) * KC)
                        copy(lnh[:, t], lnf[:, t], "lnh_s")

                    def raw(t):
                        act.wait_ge(s["qkv_s"], g * GT + t + 1)
                        flat = psum[:, 2 * (t % 2):2 * (t % 2) + 2, :].rearrange("p b c -> p (b c)")
                        if t >= 2:
                            act.wait_ge(s["ss_s"], g * GT + t - 1)
                        act.activation(sq[:, t % 2, :], flat[:, 0:2 * D], ACT.Square).then_inc(s["sq_s"], 1)
                        vt = v[:, ds(gg * GT + t, 1), :, 0:HD]
                        copy(vt[:, 0], flat[:, 2 * D:3 * D].rearrange("p (h d) -> p h d", h=H), "vh_s")
                        copy(qkv[:, t, :], flat[:, 0:3 * D], "raw_s")

                    def high_parts(t):
                        act.wait_ge(s["ng_s"], g * GT + t + 1)
                        if t >= 2:
                            act.wait_ge(s["t12"], g * 12 + 3 * (t - 1))
                        copy(parts[:, t % 2, 0:H, 0:HD], qkv[:, t, 0:D].rearrange("p (h d) -> p h d", h=H), "hi_s")
                        kk = qkv[:, t, D:2 * D].rearrange("p (h d) -> p h d", h=H).unsqueeze(2).broadcast_to((P, H, 2, HD))
                        copy(parts[:, t % 2, H:2 * H, :].rearrange("p h (r d) -> p h r d", r=2), kk, "hi_s")

                    def evacuate(t):
                        for c in range(3):
                            if (3 * t + c) % 2 == 0:
                                act.wait_ge(s["t12"], g * 12 + 3 * t + c + 1)
                                src = psum[:, 4 + (3 * t + c) % 4, :].rearrange("p (h k) -> p h k", h=H)
                                cols = ds(gg * (GT * P) + t * P, P)
                                dst = qT[:, :, cols] if c == 0 else kT[:, :, c - 1, cols]
                                copy(dst, src, "ev_a")

                    raw(0)
                    raw(1)
                    raw(2)
                    high_parts(0)
                    raw(3)
                    for t in range(GT):
                        if t + 1 < GT:
                            high_parts(t + 1)
                        evacuate(t)

                def queries_copied(gg):
                    copy(qs[:, 0:2], qT[:, 0:2, ds(gg * (GT * P), GT * P)].bitcast(F32), "qs_s")

                def exponentials(g, u):
                    act.wait_ge(s["mx_s"], g * UNITS + u + 1)
                    if u >= 3:
                        act.wait_ge(s["pt_s"], (g * UNITS + (u - 2 if u < UNITS else u)) * 3)
                    z, i = 3 * (u % 2), u % UNITS
                    act.activation(prob[:, i % 3, :].rearrange("p (c k) -> p c k", c=3), psum[:, z:z + 3, 0:PIECE],
                                   ACT.Exp, bias=neg_max[:, i:i + 1],
                                   accum_out=denom[:, i:i + 1]).then_inc(s["exp_s"], 1)

                def attention(gg, following):
                    g = b * GPB + gg

                    def chunk_high(u, c):
                        act.wait_ge(s["pt_s"], (g * UNITS + u) * 3 + c + 1)
                        copy(pT_h[:, c * CK:(c + 1) * CK, (u % GT) * P:(u % GT + 1) * P],
                             psum[:, 6 + USES["chunk", u, c][0], 0:PIECE].rearrange("p (k c) -> p k c", k=CK), "ph_s")

                    def repeated(p):
                        bank, _ = USES["reciprocals", p]
                        act.wait_ge(s["sr_s"], g * PAIRS + p + 1)
                        copy(rep_rd[:, p % 2, :], psum[:, 6 + bank, 0:2 * P], f"ring{bank}")

                    def out_high(p):
                        bank, before = USES["result", p]
                        act.wait_ge(s[f"ring{bank}"], 1 + g * RING[bank] + before + 1)
                        copy(oT_h[:, p // 2, p % 2 * 2 * P:(p % 2 + 1) * 2 * P], oT[:, p % 2, :], "oh_s")

                    for u in range(UNITS):
                        chunk_high(u, 0)
                        chunk_high(u, 1)
                        if u + 1 < UNITS:
                            exponentials(g, u + 1)
                        chunk_high(u, 2)
                        if following and u == UNITS - 2:
                            queries_copied(gg + 1)
                        if u % 2 == 0 and u:
                            out_high(u // 2 - 1)
                        if u % 2:
                            repeated(u // 2)
                    if following:
                        exponentials(g, UNITS)
                    out_high(PAIRS - 1)

                projected(act, b)
                queries_copied(0)
                exponentials(b * GPB, 0)
                with act.Fori(0, GPB - 1) as gg:
                    attention(gg, True)
                attention(GPB - 1, False)

            def gate_logits(layer, gw_raw, gw_h, xT_h, slots, logitT, logit):
                def logits_out(g):
                    act.wait_ge(s["lg_s"], layer * GROUPS + g + 1)
                    copy(logitT[:, g * GT * P:(g + 1) * GT * P], psum[0:E, 4 + g % 2, :], "lgt")

                act.wait_ge(s["gw_in"], 16 * (layer + 1))
                copy(gw_h[:], gw_raw[:], "gw_hs")
                for t in range(TILES):
                    n = layer * TILES + t
                    cols = slice((t % slots) * P, (t % slots + 1) * P)
                    act.wait_ge(s["tp0"], n + 1)
                    if t >= slots:
                        act.wait_ge(s["lg_s"], layer * GROUPS + (t - slots) // GT + 1)
                    copy(xT_h[:, :, cols], psum[:, t % 4, 0:D].rearrange("p (k c) -> p k c", k=KC), "gx_h")
                    if t % GT == GT - 1 and t > GT:
                        logits_out(t // GT - 1)
                logits_out(GROUPS - 1)
                act.wait_ge(s["lg_t"], layer + 1)
                copy(logit[:].rearrange("p t e -> p (t e)"), psum[:, 6, 0:TILES * E], "lgc")

            attention_done(act)
            act.wait_ge(s["shared_in"], 16)
            copy(w_h[0][:], w_raw[:], "ws_h")
            gate_logits(0, gate_w, gate_h, xT_h, TILES, logitT, logit)
            act.wait_ge(s["rt"], RT_SHIFTED)
            act.activation(logit[:], logit[:], ACT.Exp).then_inc(s["rt_e"], 1)

            def x_high_shared(n):
                if not isinstance(n, int):
                    act.wait_ge(s["gu"], n * 4)
                copy(xbT_h[:], xT_h[:, :, ds(n * P, P)].bitcast(F32), "xh_s")

            def x_high(m):
                act.wait_ge(s["tx"], 1 + m + 1)
                copy(xbT_h[:], psum[:, 4, 0:D].rearrange("p (k c) -> p k c", k=KC), "xh_s")

            def silus(n):
                for c, (lo, hi) in enumerate(((0, FA), (FA, F))):
                    act.wait_ge(s["gu"], n * 4 + 2 * c + 1)
                    act.activation(silu[:, lo:hi], psum[:, 2 * c, 0:hi - lo], ACT.Silu).then_inc(s["si_s"], 1)

            def hidden_high(n):
                for c in range(2):
                    act.wait_ge(s["th"], n * 2 + c + 1)
                    copy(hT_h[:, 3 * c:3 * c + 3, :], psum[:, 5 + c, 0:3 * P].rearrange("p (k c) -> p k c", k=3), "hh_s")

            def store_result(m):
                act.wait_ge(s["yo"], m + (SHARED + 1))
                act.wait_ge(s["yst"], 1 + m * 16)
                copy(y_sb[:], psum[:, 7, 0:D], "ye")
                act.wait_ge(s["ye"], m + (SHARED + 2))
                act.dma_start(results[ds(m * P, P), :], y_sb[:]).then_inc(s["yst"], 16)

            x_high_shared(0)
            with act.Fori(0, SHARED - 1) as n:
                silus(n)
                x_high_shared(n + 1)
                hidden_high(n)
            silus(SHARED - 1)
            x_high(0)
            hidden_high(SHARED - 1)
            act.wait_ge(s["tbl"], 3)

            def weights_high(w, side, c):
                act.wait_ge(s["wr_in"], 16 * w)
                copy(w_h[side][:, c * WCUT:(c + 1) * WCUT], w_raw[:, c * WCUT:(c + 1) * WCUT], "ws_h")

            def routed_expert(w, side, one=False, last=False):
                first = act.value_load(table[0:1, 0, ds(w, 1)], min_val=0, max_val=ROUTED - LEAST)
                more = act.value_load(table[0:1, 1, ds(w, 1)], min_val=LEAST - 1, max_val=TILES - 1)
                n = act.snap(first + SHARED)
                silus(n)
                x_high(first + 1)
                if one:
                    act.wait_ge(s["yo"], SHARED)
                else:
                    store_result(act.value_load(table[0:1, 2, ds(w, 1)], min_val=LEAST - 1, max_val=ROUTED - LEAST))
                for c in range(0 if last else WCUTS - 2):
                    weights_high(w + 1, 1 - side, c)
                hidden_high(n)
                if not last:
                    weights_high(w + 1, 1 - side, WCUTS - 2)
                with act.Fori(0, more) as i:
                    n = act.snap(first + i + (SHARED + 1))
                    silus(n)
                    x_high(first + i + 2)
                    store_result(first + i)
                    hidden_high(n)

            routed_expert(1, 1, one=True)
            with act.Fori(0, E // 2 - 1) as p:
                for side in range(2):
                    routed_expert(2 * p + 2 + side, side)
            routed_expert(E, 0, last=True)
            store_result(act.value_load(table[0:1, 2, E + 1:E + 2], min_val=LEAST * E - 1, max_val=ROUTED - 1))

            act.wait_ge(s["a1_in"], 64)
            copy(c_h[:], c_raw[:], "a1_h")
            copy(a_h[:], a_raw[:], "a1_h")
            act.wait_ge(s["c1_pe"], 1)
            copy(cT_h[:], psum[0:PX, 0, 0:KX * P].rearrange("p (k c) -> p k c", k=KX), "c1_act")
            act.wait_ge(s["c1_dve"], 1)
            for k in range(KX):
                for src, dst in ((cT_h, cd_h), (cT_l, cd_l)):
                    act.wait_ge(s["c1_act"], 1)
                    copy(dst[:, k], src[:, k, :].bitcast(F32).rearrange("p (b c) -> p b c", b=B).unsqueeze(2)
                         .broadcast_to((PX, B, 2, C)), "c1_act")
            act.wait_ge(s["c1_pe"], 3)
            act.wait_ge(s["zk"], 2)
            for k in range(KC):
                for hh in range(2):
                    half = slice(hh * C, (hh + 1) * C)
                    head = 2 * k + hh
                    copy(kb_h[half, :, k, head * C:(head + 1) * C],
                         psum[half, 1, k * P:(k + 1) * P].rearrange("p (b c) -> p b c", b=B), "c1_act")
                    copy(vb_h[half, :, k, hh * HD:(hh + 1) * HD],
                         psum[half, 2, :].rearrange("p (b d) -> p b d", b=B)[:, :, head * HD:(head + 1) * HD], "c1_act")
            act.wait_ge(s["c1_dve"], 1 + 4 * KC)
            act.wait_ge(s["c1_act"], 5 + 4 * KC)

            def group_copied(g):
                act.wait_ge(s["xn_s"], 2 * TILES + (g + 1) * GT)
                for t in range(GT):
                    copy(xs1[:, t, :], xn[:, ds(g * GT + t, 1), :].rearrange("p o d -> p (o d)"), "xs1_s")

            def queries1(g):
                for half in range(2):
                    act.wait_ge(s["tp1"], g * 2 + half + 1)
                    copy(x1_h[:, :, half * 2 * P:(half + 1) * 2 * P], x1_bank(half), "x1h")
                for k in range(KC):
                    act.wait_ge(s["q1"], g * KC + k + 1)
                    act.activation(q1_h[:, k, :], psum[:, 4 + k, :], ACT.Copy, scale=HD ** -0.5).then_inc(s["q1h"], 1)

            def attention1(g, b, following):
                if following:
                    group_copied(g + 1)
                for t in range(GT):
                    act.wait_ge(s["sb1"], g * GT + t + 1)
                    act.activation(p1[:, t, :], p1[:, t, :], ACT.Exp).then_inc(s["e1"], 1)
                if following:
                    queries1(g + 1)
                for t in range(GT):
                    act.wait_ge(s["pt1"], g * GT + t + 1)
                    copy(p1T_h[:, :, t * P:(t + 1) * P], psum[:, t, 0:D].rearrange("p (k c) -> p k c", k=KC), "p1h")
                for k in range(KC):
                    act.wait_ge(s["o1"], g * KC + k + 1)
                    copy(o1_h[:, k, :], psum[:, 6 + k, :], "o1h")

            group_copied(0)
            queries1(0)
            for b in range(B):
                with act.Fori(0, GPB if b < B - 1 else GPB - 1) as gg:
                    attention1(b * GPB + gg, b, True)
            attention1(GROUPS - 1, B - 1, False)

            gate_logits(1, gate1_w, gate1_h, x2T_h, 2 * GT, logit1T, gates)
            act.wait_ge(s["lgc"], 2)
            act.activation(gates[:], gates[:], ACT.Exp, scale=-1.0).then_inc(s["r1_e"], 1)

            def rows_high(n):
                for t in range(CT):
                    act.wait_ge(s["xe_t"], n * CT + t + 1)
                    copy(xe_h[:, :, t * P:(t + 1) * P], psum[:, 6 + t % 2, 0:D].rearrange("p (k c) -> p k c", k=KC), "xe_hs")

            def weights_high(w, side):
                act.wait_ge(s["v_in"], 16 * (w + 1))
                for c in range(CUTS):
                    cols = slice(c * CUT, (c + 1) * CUT)
                    copy(v_h[side][:, cols], v_raw[:, cols], "vs_hs")
                    yield

            def expert1(e, side, last):
                if not last:
                    act.wait_ge(s["yb1"], 1 + e * CT)
                    cuts = weights_high(e + 1, 1 - side)
                for f in range(FT1):
                    act.wait_ge(s["h1"], e * FT1 + f + 1)
                    if f >= 2:
                        act.wait_ge(s["gls"], e * FT1 + f - 1)
                    act.activation(gl[:, f % 2, :], psum[:, f % 2, :], ACT.Gelu, bias=b1[:, ds(e * FT1 + f, 1)]).then_inc(s["gl_s"], 1)
                    if not last and f % 2:
                        next(cuts)
                if not last:
                    rows_high(e + 1)

            for _ in weights_high(0, 0):
                pass
            act.wait_ge(s["b_in"], 32)
            rows_high(0)
            with act.Fori(0, E // 2 - 1) as p:
                for side in range(2):
                    expert1(2 * p + side, side, False)
            expert1(E - 2, 0, False)
            expert1(E - 1, 1, True)

        @block.vector
        def _(dve):
            def statistics(n, g, src):
                for t in range(g * GT, (g + 1) * GT):
                    dve.bn_stats(stat[:, t, :], src[:, t, :]).then_inc(s["stat_s"], 1)
                dve.wait_ge(s["stat_s"], n * TILES + (g + 1) * GT)
                for t in range(g * GT, (g + 1) * GT):
                    dve.bn_aggr(mean_var[:, t, :], stat[:, t, :]).then_inc(s["aggr_s"], 1)

            def normalized(n, g, src):
                dve.wait_ge(s["rstd_s"], n * GROUPS + g + 1)
                for t in range(g * GT, (g + 1) * GT):
                    dve.tensor_scalar(xn[:, t, :], src[:, t, :], mean_var[:, t, 0:1], rstd[:, t:t + 1],
                                      ALU.subtract, ALU.mult).then_inc(s["xn_s"], 1)

            def norm(n, src, prepare, follow):
                statistics(n, 0, src)
                statistics(n, 1, src)
                prepare()
                for g in range(GROUPS):
                    normalized(n, g, src)
                    if g + 2 < GROUPS:
                        statistics(n, g + 2, src)
                    if g:
                        for t in range((g - 1) * GT, g * GT):
                            follow(t)
                for t in range(TILES - GT, TILES):
                    follow(t)

            def low_gate(layer, gw_raw, gw_h, gw_l):
                dve.wait_ge(s["gw_hs"], layer + 1)
                dve.tensor_tensor(gw_l[:], gw_raw[:], gw_h[:].bitcast(F32), ALU.subtract).then_inc(s["gw_ls"], 1)

            def low_tile(layer, t, xT_h, xT_l, slots):
                cols = slice((t % slots) * P, (t % slots + 1) * P)
                dve.wait_ge(s["gx_h"], layer * TILES + t + 1)
                dve.tensor_tensor(xT_l[:, :, cols], psum[:, t % 4, 0:D].rearrange("p (k c) -> p k c", k=KC),
                                  xT_h[:, :, cols].bitcast(F32), ALU.subtract).then_inc(s["gx_l"], 1)

            dve.wait_ge(s["consts"], 8 * 16)
            dve.bn_stats(cstat[:], xc[:]).then_inc(s["c_dve"], 1)
            dve.wait_ge(s["c_dve"], 1)
            dve.bn_aggr(cmv[:], cstat[:]).then_inc(s["c_dve"], 1)
            dve.wait_ge(s["x_in"], 16 * GROUPS)
            statistics(0, 0, x)
            statistics(0, 1, x)
            dve.wait_ge(s["c_pool"], 2)
            dve.tensor_scalar(xcn[:], xc[:], cmv[:, 0:1], crs[:], ALU.subtract, ALU.mult).then_inc(s["c_dve"], 1)
            statistics(0, 2, x)
            dve.wait_ge(s["c_pe"], 1)
            for k in range(KX):
                dve.tensor_scalar(cf[:, k, :], psum[0:PX, 0, k * P:(k + 1) * P], lnx_g[:, k:k + 1], lnx_b[:, k:k + 1],
                                  ALU.mult, ALU.add).then_inc(s["c_dve"], 1)
            statistics(0, 3, x)
            dve.wait_ge(s["c_act"], 1)
            dve.tensor_copy(mask_f[:], mask_u8[:]).then_inc(s["mask_s"], 1)
            dve.wait_ge(s["mask_s"], 1)
            dve.wait_ge(s["cst"], 5)
            for b in range(B):
                dve.tensor_scalar(mask_rows[0:1, b, PIECE - P + b * C:PIECE - P + (b + 1) * C], mask_f[:, b * C:(b + 1) * C], 1.0, BIG,
                                  ALU.subtract, ALU.mult).then_inc(s["mask_s"], 1)
            dve.tensor_tensor(cl[:], cf[:], ch[:].bitcast(F32), ALU.subtract).then_inc(s["mask_s"], 1)
            dve.wait_ge(s["wsp_h"], 1)
            dve.tensor_tensor(wkvx_l[:], wkvx[:], wkvx_h[:].bitcast(F32), ALU.subtract).then_inc(s["mask_s"], 1)
            for g in range(GROUPS):
                normalized(0, g, x)
            dve.wait_ge(s["c_act"], 3)
            dve.tensor_reduce(cms[:], csq[:].rearrange("p (h d) -> p h d", h=H), AX.X, ALU.add).then_inc(s["c_dve"], 1)
            dve.wait_ge(s["c_pool"], 4)
            ck = ckv[:, 0:D].rearrange("p (h d) -> p h d", h=H)
            dve.tensor_tensor(ck, ck, cms[:].unsqueeze(2).broadcast_to((P, H, HD)), ALU.mult).then_inc(s["c_dve"], 1)
            dve.wait_ge(s["c_dve"], 7)
            dve.tensor_tensor(ckv[:, 0:D], ckv[:, 0:D], qk_gain[:, D:], ALU.mult).then_inc(s["c_dve"], 1)
            dve.wait_ge(s["c_act"], 4)
            dve.tensor_tensor(v[:, KT - 1, :, HD:], ckv[:, D:].rearrange("p (h d) -> p h d", h=H),
                              v[:, KT - 1, :, 0:HD].bitcast(F32), ALU.subtract).then_inc(s["c_dve"], 1)
            dve.wait_ge(s["c_act"], 5)
            khead = ck.unsqueeze(2).broadcast_to((P, H, 2, HD))
            dve.tensor_tensor(cparts[:, H:, :].rearrange("p h (r d) -> p h r d", r=2), khead,
                              cparts[:, 0:H, :].rearrange("p h (r d) -> p h r d", r=2).bitcast(F32),
                              ALU.subtract).then_inc(s["c_dve"], 1)
            dve.wait_ge(s["c_pe"], 4)
            dve.tensor_copy(kT[:, :, 1, CTX0:], psum[:, 3, :].rearrange("p (h k) -> p h k", h=H)).then_inc(s["c_dve"], 1)

            dve.wait_ge(s["xn_s"], TILES)
            with dve.Fori(0, B) as b:
                with dve.Fori(0, GPB) as gg:
                    g = b * GPB + gg
                    for t in range(GT):
                        dve.tensor_copy(xt[:, t, :], xn[:, ds(g * GT + t, 1), :].rearrange("p o d -> p (o d)")).then_inc(s["xt_s"], 1)
                    for t in range(GT):
                        dve.wait_ge(s["tp"], g * GT + t + 1)
                        for k in range(KC):
                            dve.tensor_scalar(lnf[:, t, k, :], psum[:, 4 + t, k * P:(k + 1) * P], ln_g[:, k:k + 1],
                                              ln_b[:, k:k + 1], ALU.mult, ALU.add).then_inc(s["lnf_s"], 1)

                    def sums_of_squares(t):
                        dve.wait_ge(s["sq_s"], g * GT + t + 1)
                        dve.tensor_reduce(ssq[:, t, :], sq[:, t % 2, :].rearrange("p (h d) -> p h d", d=HD), AX.X,
                                          ALU.add).then_inc(s["ss_s"], 1)

                    def rms_scaled(t):
                        dve.wait_ge(s["raw_s"], g * GT + t + 1)
                        dve.wait_ge(s["rms_s"], g * GT + t + 1)
                        qk = qkv[:, t, 0:2 * D].rearrange("p (h d) -> p h d", d=HD)
                        dve.tensor_tensor(qk, qk, rms[:, t, :].unsqueeze(2).broadcast_to((P, 2 * H, HD)),
                                          ALU.mult).then_inc(s["nrm_s"], 1)
                        dve.wait_ge(s["nrm_s"], g * GT + t + 1)
                        dve.tensor_tensor(qkv[:, t, D:2 * D], qkv[:, t, D:2 * D], qk_gain[:, D:], ALU.mult).then_inc(s["ng_s"], 1)

                    def low_parts(t):
                        dve.wait_ge(s["hi_s"], (g * GT + t + 1) * 2)
                        dve.tensor_tensor(parts[:, t % 2, 0:H, HD:], qkv[:, t, 0:D].rearrange("p (h d) -> p h d", h=H),
                                          parts[:, t % 2, 0:H, 0:HD].bitcast(F32), ALU.subtract).then_inc(s["lo_s"], 1)
                        kk = qkv[:, t, D:2 * D].rearrange("p (h d) -> p h d", h=H).unsqueeze(2).broadcast_to((P, H, 2, HD))
                        dve.tensor_tensor(parts[:, t % 2, 2 * H:, :].rearrange("p h (r d) -> p h r d", r=2), kk,
                                          parts[:, t % 2, H:2 * H, :].rearrange("p h (r d) -> p h r d", r=2).bitcast(F32),
                                          ALU.subtract).then_inc(s["lo_s"], 1)

                    def evacuate(t):
                        for c in range(3):
                            if (3 * t + c) % 2:
                                dve.wait_ge(s["t12"], g * 12 + 3 * t + c + 1)
                                src = psum[:, 4 + (3 * t + c) % 4, :].rearrange("p (h k) -> p h k", h=H)
                                cols = ds(gg * (GT * P) + t * P, P)
                                dst = qT[:, :, cols] if c == 0 else kT[:, :, c - 1, cols]
                                dve.tensor_copy(dst, src).then_inc(s["ev_d"], 1)

                    sums_of_squares(0)
                    sums_of_squares(1)
                    rms_scaled(0)
                    sums_of_squares(2)
                    rms_scaled(1)
                    low_parts(0)
                    sums_of_squares(3)
                    rms_scaled(2)
                    low_parts(1)
                    evacuate(0)
                    rms_scaled(3)
                    for t in range(1, GT):
                        if t + 1 < GT:
                            low_parts(t + 1)
                        evacuate(t)

                def queries_copied(gg):
                    dve.tensor_copy(qs[:, 2:4], qT[:, 2:4, ds(gg * (GT * P), GT * P)].bitcast(F32)).then_inc(s["qs_s"], 1)

                def maxima(g, u):
                    dve.wait_ge(s["sc_s"], g * UNITS + u + 1)
                    z, i = 3 * (u % 2), u % UNITS
                    dve.tensor_reduce(neg_max[:, i:i + 1], psum[:, z:z + 3, 0:PIECE],
                                      AX.XY, ALU.max, negate=True).then_inc(s["mx_s"], 1)

                def reciprocals(g, u):
                    dve.wait_ge(s["exp_s"], g * UNITS + u + 1)
                    i = u % UNITS
                    dve.reciprocal(rdenom[:, i:i + 1], denom[:, i:i + 1]).then_inc(s["rc_s"], 1)

                def attention(gg, following):
                    g = b * GPB + gg

                    def chunk_low(u, c):
                        bank, _ = USES["chunk", u, c]
                        cols = slice((u % GT) * P, (u % GT + 1) * P)
                        dve.wait_ge(s["ph_s"], (g * UNITS + u) * 3 + c + 1)
                        dve.tensor_tensor(pT_l[:, c * CK:(c + 1) * CK, cols],
                                          psum[:, 6 + bank, 0:PIECE].rearrange("p (k c) -> p k c", k=CK),
                                          pT_h[:, c * CK:(c + 1) * CK, cols].bitcast(F32), ALU.subtract).then_inc(s[f"ring{bank}"], 1)

                    def out_scaled(p):
                        bank, _ = USES["result", p]
                        r_bank, before = USES["reciprocals", p]
                        dve.wait_ge(s[f"ring{r_bank}"], 1 + g * RING[r_bank] + before + 1)
                        dve.wait_ge(s["o_s"], g * PAIRS + p + 1)
                        if p >= 2:
                            dve.wait_ge(s["ol_s"], g * PAIRS + p - 1)
                        dve.tensor_tensor(oT[:, p % 2, :], psum[:, 6 + bank, 0:2 * P], rep_rd[:, p % 2, :], ALU.mult
                                          ).then_inc(s[f"ring{bank}"], 1)

                    for u in range(UNITS):
                        chunk_low(u, 0)
                        chunk_low(u, 1)
                        if u + 2 < UNITS:
                            maxima(g, u + 2)
                        elif following and u == UNITS - 1:
                            maxima(g, UNITS)
                        chunk_low(u, 2)
                        if u + 1 < UNITS:
                            reciprocals(g, u + 1)
                        if following and u == UNITS - 3:
                            queries_copied(gg + 1)
                        if u % 2 == 0 and u:
                            out_scaled(u // 2 - 1)
                    out_scaled(PAIRS - 1)
                    if following:
                        reciprocals(g, UNITS)
                        maxima(g, UNITS + 1)
                    for t in range(GT):
                        bank, _ = USES["output", t]
                        dve.wait_ge(s["y_s"], g * GT + t + 1)
                        if t == 0:
                            dve.wait_ge(s["xb_s"], (g + 1) * GT)
                        xg = x[:, ds(g * GT + t, 1), :]
                        dve.tensor_tensor(xg[:, 0], psum[:, 6 + bank, 0:D], xg[:, 0], ALU.add).then_inc(s[f"ring{bank}"], 1)

                projected(dve, b)
                queries_copied(0)
                maxima(b * GPB, 0)
                reciprocals(b * GPB, 0)
                maxima(b * GPB, 1)
                with dve.Fori(0, GPB - 1) as gg:
                    attention(gg, True)
                attention(GPB - 1, False)

            attention_done(dve)
            norm(1, x, lambda: low_gate(0, gate_w, gate_h, gate_l), lambda t: low_tile(0, t, xT_h, xT_l, TILES))
            steps = [0]

            def step(ins):
                ins.then_inc(s["rt"], 1)
                steps[0] += 1
                dve.wait_ge(s["rt"], steps[0])

            def over_experts(a):
                return a[:].unsqueeze(2).broadcast_to((P, TILES, E))

            dve.wait_ge(s["lgc"], 1)
            dve.wait_ge(s["cst"], 11)
            step(dve.tensor_reduce(mx[:], logit[:], AX.X, ALU.max))
            step(dve.tensor_tensor(logit[:], logit[:], over_experts(mx), ALU.subtract))
            dve.wait_ge(s["rt_e"], 1)
            step(dve.tensor_reduce(rsum[:], logit[:], AX.X, ALU.add))
            step(dve.reciprocal(rsum[:], rsum[:]))
            step(dve.tensor_tensor(logit[:], logit[:], over_experts(rsum), ALU.mult))
            for k in range(2):
                step(dve.tensor_reduce(weight[k][:], logit[:], AX.X, ALU.max))
                step(dve.tensor_tensor(eq[:], logit[:], over_experts(weight[k]), ALU.is_equal))
                step(dve.tensor_tensor(eq[:], eq[:], favour[:], ALU.mult))
                step(dve.tensor_reduce(mx[:], eq[:], AX.X, ALU.max))
                step(dve.tensor_tensor(pick[k][:], eq[:], over_experts(mx), ALU.is_equal))
                if k == 0:
                    step(dve.scalar_tensor_tensor(out=logit[:], in0=pick[0][:], scalar=-2.0, in1=logit[:],
                                                  op0=ALU.mult, op1=ALU.add))
            step(dve.tensor_tensor(both[:], pick[0][:], pick[1][:], ALU.add))
            def running_totals(n, scan, totals):
                dve.wait_ge(s["rt_pe"], n)
                step(dve.tensor_copy(totals[:], psum[:, 6, 0:P].rearrange("p (t e) -> p t e", e=E)))
                step(dve.tensor_copy(scan[0][:], totals[:]))
                src, shift = 0, 1
                while shift < TILES:
                    a, o = scan[src], scan[1 - src]
                    dve.tensor_copy(o[:, 0:shift], a[:, 0:shift]).then_inc(s["rt"], 1)
                    steps[0] += 1
                    step(dve.tensor_tensor(o[:, shift:], a[:, shift:], a[:, 0:TILES - shift], ALU.add))
                    src, shift = 1 - src, shift * 2
                return scan[src], scan[1 - src]

            def tokens_before(sums, free, totals):
                step(dve.tensor_tensor(free[:], sums[:], totals[:], ALU.subtract))
                step(dve.tensor_tensor(free[:], psum[:, 5, 0:P].rearrange("p (t e) -> p t e", e=E), free[:], ALU.add))
                return free

            sums, free = running_totals(1, scan, totals)
            step(dve.tensor_scalar(blocks[:], sums[:, TILES - 1, :], float(P - 1), None, ALU.add))
            step(dve.tensor_copy(blocks_i[:], blocks[:]))
            step(dve.tensor_scalar(blocks_i[:], blocks_i[:], 7, None, ALU.logical_shift_right))
            step(dve.tensor_copy(blocks[:], blocks_i[:]))
            step(dve.tensor_scalar(blocks[:], blocks[:], float(LEAST), None, ALU.max))
            step(dve.memset(starts[0][:, 0:1], 0.0))
            step(dve.tensor_copy(starts[0][:, 1:], blocks[:]))
            at, shift = 0, 1
            while shift < E + 1:
                a, o = starts[at], starts[1 - at]
                dve.tensor_copy(o[:, 0:shift], a[:, 0:shift]).then_inc(s["rt"], 1)
                steps[0] += 1
                step(dve.tensor_tensor(o[:, shift:], a[:, shift:], a[:, 0:E + 1 - shift], ALU.add))
                at, shift = 1 - at, shift * 2
            first_block = starts[at]
            ranks = tokens_before(sums, free, totals)
            step(dve.scalar_tensor_tensor(out=totals[:], in0=first_block[:, 0:E].unsqueeze(1).broadcast_to((P, TILES, E)),
                                          scalar=float(P), in1=ranks[:], op0=ALU.mult, op1=ALU.add))
            for k in range(2):
                step(dve.tensor_tensor(eq[:], pick[k][:], totals[:], ALU.mult))
                step(dve.tensor_reduce(slot_f[:], eq[:], AX.X, ALU.add))
                step(dve.tensor_copy(slot[k][:], slot_f[:]))
            step(dve.memset(table[:], 0))
            dve.tensor_copy(table[:, 0, 1:E + 2], first_block[:]).then_inc(s["tbl"], 1)
            dve.tensor_scalar(table[:, 1, 1:E + 1], blocks[:], -1.0, None, ALU.add).then_inc(s["tbl"], 1)
            dve.tensor_scalar(table[:, 2, 1:E + 2], first_block[:], -1.0, None, ALU.add).then_inc(s["tbl"], 1)
            step(dve.tensor_tensor(rsum[:], weight[0][:], weight[1][:], ALU.add))
            step(dve.tensor_scalar(rsum[:], rsum[:], 1e-20, None, ALU.add))
            step(dve.reciprocal(rsum[:], rsum[:]))
            for k in range(2):
                step(dve.tensor_tensor(weight[k][:], weight[k][:], rsum[:], ALU.mult))
            step(dve.memset(hid[:, F:], 0.0))
            assert steps[0] == RT_PADDED

            def x_low_shared(n):
                dve.wait_ge(s["xh_s"], n + 1)
                dve.tensor_copy(xbT_l[:], xT_l[:, :, ds(n * P, P)].bitcast(F32)).then_inc(s["xl_s"], 1)

            def x_low(n):
                dve.wait_ge(s["xh_s"], n + 1)
                dve.tensor_tensor(xbT_l[:], psum[:, 4, 0:D].rearrange("p (k c) -> p k c", k=KC), xbT_h[:].bitcast(F32),
                                  ALU.subtract).then_inc(s["xl_s"], 1)

            def hiddens(n):
                for c, (lo, hi) in enumerate(((0, FA), (FA, F))):
                    dve.wait_ge(s["si_s"], n * 2 + c + 1)
                    dve.wait_ge(s["gu"], n * 4 + 2 * c + 2)
                    dve.tensor_tensor(hid[:, lo:hi], psum[:, 2 * c + 1, 0:hi - lo], silu[:, lo:hi], ALU.mult).then_inc(s["h_s"], 1)

            def hidden_low(n):
                for c in range(2):
                    dve.wait_ge(s["hh_s"], n * 2 + c + 1)
                    dve.tensor_tensor(hT_l[:, 3 * c:3 * c + 3, :], psum[:, 5 + c, 0:3 * P].rearrange("p (k c) -> p k c", k=3),
                                      hT_h[:, 3 * c:3 * c + 3, :].bitcast(F32), ALU.subtract).then_inc(s["hl_s"], 1)

            def add_shared(n):
                dve.wait_ge(s["yo"], n + 1)
                xg = x[:, ds(n, 1), :]
                dve.tensor_tensor(xg[:, 0], psum[:, 7, 0:D], xg[:, 0], ALU.add).then_inc(s["ye"], 1)

            x_low_shared(0)
            hiddens(0)
            x_low_shared(1)
            hidden_low(0)
            with dve.Fori(0, SHARED - 2) as i:
                hiddens(i + 1)
                x_low_shared(i + 2)
                add_shared(i)
                hidden_low(i + 1)
            hiddens(SHARED - 1)
            x_low(SHARED)
            add_shared(SHARED - 2)
            hidden_low(SHARED - 1)
            hiddens(SHARED)
            x_low(SHARED + 1)
            add_shared(SHARED - 1)
            hidden_low(SHARED)
            dve.wait_ge(s["tbl"], 3)
            total = dve.value_load(table[0:1, 0, E + 1:E + 2], min_val=LEAST * E, max_val=ROUTED)
            with dve.Fori(0, total - 1) as i:
                n = dve.snap(i + (SHARED + 1))
                hiddens(n)
                x_low(n + 1)
                hidden_low(n)
            blocks_done(dve)
            dve.memset(kb_h[:].bitcast(F32), 0.0)
            dve.memset(kb_l[:].bitcast(F32), 0.0).then_inc(s["zk"], 1)
            dve.memset(vb_h[:].bitcast(F32), 0.0)
            dve.memset(vb_l[:].bitcast(F32), 0.0).then_inc(s["zk"], 1)

            def combine(g):
                for t in range(g * GT, (g + 1) * GT):
                    dve.wait_ge(s[f"got{t % 4}"], 32 * (t // 4 + 1))
                    for k in range(2):
                        last = dve.scalar_tensor_tensor(out=x[:, t, :], in0=y_got[:, 2 * (t % 4) + k, :], scalar=weight[k][:, t:t + 1],
                                                        in1=x[:, t, :], op0=ALU.mult, op1=ALU.add)
                        if k == 0:
                            step(last)
                    last.then_inc(s["out0"], 1)
                dve.wait_ge(s["out0"], (g + 1) * GT)

            combine(0)
            statistics(2, 0, x)
            dve.wait_ge(s["a1_h"], 2)
            dve.tensor_tensor(c_l[:], c_raw[:], c_h[:].bitcast(F32), ALU.subtract).then_inc(s["a1_l"], 1)
            dve.tensor_tensor(a_l[:], a_raw[:], a_h[:].bitcast(F32), ALU.subtract).then_inc(s["a1_l"], 1)
            dve.wait_ge(s["c1_act"], 1)
            dve.tensor_tensor(cT_l[:], psum[0:PX, 0, 0:KX * P].rearrange("p (k c) -> p k c", k=KX), cT_h[:].bitcast(F32),
                              ALU.subtract).then_inc(s["c1_dve"], 1)
            combine(1)
            statistics(2, 1, x)
            normalized(2, 0, x)
            combine(2)
            statistics(2, 2, x)
            normalized(2, 1, x)
            dve.wait_ge(s["c1_act"], 5 + 4 * KC)
            dve.wait_ge(s["zk"], 2)
            for k in range(KC):
                for hh in range(2):
                    half = slice(hh * C, (hh + 1) * C)
                    head = 2 * k + hh
                    cols = slice(head * C, (head + 1) * C)
                    dve.tensor_tensor(kb_l[half, :, k, cols], psum[half, 1, k * P:(k + 1) * P].rearrange("p (b c) -> p b c", b=B),
                                      kb_h[half, :, k, cols].bitcast(F32), ALU.subtract).then_inc(s["c1_dve"], 1)
                    cols = slice(hh * HD, (hh + 1) * HD)
                    dve.tensor_tensor(vb_l[half, :, k, cols],
                                      psum[half, 2, :].rearrange("p (b d) -> p b d", b=B)[:, :, head * HD:(head + 1) * HD],
                                      vb_h[half, :, k, cols].bitcast(F32), ALU.subtract).then_inc(s["c1_dve"], 1)
            combine(3)
            statistics(2, 3, x)
            normalized(2, 2, x)
            normalized(2, 3, x)

            def tokens1(g):
                for half in range(2):
                    dve.wait_ge(s["x1h"], g * 2 + half + 1)
                    cols = slice(half * 2 * P, (half + 1) * 2 * P)
                    dve.tensor_tensor(x1_l[:, :, cols], x1_bank(half), x1_h[:, :, cols].bitcast(F32), ALU.subtract).then_inc(s["x1l"], 1)

            def queries1(g):
                for k in range(KC):
                    dve.wait_ge(s["q1h"], g * KC + k + 1)
                    dve.scalar_tensor_tensor(out=q1_l[:, k, :], in0=psum[:, 4 + k, :], scalar=HD ** -0.5,
                                             in1=q1_h[:, k, :].bitcast(F32), op0=ALU.mult, op1=ALU.subtract).then_inc(s["q1l"], 1)

            def heads(a):
                return a.rearrange("p (h c) -> p h c", h=H)

            def attention1(g, b, following):
                for t in range(GT):
                    dve.wait_ge(s["sc1"], g * GT + t + 1)
                    dve.tensor_reduce(m1[:, t, :], heads(psum[:, t, 0:H * C]), AX.X, ALU.max).then_inc(s["mx1"], 1)
                    dve.wait_ge(s["mx1"], g * GT + t + 1)
                    dve.tensor_tensor(heads(p1[:, t, :]), heads(psum[:, t, 0:H * C]),
                                      m1[:, t, :].unsqueeze(2).broadcast_to((P, H, C)), ALU.subtract).then_inc(s["sb1"], 1)
                if following:
                    tokens1(g + 1)
                for t in range(GT):
                    dve.wait_ge(s["e1"], g * GT + t + 1)
                    dve.tensor_reduce(d1[:, t, :], heads(p1[:, t, :]), AX.X, ALU.add).then_inc(s["sm1"], 1)
                dve.wait_ge(s["sm1"], g * GT + GT)
                dve.reciprocal(d1[:], d1[:]).then_inc(s["rc1"], 1)
                dve.wait_ge(s["rc1"], g + 1)
                for t in range(GT):
                    dve.tensor_tensor(heads(p1[:, t, :]), heads(p1[:, t, :]),
                                      d1[:, t, :].unsqueeze(2).broadcast_to((P, H, C)), ALU.mult).then_inc(s["pn1"], 1)
                for t in range(GT):
                    dve.wait_ge(s["p1h"], g * GT + t + 1)
                    cols = slice(t * P, (t + 1) * P)
                    dve.tensor_tensor(p1T_l[:, :, cols], psum[:, t, 0:D].rearrange("p (k c) -> p k c", k=KC),
                                      p1T_h[:, :, cols].bitcast(F32), ALU.subtract).then_inc(s["p1l"], 1)
                if following:
                    queries1(g + 1)
                for k in range(KC):
                    dve.wait_ge(s["o1h"], g * KC + k + 1)
                    dve.tensor_tensor(o1_l[:, k, :], psum[:, 6 + k, :], o1_h[:, k, :].bitcast(F32), ALU.subtract).then_inc(s["o1l"], 1)
                dve.wait_ge(s["x1b"], TILES)
                for t in range(GT):
                    dve.wait_ge(s["y1"], g * GT + t + 1)
                    xg = x[:, ds(g * GT + t, 1), :]
                    dve.tensor_tensor(xg[:, 0], psum[:, t, 0:D], xg[:, 0], ALU.add).then_inc(s["x1a"], 1)

            tokens1(0)
            queries1(0)
            for b in range(B):
                with dve.Fori(0, GPB if b < B - 1 else GPB - 1) as gg:
                    attention1(b * GPB + gg, b, True)
            attention1(GROUPS - 1, B - 1, False)

            dve.wait_ge(s["x1a"], 1 + TILES)
            norm(3, x, lambda: low_gate(1, gate1_w, gate1_h, gate1_l), lambda t: low_tile(1, t, x2T_h, x2T_l, 2 * GT))
            dve.wait_ge(s["r1_e"], 1)
            dve.wait_ge(s["k1c"], 7)
            r1 = [0]

            def step1(ins):
                ins.then_inc(s["r1"], 1)
                r1[0] += 1
                dve.wait_ge(s["r1"], r1[0])

            step1(dve.tensor_scalar(gates[:], gates[:], 1.0, None, ALU.add))
            step1(dve.reciprocal(gates[:], gates[:]))
            assert r1[0] == R1_GATES
            step1(dve.memset(known[:], 0.0))
            for j in range(3):
                step1(dve.memset(pair[:, j, :], (j + 1) << (BITS - 2)))
            with dve.Fori(0, ROUNDS) as i:
                dve.wait_ge(s["srch"], 1 + i)
                dve.wait_ge(s["shf"], 1 + i)
                dve.tensor_tensor(cand[:], known[:].bitcast(I32).unsqueeze(1).broadcast_to((P, 3, E)), pair[:],
                                  ALU.bitwise_or).then_inc(s["cnd"], 1)
                dve.wait_ge(s["cnd"], i + 1)
                dve.tensor_tensor(over[:], gates[:].unsqueeze(1).broadcast_to((P, 3, TILES, E)),
                                  cand[:].bitcast(F32).unsqueeze(2).broadcast_to((P, 3, TILES, E)),
                                  ALU.is_ge).then_inc(s["cmpd"], 1)
                dve.tensor_scalar(pair[:], pair[:], 2, None, ALU.logical_shift_right).then_inc(s["shf"], 1)
                dve.wait_ge(s["cnt"], i + 1)
                dve.tensor_reduce(tally3[:], psum[:, 7, 0:3 * P].rearrange("p (j t e) -> p j e t", j=3, e=E), AX.X,
                                  ALU.add).then_inc(s["round"], 1)
                dve.wait_ge(s["round"], i * 3 + 1)
                dve.scalar_tensor_tensor(out=trial[:], in0=tally3[:], scalar=float(CHOSEN), in1=cand[:].bitcast(F32),
                                         op0=ALU.is_ge, op1=ALU.mult).then_inc(s["round"], 1)
                dve.wait_ge(s["round"], i * 3 + 2)
                dve.tensor_reduce(best[:], trial[:].rearrange("p j e -> p e j"), AX.X, ALU.max).then_inc(s["round"], 1)
                dve.wait_ge(s["round"], i * 3 + 3)
                dve.tensor_tensor(known[:], known[:], best[:], ALU.max).then_inc(s["srch"], 1)
            dve.wait_ge(s["srch"], 1 + ROUNDS)
            least = known[:].unsqueeze(1).broadcast_to((P, TILES, E))
            step1(dve.tensor_tensor(above[:], gates[:], least, ALU.is_gt))
            step1(dve.tensor_tensor(ties[:], gates[:], least, ALU.is_equal))
            dve.wait_ge(s["cnt"], ROUNDS + 1)
            step1(dve.tensor_reduce(tally[:], psum[:, 7, 0:P].rearrange("p (t e) -> p e t", e=E), AX.X, ALU.add))
            step1(dve.tensor_scalar(tally[:], tally[:], -1.0, float(CHOSEN), ALU.mult, ALU.add))

            def running1(n):
                dve.wait_ge(s["rt_pe"], n)
                step1(dve.tensor_copy(totals1[:], psum[:, 6, 0:P].rearrange("p (t e) -> p t e", e=E)))
                step1(dve.tensor_copy(scan1[0][:], totals1[:]))
                src, shift = 0, 1
                while shift < TILES:
                    a, o = scan1[src], scan1[1 - src]
                    dve.tensor_copy(o[:, 0:shift], a[:, 0:shift]).then_inc(s["r1"], 1)
                    r1[0] += 1
                    step1(dve.tensor_tensor(o[:, shift:], a[:, shift:], a[:, 0:TILES - shift], ALU.add))
                    src, shift = 1 - src, shift * 2
                free = scan1[1 - src]
                step1(dve.tensor_tensor(free[:], scan1[src][:], totals1[:], ALU.subtract))
                step1(dve.tensor_tensor(free[:], psum[:, 5, 0:P].rearrange("p (t e) -> p t e", e=E), free[:], ALU.add))
                return free

            earlier = running1(2)
            step1(dve.tensor_tensor(chosen[:], earlier[:], tally[:].unsqueeze(1).broadcast_to((P, TILES, E)), ALU.is_lt))
            step1(dve.tensor_tensor(chosen[:], chosen[:], ties[:], ALU.mult))
            step1(dve.tensor_tensor(chosen[:], chosen[:], above[:], ALU.add))
            assert r1[0] == R1_CHOSEN
            earlier = running1(3)
            step1(dve.tensor_copy(place_i[:], earlier[:]))
            step1(dve.tensor_scalar(row_i[:], place_i[:], P - 1, None, ALU.bitwise_and))
            step1(dve.tensor_scalar(place_i[:], place_i[:], 7, None, ALU.logical_shift_right))
            step1(dve.tensor_copy(row_f[:], row_i[:]))
            step1(dve.tensor_copy(tile_f[:], place_i[:]))
            step1(dve.scalar_tensor_tensor(out=row_f[:], in0=row_f[:], scalar=1.0, in1=chosen[:], op0=ALU.add, op1=ALU.mult))
            step1(dve.tensor_scalar(row_f[:], row_f[:], -1.0, None, ALU.add))
            te = (P, TILES * E, CT)
            put_2d = put_f[:].rearrange("p t e c -> p (t e) c")
            step1(dve.tensor_tensor(put_2d, tile_f[:].rearrange("p t e -> p (t e)").unsqueeze(2).broadcast_to(te),
                                    columns[:, 0:CT].unsqueeze(1).broadcast_to(te), ALU.is_equal))
            step1(dve.tensor_scalar(put[:, :, :, 1, :].rearrange("p t e c -> p (t e) c"), put_2d, lane[:], None, ALU.mult))
            step1(dve.tensor_tensor(put[:, :, :, 0, :], put_f[:].rearrange("p t e c -> p t (e c)").rearrange("p t (e c) -> p t e c", e=E),
                                    tile_no[:].unsqueeze(2).unsqueeze(3).broadcast_to((P, TILES, E, CT)), ALU.mult))
            for t in range(TILES):
                if t >= 2:
                    dve.wait_ge(s["hot_pe"], t - 1)
                dve.tensor_tensor(hot[:, t % 2], columns[:].unsqueeze(1).broadcast_to((P, E, P)),
                                  row_f[:, t, :].unsqueeze(2).broadcast_to((P, E, P)), ALU.is_equal).then_inc(s["hots"], 1)
            dve.wait_ge(s["hot_pe"], TILES)
            dve.tensor_copy(found[:], psum[:, :, 0:2 * CT]).then_inc(s["found_s"], 1)
            dve.wait_ge(s["found_s"], 1)
            dve.scalar_tensor_tensor(out=tokens[:], in0=found[:, :, 0:CT], scalar=float(P), in1=found[:, :, CT:],
                                     op0=ALU.mult, op1=ALU.add).then_inc(s["found_s"], 1)

            def rows_low(n):
                for t in range(CT):
                    cols = slice(t * P, (t + 1) * P)
                    dve.wait_ge(s["xe_hs"], n * CT + t + 1)
                    dve.tensor_tensor(xe_l[:, :, cols], psum[:, 6 + t % 2, 0:D].rearrange("p (k c) -> p k c", k=KC),
                                      xe_h[:, :, cols].bitcast(F32), ALU.subtract).then_inc(s["xe_ls"], 1)

            def weights_low(w, side, c):
                cols = slice(c * CUT, (c + 1) * CUT)
                dve.wait_ge(s["vs_hs"], w * CUTS + c + 1)
                dve.tensor_tensor(v_l[side][:, cols], v_raw[:, cols], v_h[side][:, cols].bitcast(F32), ALU.subtract).then_inc(s["vs_ls"], 1)

            def expert1(e, side, last):
                dve.tensor_copy(gval[:, side, :], gathered[side][:, :, ds(D + e, 1)].rearrange("p t o -> p (t o)")).then_inc(s["gval_s"], 1)
                for f in range(FT1):
                    dve.wait_ge(s["gl_s"], e * FT1 + f + 1)
                    dve.tensor_copy(g_h[:, f, :], gl[:, f % 2, :]).then_inc(s["gh_s"], 1)
                    dve.wait_ge(s["gh_s"], e * FT1 + f + 1)
                    dve.tensor_tensor(g_l[:, f, :], gl[:, f % 2, :], g_h[:, f, :].bitcast(F32), ALU.subtract).then_inc(s["gls"], 1)
                    if not last and f % 4 == 3:
                        weights_low(e + 1, 1 - side, f // 4)
                if not last:
                    for c in range(2, CUTS):
                        weights_low(e + 1, 1 - side, c)
                    rows_low(e + 1)
                dve.wait_ge(s["sadd"], 16 + e * (CT * 16))
                dve.wait_ge(s["gval_s"], e + 1)
                for t in range(CT):
                    dve.wait_ge(s["yb1"], 1 + e * CT + t + 1)
                    dve.tensor_tensor(ye1[:, t, :], psum[:, 2 + t, 0:D], b2[:, ds(e, 1), :].rearrange("p o d -> p (o d)"),
                                      ALU.add).then_inc(s["y1e"], 1)
                for t in range(CT):
                    dve.wait_ge(s["y1e"], 1 + e * CT + t + 1)
                    dve.tensor_scalar(ye1[:, t, :], ye1[:, t, :], gval[:, side, t:t + 1], None, ALU.mult).then_inc(s["ys1"], 1)

            rows_low(0)
            dve.wait_ge(s["b_in"], 32)
            with dve.Fori(0, E // 2 - 1) as p:
                for side in range(2):
                    expert1(2 * p + side, side, False)
            expert1(E - 2, 0, False)
            expert1(E - 1, 1, True)

        @block.tensor
        def _(pe):
            def products(o, pairs):
                for n, (l, r) in enumerate(pairs):
                    last = pe.matmul(o, l, r, start=n == 0, stop=n == len(pairs) - 1)
                return last

            pe.wait_ge(s["ident"], 2)
            pe.wait_ge(s["c_dve"], 3)
            for k in range(KX):
                last = pe.transpose(psum[0:PX, 0, k * P:(k + 1) * P], xcn[:, k * PX:(k + 1) * PX], ident[:])
            last.then_inc(s["c_pe"], 1)
            pe.wait_ge(s["mask_s"], 5)
            pe.wait_ge(s["c_act"], 1)
            products(psum[:, 1, :], [(l[:, k, :], r[:, k, :]) for k in range(KX)
                                     for l, r in ((ch, wkvx_h), (ch, wkvx_l), (cl, wkvx_h))]).then_inc(s["c_pe"], 1)
            pe.wait_ge(s["ident"], 3)
            pe.wait_ge(s["c_dve"], 10)
            for r in range(2):
                for h in range(H):
                    last = pe.transpose(psum[:, 2 + r, h * P:(h + 1) * P].bitcast(F32R), cparts[:, r * H + h, :], ident_r[:])
                last.then_inc(s["c_pe"], 1)

            with pe.Fori(0, B) as b:
                with pe.Fori(0, GPB) as gg:
                    g = b * GPB + gg
                    pe.wait_ge(s["ev_a"], 1 + g * 6)
                    pe.wait_ge(s["ev_d"], 1 + g * 6)
                    for bank in range(2):
                        pe.wait_ge(s[f"ring{bank}"], 1 + b * (GPB * RING[bank]))
                    for t in range(GT):
                        pe.wait_ge(s["xt_s"], g * GT + t + 1)
                        for k in range(KC):
                            last = pe.transpose(psum[:, 4 + t, k * P:(k + 1) * P], xt[:, t, k * P:(k + 1) * P], ident[:])
                        last.then_inc(s["tp"], 1)
                    for t in range(GT):
                        if t == 0:
                            pe.wait_ge(s["wsp_l"], 2)
                        pe.wait_ge(s["lnl_s"], g * GT + t + 1)
                        if t >= 2:
                            pe.wait_ge(s["raw_s"], g * GT + t - 1)
                        z = 2 * (t % 2)
                        for bank, lo, hi in ((z, 0, 2 * D), (z + 1, 2 * D, 3 * D)):
                            last = products(psum[:, bank, 0:hi - lo],
                                            [(l[:, t, k, :], r[:, k, lo:hi]) for k in range(KC)
                                             for l, r in ((lnh, wqkv_h), (lnh, wqkv_l), (lnl, wqkv_h))])
                        last.then_inc(s["qkv_s"], 1)
                    for t in range(GT):
                        pe.wait_ge(s["hi_s"], (g * GT + t + 1) * 2)
                        pe.wait_ge(s["lo_s"], (g * GT + t + 1) * 2)
                        for c in range(3):
                            n = 3 * t + c
                            if n >= 4:
                                pe.wait_ge(s["ev_d"] if n % 2 else s["ev_a"], 1 + g * 6 + n // 2 - 1)
                            for h in range(H):
                                last = pe.transpose(psum[:, 4 + n % 4, h * P:(h + 1) * P].bitcast(F32R),
                                                    parts[:, t % 2, c * H + h, :], ident_r[:])
                            last.then_inc(s["t12"], 1)

                def scores(g, u):
                    if u % UNITS == 0:
                        pe.wait_ge(s["qs_s"], (g + u // UNITS) * 2 + 2)
                    if u >= 2:
                        pe.wait_ge(s["exp_s"], g * UNITS + u - 1)
                    h, t = divmod(u % UNITS, GT)
                    q = qs[:, h, t * P:(t + 1) * P]
                    z = 3 * (u % 2)
                    for c in range(3):
                        lo, hi = c * PIECE, (c + 1) * PIECE
                        pairs = [(q, kT[:, h, 0, lo:hi]), (q, kT[:, h, 1, lo:hi])]
                        if hi == KEYS:
                            pairs.insert(0, (first_row[:], mask_rows[:, ds(b, 1), :].rearrange("p o k -> p (o k)")))
                        last = products(psum[:, z + c, 0:PIECE], pairs)
                    last.then_inc(s["sc_s"], 1)

                def attention(gg, following):
                    g = b * GPB + gg

                    def ring_bank(*use):
                        bank, before = USES[use]
                        pe.wait_ge(s[f"ring{bank}"], 1 + g * RING[bank] + before)
                        return 6 + bank

                    def transposes(u, c):
                        pe.wait_ge(s["exp_s"], g * UNITS + u + 1)
                        bank = ring_bank("chunk", u, c)
                        for k in range(CK):
                            last = pe.transpose(psum[:, bank, k * P:(k + 1) * P],
                                                prob[:, u % 3, (c * CK + k) * P:(c * CK + k + 1) * P], ident[:])
                        last.then_inc(s["pt_s"], 1)

                    def repeat_reciprocals(p):
                        pe.wait_ge(s["rc_s"], g * UNITS + 2 * p + 2)
                        bank = ring_bank("reciprocals", p)
                        for t in range(2):
                            u = 2 * p + t
                            last = pe.matmul(psum[:, bank, t * P:(t + 1) * P], rdenom[:, u:u + 1].broadcast_to((P, P)), ident[:],
                                             start=True, stop=True)
                        last.then_inc(s["sr_s"], 1)

                    def values(p):
                        if p == 0:
                            pe.wait_ge(s["vl_s"], (b + 1) * (GPB * GT))
                        chunk_bank, before = USES["chunk", 2 * p + 1, 2]
                        if chunk_bank != USES["result", p][0]:
                            pe.wait_ge(s[f"ring{chunk_bank}"], 1 + g * RING[chunk_bank] + before + 1)
                        bank = ring_bank("result", p)
                        cols = slice(p % 2 * 2 * P, (p % 2 + 1) * 2 * P)
                        products(psum[:, bank, 0:2 * P], [(v[:, k, p // 2, :], part[:, k, cols]) for k in range(KT)
                                                          for part in (pT_h, pT_l)]).then_inc(s["o_s"], 1)

                    for u in range(UNITS):
                        transposes(u, 0)
                        transposes(u, 1)
                        if u + 2 < UNITS:
                            scores(g, u + 2)
                        elif following and u == UNITS - 1:
                            scores(g, UNITS)
                        transposes(u, 2)
                        if u % 2 == 0 and u:
                            values(u // 2 - 1)
                        if u % 2:
                            repeat_reciprocals(u // 2)
                    if following:
                        scores(g, UNITS + 1)
                    values(PAIRS - 1)
                    for t in range(GT):
                        bank = ring_bank("output", t)
                        if t == 0:
                            pe.wait_ge(s["ol_s"], g * PAIRS + PAIRS - 1)
                        if t == GT - 2:
                            pe.wait_ge(s["ol_s"], (g + 1) * PAIRS)
                        cols = slice(t * P, (t + 1) * P)
                        products(psum[:, bank, 0:D], [(o[:, h, cols], w[:, h, :]) for h in range(H)
                                                      for o, w in ((oT_h, wo_h), (oT_h, wo_l), (oT_l, wo_h))]
                                 ).then_inc(s["y_s"], 1)

                pe.wait_ge(s["ev_a"], 1 + (b + 1) * (GPB * 6))
                pe.wait_ge(s["ev_d"], 1 + (b + 1) * (GPB * 6))
                scores(b * GPB, 0)
                scores(b * GPB, 1)
                with pe.Fori(0, GPB - 1) as gg:
                    attention(gg, True)
                attention(GPB - 1, False)

            def gate_logits(layer, xT_h, xT_l, slots, gw_h, gw_l, logitT):
                def transposed(t):
                    pe.wait_ge(s["xn_s"], (3 if layer else 1) * TILES + t + 1)
                    if t >= 4:
                        pe.wait_ge(s["gx_l"], layer * TILES + t - 3)
                    for k in range(KC):
                        last = pe.transpose(psum[:, t % 4, k * P:(k + 1) * P], xn[:, t, k * P:(k + 1) * P], ident[:])
                    last.then_inc(s["tp0"], 1)

                def logits(g):
                    at = GT * g % slots * P
                    cols = slice(at, at + GT * P)
                    pe.wait_ge(s["gx_l"], layer * TILES + (g + 1) * GT)
                    products(psum[0:E, 4 + g % 2, :], [(w[:, k, :], a[:, k, cols]) for k in range(KC)
                                                       for a, w in ((xT_h, gw_h), (xT_h, gw_l), (xT_l, gw_h))]
                             ).then_inc(s["lg_s"], 1)

                pe.wait_ge(s["gw_ls"], layer + 1)
                for t in range(TILES):
                    transposed(t)
                    if t % GT == 1 and t > GT:
                        g = t // GT - 1
                        if g >= 2:
                            pe.wait_ge(s["lgt"], layer * GROUPS + g - 1)
                        logits(g)
                pe.wait_ge(s["lgt"], layer * GROUPS + GROUPS - 2)
                logits(GROUPS - 1)
                for t in range(TILES):
                    if t % GT == 0:
                        pe.wait_ge(s["lgt"], layer * GROUPS + t // GT + 1)
                    last = pe.transpose(psum[:, 6, t * E:(t + 1) * E], logitT[:, t * P:(t + 1) * P], ident[0:E, 0:E])
                last.then_inc(s["lg_t"], 1)

            def count_before(flags, before, ones):
                f = flags[:].rearrange("p t e -> p (t e)")
                pe.matmul(psum[:, 5, 0:P], before[:], f, start=True, stop=True)
                pe.matmul(psum[:, 6, 0:P], ones[:], f, start=True, stop=True).then_inc(s["rt_pe"], 1)

            attention_done(pe)
            gate_logits(0, xT_h, xT_l, TILES, gate_h, gate_l, logitT)
            pe.wait_ge(s["lgc"], 1)
            pe.wait_ge(s["rt"], RT_PICKED)
            count_before(both, before, ones)

            def x_transposed(m):
                pe.wait_ge(s["xbi"], (m + 1) * 16)
                for k in range(KC):
                    last = pe.transpose(psum[:, 4, k * P:(k + 1) * P], xb[:, k * P:(k + 1) * P], ident[:])
                last.then_inc(s["tx"], 1)

            def gate_up(n, side):
                wh, wl = w_h[side], w_l[side]
                pe.wait_ge(s["xl_s"], n + 1)
                for c, (lo, hi) in enumerate(((0, FA), (FA, F))):
                    pe.wait_ge(s["h_s"], 1 + n * 2)
                    for up in range(2):
                        cols = [slice((up * KC + k) * F + lo, (up * KC + k) * F + hi) for k in range(KC)]
                        products(psum[:, 2 * c + up, 0:hi - lo],
                                 [(a[:, k, :], w[:, cols[k]]) for k in range(KC)
                                  for a, w in ((xbT_h, wh), (xbT_h, wl), (xbT_l, wh))]).then_inc(s["gu"], 1)

            def hidden_transposed(n):
                for c in range(2):
                    pe.wait_ge(s["h_s"], 1 + n * 2 + c + 1)
                    for k in range(3):
                        last = pe.transpose(psum[:, 5 + c, k * P:(k + 1) * P], hid[:, (3 * c + k) * P:(3 * c + k + 1) * P], ident[:])
                    last.then_inc(s["th"], 1)

            def down_products(n, side):
                wh, wl = w_h[side], w_l[side]
                pe.wait_ge(s["ye"], 1 + n)
                down = 2 * KC * F
                for c in range(2):
                    pe.wait_ge(s["hl_s"], n * 2 + c + 1)
                    for k in range(3 * c, 3 * c + 3):
                        for m, (a, w) in enumerate(((hT_h, wh), (hT_h, wl), (hT_l, wh))):
                            last = pe.matmul(psum[:, 7, 0:D], a[:, k, :], w[:, down + k * D:down + (k + 1) * D],
                                             start=k == 0 and m == 0, stop=k == FT - 1 and m == 2)
                last.then_inc(s["yo"], 1)

            pe.wait_ge(s["ws_l"], 1)
            gate_up(0, 0)
            pe.wait_ge(s["rt"], RT_PADDED)
            hidden_transposed(0)
            with pe.Fori(0, SHARED - 2) as i:
                gate_up(i + 1, 0)
                down_products(i, 0)
                hidden_transposed(i + 1)
            gate_up(SHARED - 1, 0)
            x_transposed(0)
            down_products(SHARED - 2, 0)
            hidden_transposed(SHARED - 1)
            with pe.Fori(0, E // 2) as p:
                for side in (1, 0):
                    w = 2 * p + (1 if side else 2)
                    first = pe.value_load(table[0:1, 0, ds(w, 1)], min_val=0, max_val=ROUTED - LEAST)
                    more = pe.value_load(table[0:1, 1, ds(w, 1)], min_val=LEAST - 1, max_val=TILES - 1)
                    pe.wait_ge(s["ws_l"], w + 1)
                    pe.sem_inc(s["met"], 1)
                    n = pe.snap(first + SHARED)
                    gate_up(n, side)
                    x_transposed(first + 1)
                    down_products(first + (SHARED - 1), 1 - side)
                    hidden_transposed(n)
                    with pe.Fori(0, more) as i:
                        n = pe.snap(first + i + (SHARED + 1))
                        gate_up(n, side)
                        x_transposed(first + i + 2)
                        down_products(first + i + SHARED, side)
                        hidden_transposed(n)
            total = pe.value_load(table[0:1, 0, E + 1:E + 2], min_val=LEAST * E, max_val=ROUTED)
            down_products(total + (SHARED - 1), 0)

            pe.wait_ge(s["a1_in"], 64)
            for k in range(KX):
                last = pe.transpose(psum[0:PX, 0, k * P:(k + 1) * P], xc1[:, k * PX:(k + 1) * PX], ident[:])
            last.then_inc(s["c1_pe"], 1)
            pe.wait_ge(s["a1_l"], 2)
            pe.wait_ge(s["c1_dve"], 1)
            pe.wait_ge(s["c1_act"], 5)
            for k in range(KC):
                cols = slice(k * P, (k + 1) * P)
                last = products(psum[:, 1, cols], [(w[:, 0, c, cols], a[:, c, :]) for c in range(KX)
                                                   for w, a in ((c_h, cT_h), (c_h, cT_l), (c_l, cT_h))])
            last.then_inc(s["c1_pe"], 1)
            for b in range(B):
                last = products(psum[:, 2, b * D:(b + 1) * D],
                                [(a[:, c, b].rearrange("p r c -> p (r c)"), w[:, 1, c, :]) for c in range(KX)
                                 for w, a in ((c_h, cd_h), (c_h, cd_l), (c_l, cd_h))])
            last.then_inc(s["c1_pe"], 1)
            pe.wait_ge(s["c1_dve"], 1 + 4 * KC)
            pe.wait_ge(s["c1_act"], 5 + 4 * KC)

            def queries1(g):
                for t in range(GT):
                    pe.wait_ge(s["xs1_s"], g * GT + t + 1)
                    for k in range(KC):
                        last = pe.transpose(x1_bank(t // 2)[:, k, t % 2 * P:(t % 2 + 1) * P], xs1[:, t, k * P:(k + 1) * P], ident[:])
                    if t % 2:
                        last.then_inc(s["tp1"], 1)
                pe.wait_ge(s["x1l"], (g + 1) * 2)
                for m in range(KC):
                    cols = slice(m * P, (m + 1) * P)
                    products(psum[:, 4 + m, :], [(w[:, 0, k, cols], a[:, k, :]) for k in range(KC)
                                                 for w, a in ((a_h, x1_h), (a_h, x1_l), (a_l, x1_h))]).then_inc(s["q1"], 1)

            def attention1(g, b, following):
                pe.wait_ge(s["q1l"], (g + 1) * KC)
                pe.wait_ge(s["x1a"], 1 + g * GT)
                for t in range(GT):
                    cols = slice(t * P, (t + 1) * P)
                    products(psum[:, t, 0:H * C], [(q[:, k, cols], kb[:, b, k, :]) for k in range(KC)
                                                   for q, kb in ((q1_h, kb_h), (q1_h, kb_l), (q1_l, kb_h))]).then_inc(s["sc1"], 1)
                if following:
                    queries1(g + 1)
                for t in range(GT):
                    pe.wait_ge(s["pn1"], g * GT + t + 1)
                    for k in range(KC):
                        last = pe.transpose(psum[:, t, k * P:(k + 1) * P], p1[:, t, k * P:(k + 1) * P], ident[:])
                    last.then_inc(s["pt1"], 1)
                pe.wait_ge(s["p1l"], (g + 1) * GT)
                for k in range(KC):
                    products(psum[:, 6 + k, :], [(a[:, b, k, :], p[:, k, :]) for a, p in
                                                 ((vb_h, p1T_h), (vb_h, p1T_l), (vb_l, p1T_h))]).then_inc(s["o1"], 1)
                pe.wait_ge(s["o1l"], (g + 1) * KC)
                for t in range(GT):
                    cols = slice(t * P, (t + 1) * P)
                    products(psum[:, t, 0:D], [(o[:, k, cols], w[:, 1, k, :]) for k in range(KC)
                                                   for o, w in ((o1_h, a_h), (o1_h, a_l), (o1_l, a_h))]).then_inc(s["y1"], 1)

            queries1(0)
            for b in range(B):
                with pe.Fori(0, GPB if b < B - 1 else GPB - 1) as gg:
                    attention1(b * GPB + gg, b, True)
            attention1(GROUPS - 1, B - 1, False)

            pe.wait_ge(s["x1a"], 1 + TILES)
            gate_logits(1, x2T_h, x2T_l, 2 * GT, gate1_h, gate1_l, logit1T)
            with pe.Fori(0, ROUNDS) as i:
                pe.wait_ge(s["cmpd"], i + 1)
                pe.matmul(psum[:, 7, 0:3 * P], ones_b[:], over[:].rearrange("p j t e -> p (j t e)"), start=True, stop=True).then_inc(s["cnt"], 1)
            pe.wait_ge(s["r1"], R1_FLAGS)
            pe.matmul(psum[:, 7, 0:P], ones1[:], above[:].rearrange("p t e -> p (t e)"), start=True, stop=True).then_inc(s["cnt"], 1)
            count_before(ties, before1, ones1)
            pe.wait_ge(s["r1"], R1_CHOSEN)
            count_before(chosen, before1, ones1)
            pe.wait_ge(s["hots"], 1)
            for t in range(TILES):
                pe.wait_ge(s["hots"], t + 1)
                for e in range(E):
                    last = pe.matmul(psum[:, e, 0:2 * CT], hot[:, t % 2, e, :], put[:, t, e].rearrange("p v c -> p (v c)"),
                                     start=t == 0, stop=t == TILES - 1)
                last.then_inc(s["hot_pe"], 1)

            def rows_transposed(n, side, t):
                if t == 0:
                    pe.wait_ge(s[f"ga{side}"], (n // 2 + 1) * (CT * 16))
                if t >= 2:
                    pe.wait_ge(s["xe_ls"], n * CT + t - 1)
                for k in range(KC):
                    last = pe.transpose(psum[:, 6 + t % 2, k * P:(k + 1) * P], gathered[side][:, t, k * P:(k + 1) * P], ident[:])
                last.then_inc(s["xe_t"], 1)

            def expert1(e, side, last_one):
                wh, wl = v_h[side], v_l[side]
                pe.wait_ge(s["vs_ls"], (e + 1) * CUTS)
                pe.wait_ge(s["xe_ls"], (e + 1) * CT)
                for f in range(FT1):
                    if f >= 2:
                        pe.wait_ge(s["gl_s"], e * FT1 + f - 1)
                    cols = [slice(k * F1 + f * P, k * F1 + (f + 1) * P) for k in range(KC)]
                    products(psum[:, f % 2, :], [(w[:, cols[k]], a[:, k, :]) for k in range(KC)
                                                 for w, a in ((wh, xe_h), (wh, xe_l), (wl, xe_h))]).then_inc(s["h1"], 1)
                pe.wait_ge(s["y1e"], 1 + e * CT)
                for f in range(FT1):
                    pe.wait_ge(s["gls"], e * FT1 + f + 1)
                    for t in range(CT):
                        cols = slice(t * P, (t + 1) * P)
                        w2 = slice(W1 + f * D, W1 + (f + 1) * D)
                        for m, (a, w) in enumerate(((g_h, wh), (g_h, wl), (g_l, wh))):
                            last = pe.matmul(psum[:, 2 + t, 0:D], a[:, f, cols], w[:, w2],
                                             start=f == 0 and m == 0, stop=f == FT1 - 1 and m == 2)
                        if f == FT1 - 1:
                            last.then_inc(s["yb1"], 1)
                    if not last_one and 3 <= f < 3 + CT:
                        rows_transposed(e + 1, 1 - side, f - 3)

            pe.wait_ge(s["found_s"], 2)
            for t in range(CT):
                rows_transposed(0, 0, t)
            with pe.Fori(0, E // 2 - 1) as p:
                for side in range(2):
                    expert1(2 * p + side, side, False)
            expert1(E - 2, 0, False)
            expert1(E - 1, 1, True)


def kernel(**inputs):
    import concourse.bacc as bacc
    from concourse.bass_utils import run_bass_kernel_spmd

    i = {k: np.asarray(v) for k, v in inputs.items()}

    def chunked(w, n):
        return w.reshape(n, -1, w.shape[-1]).transpose(1, 0, 2)

    def columns(vec, n):
        return vec.reshape(n, -1).T

    def rows_first(w):
        e, r, m = w.shape
        return w.reshape(e, r // P, P, m).transpose(0, 2, 1, 3).reshape(e, P, -1)

    def expert_weights(i):
        gate, up, down = (np.concatenate([i[f"L0_ffn_shared_{n}"][None], i[f"L0_ffn_expert_{n}"]]).transpose(0, 2, 1)
                          for n in ("gate", "up", "down"))
        down = np.pad(down, ((0, 0), (0, FT * P - F), (0, 0)))
        return np.concatenate([rows_first(gate), rows_first(up), rows_first(down)], 2)

    wo = i["L0_xattn_Wo"].T.reshape(H, HD, D)
    arrays = {
        "x": i["x"].reshape(T, D),
        "ctx": i["ctx_768"].reshape(B * C, DC),
        "mask": i["mask_BxS2_bk0"].reshape(1, B * C),
        "lnx_g": columns(i["L0_xattn_ln_x_g"], KX), "lnx_b": columns(i["L0_xattn_ln_x_b"], KX),
        "ln_g": columns(i["L0_xattn_ln_l_g"], KC), "ln_b": columns(i["L0_xattn_ln_l_b"], KC),
        "qk_gain": np.concatenate([i["L0_xattn_qn_g"]] * H + [i["L0_xattn_kn_g"]] * H),
        "bo0": i["L0_xattn_bo"],
        "wkvx": chunked(i["L0_xattn_Wkv"].T, KX),
        "wqkv": chunked(np.concatenate([i["L0_xattn_Wq"].T, i["L0_xattn_Wlkv"].T], 1), KC),
        "gate1": chunked(i["L1_ffn_Wg"], KC),
        "wkv1": np.stack([chunked(i["L1_xattn_Wk"].T, KX), chunked(i["L1_xattn_Wv"].T, KX)], 1),
        "wqo1": np.stack([chunked(i["L1_xattn_Wq"].T, KC), chunked(i["L1_xattn_Wo"].T, KC)], 1),
        "bo1": i["L1_xattn_bo"],
        "b1": i["L1_ffn_b1"].reshape(E, FT1, P).transpose(2, 0, 1).reshape(P, E * FT1),
        "b2": i["L1_ffn_b2"].reshape(E * D),
        "experts1": np.concatenate([rows_first(i["L1_ffn_W1"]), rows_first(i["L1_ffn_W2"])], 2),
        "gate0": chunked(i["L0_ffn_gate_w"].T, KC),
        "experts0": expert_weights(i),
        "wo0": np.concatenate([wo, wo], 1).transpose(1, 0, 2),
    }
    arrays = {k: np.ascontiguousarray(a) for k, a in arrays.items()}
    nc = bacc.Bacc("TRN2", target_bir_lowering=False, num_devices=1)
    ap = {k: nc.dram_tensor("in_" + k, a.shape, mybir.dt.from_np(a.dtype), kind="ExternalInput").ap() for k, a in arrays.items()}
    out = nc.dram_tensor("y", (T, D), F32, kind="ExternalOutput").ap()
    build(nc, ap, out)
    r = run_bass_kernel_spmd(nc, [{"in_" + k: a for k, a in arrays.items()}], core_ids=[0])
    return r.results[0]["y"].reshape(B, S, D)
```
